# Optimizing a Trainium2 kernel written in Bass

```python
import numpy as np
import jax
import jax.numpy as jnp

def _softmax(x, axis=-1):
    return jax.nn.softmax(x, axis=axis)

def _gelu(x):
    return jax.nn.gelu(x, approximate=True)

def _silu(x):
    return jax.nn.silu(x)

def _sigmoid(x):
    return jax.nn.sigmoid(x)

def _layernorm(x, axis=-1, eps=1e-05):
    m = jnp.mean(x, axis=axis, keepdims=True)
    v = jnp.var(x, axis=axis, keepdims=True)
    return (x - m) / jnp.sqrt(v + eps)

def _scatter_add(tgt, idx, src, axis=0):
    return tgt.at[idx].add(src)

def _segment_sum(src, seg, n):
    return jax.ops.segment_sum(src, seg, n)
kernel_name = 'mk_xattn_ffn_d4_seqx_r8_16f22b'

def setup_inputs(seed: int=0):
    np.random.seed(seed)
    _w = jnp.asarray

    def _rec_inputs():
        import jax
        import jax.numpy as jnp
        _rk = jax.random.key(seed)
        x = -0.0002928 + 1 * jax.random.normal(jax.random.fold_in(_rk, 1), (32, 128, 128), jnp.float32)
        _lenS = 128 - jax.random.randint(jax.random.fold_in(_rk, 7), (32,), 0, max(1, 128 // 4) + 1, jnp.int32)
        _lenS2 = 128 - jax.random.randint(jax.random.fold_in(_rk, 8), (32,), 0, max(1, 128 // 4) + 1, jnp.int32)
        _ctx_1024P = jax.random.normal(jax.random.fold_in(_rk, 11), (32, 16, 128), jnp.float32)
        _ctx_1024c = jax.random.dirichlet(jax.random.fold_in(_rk, 511), 0.3 * jnp.ones((16,), jnp.float32), (32, 128))
        _ctx_1024t = jnp.einsum('bsk,bkd->bsd', _ctx_1024c, _ctx_1024P)
        _ctx_1024t = _ctx_1024t * jax.lax.rsqrt(jnp.mean(jnp.square(_ctx_1024t)) + 1e-12) * 0.953939
        ctx_1024 = -1.39393e-06 + 0.999914 * (_ctx_1024t + 0.3 * jax.random.normal(jax.random.fold_in(_rk, 611), (32, 128, 128), jnp.float32))
        _validS = jnp.arange(128)[None, :] < _lenS[:, None]
        _validS2 = jnp.arange(128)[None, :] < _lenS2[:, None]
        _causal = jnp.tril(jnp.ones((128, 128), dtype=bool))
        mask_BxS2_ff1 = jnp.where(jnp.ones((32, 128), dtype=bool), 1.0, 0.0).astype(jnp.float32)
        mask_1x1xSxS2_bk0 = jnp.logical_not(jnp.broadcast_to(_validS2[0:1, None, None, :], (1, 1, 128, 128)))
        return (x, ctx_1024, mask_BxS2_ff1, mask_1x1xSxS2_bk0)
    x, ctx_1024, mask_BxS2_ff1, mask_1x1xSxS2_bk0 = _rec_inputs()

    def _L0_xattn_setup():
        import jax, jax.numpy as jnp
        import numpy as np
        D_MODEL = 128
        N_HEADS = 16
        D_HEAD = D_MODEL // N_HEADS
        WINDOW = 128

        def _heads(x):
            B, S, _ = x.shape
            return x.reshape(B, S, N_HEADS, D_HEAD).transpose(0, 2, 1, 3)
        key = jax.random.key(seed)
        ks = jax.random.split(key, 11)
        B, S = (1, 512)
        s = 1.0 / np.sqrt(D_MODEL)
        return {'query': jax.random.normal(ks[0], (B, S, D_MODEL), jnp.float32), 'key': jax.random.normal(ks[1], (B, S, D_MODEL), jnp.float32), 'value': jax.random.normal(ks[2], (B, S, D_MODEL), jnp.float32), 'Wq': jax.random.normal(ks[3], (D_MODEL, D_MODEL), jnp.float32) * s, 'bq': jnp.zeros((D_MODEL,), jnp.float32), 'Wk': jax.random.normal(ks[4], (D_MODEL, D_MODEL), jnp.float32) * s, 'bk': jnp.zeros((D_MODEL,), jnp.float32), 'Wv': jax.random.normal(ks[5], (D_MODEL, D_MODEL), jnp.float32) * s, 'bv': jnp.zeros((D_MODEL,), jnp.float32), 'Wo': jax.random.normal(ks[6], (D_MODEL, D_MODEL), jnp.float32) * s, 'bo': jnp.zeros((D_MODEL,), jnp.float32)}
    _L0_xattn_all = _L0_xattn_setup()
    _L0_xattn_in = {k: v for k, v in _L0_xattn_all.items() if k in ('Wq', 'bq', 'Wk', 'bk', 'Wv', 'bv', 'Wo', 'bo')}
    del _L0_xattn_all

    def _L0_ffn_setup():
        import jax, jax.numpy as jnp
        import numpy as np
        TOP_P = 0.3
        key = jax.random.key(seed)
        k1, k2, k3, k4 = jax.random.split(key, 4)
        B, S, D, H, E = (4, 512, 128, 128, 8)
        x = jax.random.normal(k1, (B, S, D), dtype=jnp.float32)
        gate_W = jax.random.normal(k2, (E, D), dtype=jnp.float32) / np.float32(np.sqrt(D))
        expert_W = jax.random.normal(k3, (E, H, D), dtype=jnp.float32) / np.float32(np.sqrt(D))
        out_W = jax.random.normal(k4, (D, H), dtype=jnp.float32) / np.float32(np.sqrt(H))
        return {'x': x, 'gate_W': gate_W, 'expert_W': expert_W, 'out_W': out_W}
    _L0_ffn_all = _L0_ffn_setup()
    _L0_ffn_in = {k: v for k, v in _L0_ffn_all.items() if k in ('gate_W', 'expert_W', 'out_W')}
    del _L0_ffn_all

    def _L1_xattn_setup():
        import jax, jax.numpy as jnp
        import numpy as np
        D_MODEL = 128
        HEADS = 16
        DEPTH = D_MODEL // HEADS
        B, S = (4, 512)
        EPS_K = 1e-06
        EPS_LN = 1e-06

        def _layernorm(x, g, b):
            m = jnp.mean(x, axis=-1, keepdims=True)
            var = jnp.var(x, axis=-1, keepdims=True)
            return (x - m) * jax.lax.rsqrt(var + EPS_LN) * g + b

        def _split_heads(x):
            bsz, sl, _ = x.shape
            return x.reshape(bsz, sl, HEADS, DEPTH).transpose(0, 2, 1, 3)
        key = jax.random.key(seed)
        ks = jax.random.split(key, 8)
        lecun = 1.0 / np.sqrt(D_MODEL)
        glorot = np.sqrt(2.0 / (D_MODEL + D_MODEL))
        return {'q': jax.random.normal(ks[0], (B, S, D_MODEL), jnp.float32), 'k': jax.random.normal(ks[1], (B, S, D_MODEL), jnp.float32), 'v': jax.random.normal(ks[2], (B, S, D_MODEL), jnp.float32), 'mask': jnp.ones((B, S), jnp.float32), 'wq': jax.random.normal(ks[3], (D_MODEL, D_MODEL), jnp.float32) * lecun, 'wk': jax.random.normal(ks[4], (D_MODEL, D_MODEL), jnp.float32) * lecun, 'wv': jax.random.normal(ks[5], (D_MODEL, D_MODEL), jnp.float32) * lecun, 'ln_gamma': jnp.ones((D_MODEL,), jnp.float32), 'ln_beta': jnp.zeros((D_MODEL,), jnp.float32), 'dense_w': jax.random.normal(ks[6], (D_MODEL, D_MODEL), jnp.float32) * glorot, 'dense_b': jnp.zeros((D_MODEL,), jnp.float32)}
    _L1_xattn_all = _L1_xattn_setup()
    _L1_xattn_in = {k: v for k, v in _L1_xattn_all.items() if k in ('wq', 'wk', 'wv', 'ln_gamma', 'ln_beta', 'dense_w', 'dense_b')}
    del _L1_xattn_all

    def _L1_ffn_setup():
        import jax, jax.numpy as jnp
        import numpy as np
        B, S, H, E, K, F = (4, 256, 128, 8, 64, 512)
        key = jax.random.key(seed)
        k0, k1, k2, k3 = jax.random.split(key, 4)
        sc = lambda d: 1.0 / np.sqrt(d).astype(np.float32)
        return {'x': jax.random.normal(k0, (B, S, H), jnp.float32), 'Wg': jax.random.normal(k1, (E, H), jnp.float32) * sc(H), 'W1': jax.random.normal(k2, (E, H, F), jnp.float32) * sc(H), 'b1': jnp.zeros((E, F), jnp.float32), 'W2': jax.random.normal(k3, (E, F, H), jnp.float32) * sc(F), 'b2': jnp.zeros((E, H), jnp.float32)}
    _L1_ffn_all = _L1_ffn_setup()
    _L1_ffn_in = {k: v for k, v in _L1_ffn_all.items() if k in ('Wg', 'W1', 'b1', 'W2', 'b2')}
    del _L1_ffn_all

    def _L2_xattn_setup():
        import jax, jax.numpy as jnp
        import numpy as np
        D_MODEL = 128
        N_HEADS = 16
        D_K = D_MODEL // N_HEADS
        B, S = (2, 256)
        key = jax.random.key(seed)
        ks = jax.random.split(key, 12)
        scale = 1.0 / np.sqrt(D_MODEL)
        inp = {'query': jax.random.normal(ks[0], (B, S, D_MODEL), jnp.float32), 'key': jax.random.normal(ks[1], (B, S, D_MODEL), jnp.float32), 'value': jax.random.normal(ks[2], (B, S, D_MODEL), jnp.float32), 'mask': jnp.tril(jnp.ones((S, S), dtype=bool))[None, None], 'W_q': jax.random.normal(ks[3], (D_MODEL, D_MODEL), jnp.float32) * scale, 'b_q': jnp.zeros((D_MODEL,), jnp.float32), 'W_k': jax.random.normal(ks[4], (D_MODEL, D_MODEL), jnp.float32) * scale, 'b_k': jnp.zeros((D_MODEL,), jnp.float32), 'W_v': jax.random.normal(ks[5], (D_MODEL, D_MODEL), jnp.float32) * scale, 'b_v': jnp.zeros((D_MODEL,), jnp.float32), 'W_o': jax.random.normal(ks[6], (D_MODEL, D_MODEL), jnp.float32) * scale, 'b_o': jnp.zeros((D_MODEL,), jnp.float32)}
        return inp
    _L2_xattn_all = _L2_xattn_setup()
    _L2_xattn_in = {k: v for k, v in _L2_xattn_all.items() if k in ('W_q', 'b_q', 'W_k', 'b_k', 'W_v', 'b_v', 'W_o', 'b_o')}
    del _L2_xattn_all

    def _L2_ffn_setup():
        import jax, jax.numpy as jnp
        import numpy as np
        E = 8
        K = 2
        D = 128
        H = 342
        B, S = (2, 256)

        def _moe_forward(x, centroid, Wg, bg, W1, b1, W2, b2):
            T = x.shape[0] * x.shape[1]
            xs = x.reshape(T, D)
            d2 = jnp.sum(xs * xs, axis=-1, keepdims=True) + jnp.sum(centroid * centroid, axis=-1)[None, :] - 2.0 * (xs @ centroid.T)
            dist = jnp.sqrt(jnp.maximum(d2, 1e-12))
            w, sel = jax.lax.top_k(dist, K)
            w = jax.nn.softmax(w.astype(jnp.float32), axis=1).astype(x.dtype)
            we = jnp.zeros((T, E), dtype=x.dtype).at[jnp.arange(T)[:, None], sel].add(w)
            out = jnp.zeros_like(xs)
            for e in range(E):
                h = jax.nn.silu(xs @ Wg[e] + bg[e]) * (xs @ W1[e] + b1[e])
                out = out + we[:, e:e + 1] * (h @ W2[e] + b2[e])
            return out.reshape(x.shape)
        key = jax.random.key(seed)
        ks = jax.random.split(key, 9)
        scale = 0.02
        return {'x': jax.random.normal(ks[0], (B, S, D), dtype=jnp.float32), 'centroid': jax.random.normal(ks[1], (E, D), dtype=jnp.float32), 'Wg': jax.random.normal(ks[2], (E, D, H), dtype=jnp.float32) * scale, 'bg': jnp.zeros((E, H), dtype=jnp.float32), 'W1': jax.random.normal(ks[3], (E, D, H), dtype=jnp.float32) * scale, 'b1': jnp.zeros((E, H), dtype=jnp.float32), 'W2': jax.random.normal(ks[4], (E, H, D), dtype=jnp.float32) * scale, 'b2': jnp.zeros((E, D), dtype=jnp.float32)}
    _L2_ffn_all = _L2_ffn_setup()
    _L2_ffn_in = {k: v for k, v in _L2_ffn_all.items() if k in ('centroid', 'Wg', 'bg', 'W1', 'b1', 'W2', 'b2')}
    del _L2_ffn_all

    def _L3_xattn_setup():
        import jax, jax.numpy as jnp
        import numpy as np
        B, S, D = (2, 256, 128)
        H, HD = (16, 64)
        key = jax.random.key(seed)
        ks = jax.random.split(key, 8)
        scale = 1.0 / np.sqrt(D)
        return {'q': jax.random.normal(ks[0], (B, S, D), jnp.float32), 'k': jax.random.normal(ks[1], (B, S, D), jnp.float32), 'v': jax.random.normal(ks[2], (B, S, D), jnp.float32), 'Wq': jax.random.normal(ks[3], (H * HD, D), jnp.float32) * scale, 'bq': jnp.zeros((H * HD,), jnp.float32), 'Wk': jax.random.normal(ks[4], (H * HD, D), jnp.float32) * scale, 'bk': jnp.zeros((H * HD,), jnp.float32), 'Wv': jax.random.normal(ks[5], (H * HD, D), jnp.float32) * scale, 'bv': jnp.zeros((H * HD,), jnp.float32), 'Wo': jax.random.normal(ks[6], (D, H * HD), jnp.float32) * scale, 'bo': jnp.zeros((D,), jnp.float32)}
    _L3_xattn_all = _L3_xattn_setup()
    _L3_xattn_in = {k: v for k, v in _L3_xattn_all.items() if k in ('Wq', 'bq', 'Wk', 'bk', 'Wv', 'bv', 'Wo', 'bo')}
    del _L3_xattn_all

    def _L3_ffn_setup():
        import jax, jax.numpy as jnp
        import numpy as np
        key = jax.random.key(seed)
        k1, k2, k3 = jax.random.split(key, 3)
        B, T, D, E = (4, 256, 128, 8)
        x = jax.random.normal(k1, (B, T, D), dtype=jnp.float32)
        gate_w = jax.random.normal(k2, (E, D), dtype=jnp.float32) * (1.0 / np.sqrt(D))
        bound = float(np.sqrt(6.0 / (D + D)))
        We = jax.random.uniform(k3, (E, D, D), dtype=jnp.float32, minval=-bound, maxval=bound)
        return {'x': x, 'gate_w': gate_w, 'We': We}
    _L3_ffn_all = _L3_ffn_setup()
    _L3_ffn_in = {k: v for k, v in _L3_ffn_all.items() if k in ('gate_w', 'We')}
    del _L3_ffn_all
    return {'x': x, 'ctx_1024': ctx_1024, 'mask_BxS2_ff1': mask_BxS2_ff1, 'mask_1x1xSxS2_bk0': mask_1x1xSxS2_bk0, 'L0_xattn_Wq': _L0_xattn_in['Wq'], 'L0_xattn_bq': _L0_xattn_in['bq'], 'L0_xattn_Wk': _L0_xattn_in['Wk'], 'L0_xattn_bk': _L0_xattn_in['bk'], 'L0_xattn_Wv': _L0_xattn_in['Wv'], 'L0_xattn_bv': _L0_xattn_in['bv'], 'L0_xattn_Wo': _L0_xattn_in['Wo'], 'L0_xattn_bo': _L0_xattn_in['bo'], 'L0_ffn_gate_W': _L0_ffn_in['gate_W'], 'L0_ffn_expert_W': _L0_ffn_in['expert_W'], 'L0_ffn_out_W': _L0_ffn_in['out_W'], 'L1_xattn_wq': _L1_xattn_in['wq'], 'L1_xattn_wk': _L1_xattn_in['wk'], 'L1_xattn_wv': _L1_xattn_in['wv'], 'L1_xattn_ln_gamma': _L1_xattn_in['ln_gamma'], 'L1_xattn_ln_beta': _L1_xattn_in['ln_beta'], 'L1_xattn_dense_w': _L1_xattn_in['dense_w'], 'L1_xattn_dense_b': _L1_xattn_in['dense_b'], 'L1_ffn_Wg': _L1_ffn_in['Wg'], 'L1_ffn_W1': _L1_ffn_in['W1'], 'L1_ffn_b1': _L1_ffn_in['b1'], 'L1_ffn_W2': _L1_ffn_in['W2'], 'L1_ffn_b2': _L1_ffn_in['b2'], 'L2_xattn_W_q': _L2_xattn_in['W_q'], 'L2_xattn_b_q': _L2_xattn_in['b_q'], 'L2_xattn_W_k': _L2_xattn_in['W_k'], 'L2_xattn_b_k': _L2_xattn_in['b_k'], 'L2_xattn_W_v': _L2_xattn_in['W_v'], 'L2_xattn_b_v': _L2_xattn_in['b_v'], 'L2_xattn_W_o': _L2_xattn_in['W_o'], 'L2_xattn_b_o': _L2_xattn_in['b_o'], 'L2_ffn_centroid': _L2_ffn_in['centroid'], 'L2_ffn_Wg': _L2_ffn_in['Wg'], 'L2_ffn_bg': _L2_ffn_in['bg'], 'L2_ffn_W1': _L2_ffn_in['W1'], 'L2_ffn_b1': _L2_ffn_in['b1'], 'L2_ffn_W2': _L2_ffn_in['W2'], 'L2_ffn_b2': _L2_ffn_in['b2'], 'L3_xattn_Wq': _L3_xattn_in['Wq'], 'L3_xattn_bq': _L3_xattn_in['bq'], 'L3_xattn_Wk': _L3_xattn_in['Wk'], 'L3_xattn_bk': _L3_xattn_in['bk'], 'L3_xattn_Wv': _L3_xattn_in['Wv'], 'L3_xattn_bv': _L3_xattn_in['bv'], 'L3_xattn_Wo': _L3_xattn_in['Wo'], 'L3_xattn_bo': _L3_xattn_in['bo'], 'L3_ffn_gate_w': _L3_ffn_in['gate_w'], 'L3_ffn_We': _L3_ffn_in['We']}

def reference(x, ctx_1024, mask_BxS2_ff1, mask_1x1xSxS2_bk0, L0_xattn_Wq, L0_xattn_bq, L0_xattn_Wk, L0_xattn_bk, L0_xattn_Wv, L0_xattn_bv, L0_xattn_Wo, L0_xattn_bo, L0_ffn_gate_W, L0_ffn_expert_W, L0_ffn_out_W, L1_xattn_wq, L1_xattn_wk, L1_xattn_wv, L1_xattn_ln_gamma, L1_xattn_ln_beta, L1_xattn_dense_w, L1_xattn_dense_b, L1_ffn_Wg, L1_ffn_W1, L1_ffn_b1, L1_ffn_W2, L1_ffn_b2, L2_xattn_W_q, L2_xattn_b_q, L2_xattn_W_k, L2_xattn_b_k, L2_xattn_W_v, L2_xattn_b_v, L2_xattn_W_o, L2_xattn_b_o, L2_ffn_centroid, L2_ffn_Wg, L2_ffn_bg, L2_ffn_W1, L2_ffn_b1, L2_ffn_W2, L2_ffn_b2, L3_xattn_Wq, L3_xattn_bq, L3_xattn_Wk, L3_xattn_bk, L3_xattn_Wv, L3_xattn_bv, L3_xattn_Wo, L3_xattn_bo, L3_ffn_gate_w, L3_ffn_We):
    import jax
    import jax.numpy as jnp

    def _L0_xattn_ref(query, key, value, Wq, bq, Wk, bk, Wv, bv, Wo, bo):
        import jax, jax.numpy as jnp
        import numpy as np
        D_MODEL = 128
        N_HEADS = 16
        D_HEAD = D_MODEL // N_HEADS
        WINDOW = 128

        def _heads(x):
            B, S, _ = x.shape
            return x.reshape(B, S, N_HEADS, D_HEAD).transpose(0, 2, 1, 3)
        B, S, _ = query.shape
        q = _heads(query @ Wq.T + bq)
        k = _heads(key @ Wk.T + bk)
        v = _heads(value @ Wv.T + bv)
        scores = jnp.einsum('bhqd,bhkd->bhqk', q, k) / np.sqrt(D_HEAD).astype(np.float32)
        idx = jnp.arange(S)
        local = jnp.abs(idx[:, None] - idx[None, :]) <= WINDOW // 2
        scores = jnp.where(local[None, None, :, :], scores, -jnp.inf)
        attn = jax.nn.softmax(scores, axis=-1)
        ctx = jnp.einsum('bhqk,bhkd->bhqd', attn, v)
        ctx = ctx.transpose(0, 2, 1, 3).reshape(B, S, D_MODEL)
        return ctx @ Wo.T + bo

    def _L0_ffn_ref(x, gate_W, expert_W, out_W):
        import jax, jax.numpy as jnp
        import numpy as np
        TOP_P = 0.3
        B, S, D = x.shape
        E = gate_W.shape[0]
        N = B * S
        p = jax.nn.softmax(jnp.einsum('bsd,ed->bse', x, gate_W), axis=-1).reshape(N, E)
        tpi = (p > TOP_P).astype(jnp.int32)
        cnt = jnp.sum(tpi[:, :, None] == jnp.arange(E)[None, None, :], axis=1)
        scale = cnt.astype(x.dtype) * p
        x2 = x.reshape(N, D)
        h = jnp.einsum('nd,ehd->neh', x2, expert_W)
        final = jnp.einsum('neh,ne->nh', h, scale)
        out = jnp.einsum('nh,dh->nd', final, out_W).reshape(B, S, D)
        return out

    def _L1_xattn_ref(q, k, v, mask, wq, wk, wv, ln_gamma, ln_beta, dense_w, dense_b):
        import jax, jax.numpy as jnp
        import numpy as np
        D_MODEL = 128
        HEADS = 16
        DEPTH = D_MODEL // HEADS
        B, S = (4, 512)
        EPS_K = 1e-06
        EPS_LN = 1e-06

        def _layernorm(x, g, b):
            m = jnp.mean(x, axis=-1, keepdims=True)
            var = jnp.var(x, axis=-1, keepdims=True)
            return (x - m) * jax.lax.rsqrt(var + EPS_LN) * g + b

        def _split_heads(x):
            bsz, sl, _ = x.shape
            return x.reshape(bsz, sl, HEADS, DEPTH).transpose(0, 2, 1, 3)
        bsz = q.shape[0]
        em = mask[:, None, :, None]
        qh = _split_heads(_layernorm(q @ wq, ln_gamma, ln_beta))
        kh = _split_heads(_layernorm(k @ wk, ln_gamma, ln_beta))
        vh = _split_heads(_layernorm(v @ wv, ln_gamma, ln_beta))
        q_prime = jax.nn.relu(qh) + EPS_K
        k_prime = (jax.nn.relu(kh) + EPS_K) * em
        vh = vh * em
        kv = jnp.einsum('bhnd,bhne->bhde', k_prime, vh)
        z = 1.0 / (jnp.einsum('bhnd,bhd->bhn', q_prime, k_prime.sum(axis=-2)) + EPS_K)
        att = jnp.einsum('bhnd,bhde,bhn->bhne', q_prime, kv, z)
        att = att.reshape(bsz, -1, D_MODEL)
        out = att @ dense_w + dense_b
        return _layernorm(out, ln_gamma, ln_beta)

    def _L1_ffn_ref(x, Wg, W1, b1, W2, b2):
        import jax, jax.numpy as jnp
        import numpy as np
        B, S, H, E, K, F = (4, 256, 128, 8, 64, 512)
        b, s, h = x.shape
        logits = jnp.einsum('bsh,eh->bse', x, Wg)
        Sm = jnp.swapaxes(jax.nn.softmax(logits, axis=-1), 1, 2)
        G, I = jax.lax.top_k(Sm, K)
        ex = jnp.take_along_axis(x[:, None, :, :], I[..., None], axis=2)
        h1 = jax.nn.gelu(jnp.einsum('bekh,ehf->bekf', ex, W1) + b1[None, :, None, :])
        out = jnp.einsum('bekf,efh->bekh', h1, W2) + b2[None, :, None, :]
        out = G[..., None] * out
        new_x = jnp.zeros_like(x).at[jnp.arange(b)[:, None, None], I].add(out)
        return new_x

    def _L2_xattn_ref(query, key, value, mask, W_q, b_q, W_k, b_k, W_v, b_v, W_o, b_o):
        import jax, jax.numpy as jnp
        import numpy as np
        D_MODEL = 128
        N_HEADS = 16
        D_K = D_MODEL // N_HEADS
        B, S = (2, 256)
        b = query.shape[0]

        def proj(x, W, bias):
            y = x @ W.T + bias
            return y.reshape(b, -1, N_HEADS, D_K).transpose(0, 2, 1, 3)
        q = proj(query, W_q, b_q)
        k = proj(key, W_k, b_k)
        v = proj(value, W_v, b_v)
        scores = jnp.einsum('bhqd,bhkd->bhqk', q, k) / jnp.sqrt(jnp.float32(D_K)).astype(q.dtype)
        scores = jnp.where(mask, scores, jnp.finfo(scores.dtype).min)
        attn = jax.nn.softmax(scores, axis=-1)
        out = jnp.einsum('bhqk,bhkd->bhqd', attn, v)
        out = out.transpose(0, 2, 1, 3).reshape(b, -1, D_MODEL)
        return out @ W_o.T + b_o

    def _L2_ffn_ref(x, centroid, Wg, bg, W1, b1, W2, b2):
        import jax, jax.numpy as jnp
        import numpy as np
        E = 8
        K = 2
        D = 128
        H = 342
        B, S = (2, 256)

        def _moe_forward(x, centroid, Wg, bg, W1, b1, W2, b2):
            T = x.shape[0] * x.shape[1]
            xs = x.reshape(T, D)
            d2 = jnp.sum(xs * xs, axis=-1, keepdims=True) + jnp.sum(centroid * centroid, axis=-1)[None, :] - 2.0 * (xs @ centroid.T)
            dist = jnp.sqrt(jnp.maximum(d2, 1e-12))
            w, sel = jax.lax.top_k(dist, K)
            w = jax.nn.softmax(w.astype(jnp.float32), axis=1).astype(x.dtype)
            we = jnp.zeros((T, E), dtype=x.dtype).at[jnp.arange(T)[:, None], sel].add(w)
            out = jnp.zeros_like(xs)
            for e in range(E):
                h = jax.nn.silu(xs @ Wg[e] + bg[e]) * (xs @ W1[e] + b1[e])
                out = out + we[:, e:e + 1] * (h @ W2[e] + b2[e])
            return out.reshape(x.shape)
        return _moe_forward(x, centroid, Wg, bg, W1, b1, W2, b2)

    def _L3_xattn_ref(q, k, v, Wq, bq, Wk, bk, Wv, bv, Wo, bo):
        import jax, jax.numpy as jnp
        import numpy as np
        B, S, D = (2, 256, 128)
        H, HD = (16, 64)
        b, s, _ = q.shape
        qh = (q @ Wq.T + bq).reshape(b, s, H, HD).transpose(0, 2, 1, 3)
        kh = (k @ Wk.T + bk).reshape(b, s, H, HD).transpose(0, 2, 1, 3)
        vh = (v @ Wv.T + bv).reshape(b, s, H, HD).transpose(0, 2, 1, 3)
        scores = jnp.einsum('bhqd,bhkd->bhqk', qh, kh) / np.sqrt(HD).astype(np.float32)
        causal = jnp.tril(jnp.ones((s, s), bool))
        scores = jnp.where(causal, scores, -jnp.inf)
        attn = jax.nn.softmax(scores, axis=-1)
        out = jnp.einsum('bhqk,bhkd->bhqd', attn, vh)
        out = out.transpose(0, 2, 1, 3).reshape(b, s, H * HD)
        return out @ Wo.T + bo

    def _L3_ffn_ref(x, gate_w, We):
        import jax, jax.numpy as jnp
        import numpy as np
        top_k = 2
        logits = jnp.einsum('btd,ed->bte', x, gate_w)
        top_val, top_idx = jax.lax.top_k(logits, top_k)
        top_w = jax.nn.softmax(top_val, axis=-1)
        y_all = jnp.einsum('btd,edm->btem', x, We)
        x_experts = jnp.take_along_axis(y_all, top_idx[..., None], axis=2)
        out = jnp.sum(x_experts * top_w[..., None], axis=2)
        return out
    x = x + _L0_xattn_ref(_layernorm(x, axis=-1), ctx_1024, ctx_1024, L0_xattn_Wq, L0_xattn_bq, L0_xattn_Wk, L0_xattn_bk, L0_xattn_Wv, L0_xattn_bv, L0_xattn_Wo, L0_xattn_bo)
    x = x + _L0_ffn_ref(_layernorm(x, axis=-1), L0_ffn_gate_W, L0_ffn_expert_W, L0_ffn_out_W)
    x = x + _L1_xattn_ref(_layernorm(x, axis=-1), ctx_1024, ctx_1024, mask_BxS2_ff1, L1_xattn_wq, L1_xattn_wk, L1_xattn_wv, L1_xattn_ln_gamma, L1_xattn_ln_beta, L1_xattn_dense_w, L1_xattn_dense_b)
    x = x + _L1_ffn_ref(_layernorm(x, axis=-1), L1_ffn_Wg, L1_ffn_W1, L1_ffn_b1, L1_ffn_W2, L1_ffn_b2)
    x = x + _L2_xattn_ref(_layernorm(x, axis=-1), ctx_1024, ctx_1024, mask_1x1xSxS2_bk0, L2_xattn_W_q, L2_xattn_b_q, L2_xattn_W_k, L2_xattn_b_k, L2_xattn_W_v, L2_xattn_b_v, L2_xattn_W_o, L2_xattn_b_o)
    x = x + _L2_ffn_ref(_layernorm(x, axis=-1), L2_ffn_centroid, L2_ffn_Wg, L2_ffn_bg, L2_ffn_W1, L2_ffn_b1, L2_ffn_W2, L2_ffn_b2)
    x = x + _L3_xattn_ref(_layernorm(x, axis=-1), ctx_1024, ctx_1024, L3_xattn_Wq, L3_xattn_bq, L3_xattn_Wk, L3_xattn_bk, L3_xattn_Wv, L3_xattn_bv, L3_xattn_Wo, L3_xattn_bo)
    x = x + _L3_ffn_ref(_layernorm(x, axis=-1), L3_ffn_gate_w, L3_ffn_We)
    return x

_drawn_inputs = setup_inputs


def setup_inputs(seed=0):
    import zlib

    import numpy as np

    out = dict(_drawn_inputs(seed))
    spreads = {'L0_xattn_bq': (0.0, 0.1),
     'L0_xattn_bk': (0.0, 2.0),
     'L0_xattn_bv': (0.0, 0.1),
     'L0_xattn_bo': (0.0, 0.1),
     'L1_xattn_ln_gamma': (1.0, 0.2),
     'L1_xattn_ln_beta': (0.0, 0.1),
     'L1_xattn_dense_b': (0.0, 0.1),
     'L1_ffn_b1': (0.0, 0.1),
     'L1_ffn_b2': (0.0, 0.1),
     'L2_xattn_b_q': (0.0, 0.1),
     'L2_xattn_b_k': (0.0, 0.1),
     'L2_xattn_b_v': (0.0, 0.1),
     'L2_xattn_b_o': (0.0, 0.1),
     'L2_ffn_bg': (0.0, 0.8),
     'L2_ffn_b1': (0.0, 0.8),
     'L2_ffn_b2': (0.0, 0.1),
     'L3_xattn_bq': (0.0, 0.285),
     'L3_xattn_bk': (0.0, 2.0),
     'L3_xattn_bv': (0.0, 0.1),
     'L3_xattn_bo': (0.0, 0.282)}
    factors = {'L2_ffn_Wg': 6.251, 'L2_ffn_W1': 6.211, 'L2_ffn_W2': 6.444}
    for name, (base, spread) in spreads.items():
        noise = np.random.default_rng([zlib.crc32(name.encode()), seed]).standard_normal(out[name].shape)
        drawn = base * np.exp(spread * noise) if base else spread * noise
        out[name] = jnp.asarray(drawn.astype(out[name].dtype))
    for name, factor in factors.items():
        out[name] = (out[name] * factor).astype(out[name].dtype)
    return out
```

```python
from contextlib import ExitStack

import concourse.bass as bass
from concourse import mybir

F32 = mybir.dt.float32
BF16 = mybir.dt.bfloat16
U8 = mybir.dt.uint8
I32 = mybir.dt.int32
ALU = mybir.AluOpType
ACT = mybir.ActivationFunctionType
AX = mybir.AxisListType

P = 128
B = 32
G = 4
NG = B // G
W = G * P
H = 16
DH = P // H
E = 8
LN_EPS = 1e-5
NEG = -3.38e38
PARTS = 3
TERMS = ((0, 0), (1, 0), (2, 0), (0, 1), (1, 1), (0, 2))


def ds(start, n):
    return bass.ds(start, n)


class Arena:

    def __init__(self, tensor, words):
        self.tensor, self.words, self.at = tensor, words, 0

    def restart(self):
        self.at = 0

    def take(self, shape, dtype=F32):
        n = 1
        for s in shape:
            n *= s
        words = n if dtype == F32 else (n + 1) // 2
        words = (words + 15) // 16 * 16
        piece = self.tensor[:, self.at:self.at + words]
        self.at += words
        assert self.at <= self.words, self.at
        if dtype != F32:
            piece = piece.bitcast(dtype)
        piece = piece[:, 0:n]
        names = " ".join(f"a{i}" for i in range(len(shape)))
        sizes = {f"a{i}": s for i, s in enumerate(shape)}
        return piece if len(shape) == 1 else piece.rearrange(f"p ({names}) -> p {names}", **sizes)


def program(nc, t, out):
    ctx = ExitStack()
    with ctx:
        def sb(name, shape, dtype=F32):
            return ctx.enter_context(nc.sbuf_tensor(name, shape, dtype))

        def sem(name):
            return ctx.enter_context(nc.semaphore(name))

        x = sb("x", [P, B, P])
        mean = sb("mean", [P, B])
        var_eps = sb("var_eps", [P, B])
        rstd = sb("rstd", [P, B])
        ident = sb("ident", [P, P])
        identb = sb("identb", [P, P], BF16)
        shift_rows = sb("shift_rows", [P, H, P], BF16)
        ones_cols = sb("ones_cols", [P, 4, 32])
        neg_half = sb("neg_half", [P, G])
        mask_bias = {l: (sb(f"maskS{l}", [P, 4, P], BF16), sb(f"maskT{l}", [P, 4, P], BF16)) for l in (0, 2, 3)}
        mask_words = sb("mask_words", [P, 2, P // 4], I32)
        aw = {l: {n: sb(f"w{n}{l}", [P, P]) for n in "qkvo"} for l in (0, 2)}
        acol = {l: sb(f"acol{l}", [P, 4]) for l in (0, 2)}
        arow = {l: sb(f"arow{l}", [P, 2, P]) for l in (0, 2)}
        gates = {l: sb(f"gate{l}", [P, E]) for l in range(4)}
        expert0 = sb("expert0", [P, 2, P])
        outw0 = sb("outw0", [P, P])
        folded = sb("folded", [P, 2, P])[:]
        we3 = sb("we3", [P, E, P])[:]
        iota_i = sb("iota_i", [P, 64], mybir.dt.int32)[:]
        wide = sb("wide", [P, 8704])[:]
        earlier = sb("earlier", [P, E * E])
        ARENA = 33 * 1024
        arena = Arena(sb("arena", [P, ARENA]), ARENA)
        bank = [ctx.enter_context(nc.psum_tensor(f"bank{i}", [P, 512], F32)) for i in range(8)]

        phase_done = sem("phase_done")
        x_in = sem("x_in")
        ww_in = sem("ww_in")
        x_out = sem("x_out")
        fw_in = {l: sem(f"fw_in{l}") for l in range(4)}
        fw_loads = {0: 3, 1: 3 + 1 + E + 1, 2: 1 + 3 + 2 + 1, 3: 2}
        w_in = {l: sem(f"w_in{l}") for l in range(4)}
        setup_v = sem("setup_v")

        def barrier(eng, phase):
            eng.drain().then_inc(phase_done, 1)
            eng.wait_ge(phase_done, 5 * (phase + 1))

        twins = {}

        def twin_sems(maker, names):
            if maker not in twins:
                twins[maker] = {n: sem(f"{n}_{maker}") for n in names}
            return twins[maker]

        def clear_twins(pool):
            for maker in twins.values():
                for signal in maker.values():
                    pool.sem_clear(signal)

        def loop(eng, group, groups=NG):
            with eng.Fori(0, groups // 2 - 1) as i:
                for u in range(2):
                    group(2 * i + u, u, False)
            for u in range(2):
                group(groups - 2 + u, u, u == 1)

        def load_sync(sp):
            for g in range(NG):
                sp.dma_start(x[:, g * G:(g + 1) * G, :],
                             t["x"][g * G:(g + 1) * G].rearrange("b s d -> s b d")).then_inc(x_in, 16)
            for l in (0, 2):
                for n in "qkvo":
                    sp.dma_start(aw[l][n][:], t[f"w{n}{l}"]).then_inc(w_in[l], 16)
                for i, n in enumerate("qk"):
                    sp.dma_start(acol[l][:, i:i + 1], t[f"b{n}{l}"].rearrange("(p a) -> p a", a=1)).then_inc(w_in[l], 16)
                for i, n in enumerate("vo"):
                    row = t[f"b{n}{l}"].rearrange("(a n) -> a n", a=1)
                    sp.dma_start(arow[l][:, i, :], row.broadcast_to([P, P])).then_inc(w_in[l], 16)
            sp.dma_start(gates[0][:], t["gate0"]).then_inc(fw_in[0], 16)
            sp.dma_start(expert0[:], t["expert0"]).then_inc(fw_in[0], 16)
            sp.dma_start(outw0[:], t["outw0"]).then_inc(fw_in[0], 16)
            sp.dma_start(gates[1][:], t["gate1"]).then_inc(fw_in[1], 16)
            sp.dma_start(wide[:, 0:4096], t["w1_1"]).then_inc(fw_in[1], 16)
            sp.dma_start(wide[:, 4096:8192], t["w2_1"]).then_inc(fw_in[1], 16)
            sp.dma_start(gates[2][:], t["gate2"]).then_inc(fw_in[2], 16)
            sp.dma_start(gates[3][:], t["gate3"]).then_inc(fw_in[3], 16)
            sp.dma_start(we3, t["we3"]).then_inc(fw_in[3], 16)
            for i in range(2):
                sp.dma_start(mask_words[:, i, :], t["mask2"][i]).then_inc(w_in[2], 16)
            barrier(sp, 0)

        def load_pool(pool):
            pool.memset(ident[:], 0.0)
            pool.memset(identb[:], 0.0)
            pool.memset(shift_rows[:], 0.0)
            pool.memset(ones_cols[:], 0.0)
            pool.memset(neg_half[:], -0.5)
            pool.memset(earlier[:], 1.0)
            for l in (0, 3):
                for m in mask_bias[l]:
                    pool.memset(m[:], 0.0)
            pool.drain()
            for m in (ident, identb):
                pool.affine_select(out=m[:], in_=m[:], compare_op=ALU.not_equal, fill=1.0, base=0,
                                   pattern=[[-1, P]], channel_multiplier=1)
            pool.affine_select(out=shift_rows[:], in_=shift_rows[:], compare_op=ALU.not_equal, fill=1.0,
                               base=0, pattern=[[-1, H], [0, P]], channel_multiplier=1)
            for j in range(4):
                pool.memset(ones_cols[:, j, 8 * j:8 * j + 8], 1.0)
            for m in mask_bias[0]:
                pool.affine_select(out=m[:], in_=m[:], compare_op=ALU.is_ge, fill=NEG, base=64,
                                   pattern=[[0, 4], [-1, P]], channel_multiplier=1)
            pool.affine_select(out=mask_bias[3][0][:], in_=mask_bias[3][0][:], compare_op=ALU.is_ge, fill=NEG,
                               base=0, pattern=[[0, 4], [-1, P]], channel_multiplier=1)
            pool.affine_select(out=mask_bias[3][1][:], in_=mask_bias[3][1][:], compare_op=ALU.is_ge, fill=NEG,
                               base=0, pattern=[[0, 4], [1, P]], channel_multiplier=-1)
            pool.drain()
            pool.affine_select(out=shift_rows[:], in_=shift_rows[:], compare_op=ALU.not_equal, fill=1.0,
                               base=-H, pattern=[[-1, H], [0, P]], channel_multiplier=1)
            for m in mask_bias[0]:
                pool.affine_select(out=m[:], in_=m[:], compare_op=ALU.is_ge, fill=NEG, base=64,
                                   pattern=[[0, 4], [1, P]], channel_multiplier=-1)
            pool.affine_select(out=earlier[:].rearrange("p (e f) -> p e f", e=E),
                               in_=earlier[:].rearrange("p (e f) -> p e f", e=E), compare_op=ALU.is_gt, fill=0.0,
                               base=0, pattern=[[1, E], [-1, E]], channel_multiplier=0)
            for g in range(NG):
                pool.wait_ge(setup_v, g + 1)
                rstd_of(pool, g * G)
            barrier(pool, 0)

        def stats_of(dve, first, bn, agg):
            for j in range(G):
                dve.bn_stats(bn[:, j, :], x[:, ds(first + j, 1), :])
            dve.drain()
            for j in range(G):
                dve.bn_aggr(agg[:, j, :], bn[:, j, :])
            dve.drain()
            dve.tensor_copy(mean[:, ds(first, G)], agg[:, :, 0])
            return dve.tensor_scalar(var_eps[:, ds(first, G)], agg[:, :, 1], LN_EPS, None, ALU.add)

        def rstd_of(pool, first):
            pool.tensor_tensor(rstd[:, ds(first, G)], var_eps[:, ds(first, G)], neg_half[:], ALU.pow)

        bn0 = sb("bn0", [P, G, 6])
        agg0 = sb("agg0", [P, G, 2])

        def load_dve(dve):
            dve.wait_ge(w_in[2], 16 * 10)
            for i, m in enumerate(mask_bias[2]):
                for j in range(4):
                    dve.tensor_scalar(m[:, j, :], mask_words[:, i, :].bitcast(U8), -1.0, -NEG, ALU.add, ALU.mult)
            for l in (0, 2):
                dve.wait_ge(w_in[l], 16 * (8 + (l == 2) * 2))
                dve.tensor_scalar(acol[l][:, 2:3], acol[l][:, 0:1], float(DH) ** -0.5, None, ALU.mult)
            for g in range(NG):
                dve.wait_ge(x_in, 16 * (g + 1))
                stats_of(dve, g * G, bn0, agg0).then_inc(setup_v, 1)
                dve.drain()
            barrier(dve, 0)

        def small_heads(l, phase):
            s = twin_sems("heads8", (
                "ctx_in0", "ctx_in1", "xn_ready", "tr_ready", "xnT_ready", "q_ready", "q_evac", "k_ready",
                "k_evac", "v_mm", "v_evac", "parts_ready", "parts_out", "stack_in0", "stack_in1", "s_ready",
                "s_free", "mhl_ready", "mt_ready", "mts_ready", "st_ready", "st_free", "pv_ready", "o_free",
                "o_ready", "x_done", "xb_ready", "zero_ready", "stats_ready"))
            arena.restart()
            stack_q = [arena.take([H, W], BF16) for _ in range(2)]
            stack_k = [arena.take([H, W], BF16) for _ in range(2)]
            probs = [arena.take([H, P]) for _ in range(2)]
            values = [arena.take([G, H, 32]) for _ in range(2)]
            ctxT = [arena.take([W]) for _ in range(2)]
            xn = [arena.take([G, P]) for _ in range(2)]
            xb = [arena.take([G, P]) for _ in range(2)]
            xnT = arena.take([W])
            qf, kf, rest = arena.take([W]), arena.take([W]), arena.take([W])
            parts = [arena.take([PARTS, W], BF16) for _ in range(2)]
            attnT = arena.take([2, G, P])
            mx, mhl = arena.take([2, H]), arena.take([2, 2 * H], BF16)
            mts = arena.take([2, P], BF16)
            inv = arena.take([2, P])
            bn, agg = arena.take([G, 6]), arena.take([G, 2])
            qd = [[nc.dram_tensor(f"parts{n}{l}{u}", [PARTS, P, W], BF16).ap() for u in range(2)] for n in "qk"]
            S, T, O, M = bank[0:2], bank[2:4], bank[4:6], bank[6:8]
            wq, wk, wv, wo = (aw[l][n] for n in "qkvo")
            maskS, maskT = mask_bias[l]
            nk = len(TERMS)

            def sync(sp):
                def load_ctx(g, u):
                    sp.dma_start(ctxT[u], t["ctxT"][:, ds(g * W, W)]).then_inc(s[f"ctx_in{u}"], 16)

                def exchange(g, u):
                    sp.wait_ge(s["parts_ready"], g + 1)
                    for a in range(2):
                        sp.dma_start(qd[a][u].rearrange("a p t -> p a t"), parts[a]).then_inc(s["parts_out"], 16)
                    sp.wait_ge(s["parts_out"], 32 * g + 32)
                    rows = [qd[a][u].rearrange("a (d h) t -> a d (h t)", h=H) for a in range(2)]
                    for a, stack in ((0, stack_q[u]), (1, stack_k[u])):
                        flat = stack.rearrange("p h t -> p (h t)")
                        for n, term in enumerate(TERMS):
                            sp.dma_start(flat[DH * n:DH * n + DH, :], rows[a][term[a]]).then_inc(s[f"stack_in{u}"], 16)

                load_ctx(0, 0)
                load_ctx(1, 1)
                if l == 2:
                    load_wide2(sp)
                sp.wait_ge(s["zero_ready"], 1)
                exchange(0, 0)

                def group(g, u, last):
                    if last:
                        return
                    sp.wait_ge(s["v_mm"], g + 1)
                    if not isinstance(g, int) or g + 2 < NG:
                        load_ctx(g + 2, u)
                    exchange(g + 1, 1 - u)
                loop(sp, group)
                barrier(sp, phase)

            def tensor(pe):
                def front(g, u, first=False):
                    pe.wait_ge(s["xn_ready"], g + 1)
                    if not first:
                        pe.wait_ge(s["k_evac"], g)
                        pe.wait_ge(s["x_done"], g - 1)
                    for j in range(G):
                        mm = pe.transpose(M[0][:, j * P:(j + 1) * P], xn[u][:, j, :], ident[:])
                    mm.then_inc(s["tr_ready"], 1)
                    pe.wait_ge(s["xnT_ready"], g + 1)
                    if not first:
                        pe.wait_ge(s["v_evac"], g)
                    pe.matmul(M[1][:], wq[:], xnT, start=True, stop=True).then_inc(s["q_ready"], 1)
                    pe.wait_ge(s[f"ctx_in{u}"], (g - u) * 8 + 16)
                    pe.matmul(M[0][:], wk[:], ctxT[u], start=True, stop=True).then_inc(s["k_ready"], 1)
                    pe.wait_ge(s["q_evac"], g + 1)
                    for j in range(G):
                        mm = pe.matmul(M[1][:, j * P:(j + 1) * P], ctxT[u][:, j * P:(j + 1) * P], wv[:],
                                       start=True, stop=True)
                    mm.then_inc(s["v_mm"], 1)

                def scores(n, u, j):
                    for c in range(4):
                        pe.wait_ge(s["s_free"], 4 * n + c + 1)
                        pe.matmul(S[c % 2][:], identb[:], maskS[:].rearrange("p a k -> p (a k)"),
                                  start=True, stop=False, skip_group_check=True)
                        for h in range(4 * c, 4 * c + 4):
                            mm = pe.matmul(S[c % 2][:, (h % 4) * P:(h % 4 + 1) * P],
                                           stack_q[u][:, h, j * P:(j + 1) * P],
                                           stack_k[u][:, h, j * P:(j + 1) * P],
                                           start=False, stop=(h % 4 == 3), skip_group_check=True)
                        mm.then_inc(s["s_ready"], 1)

                def turn_max(n, b):
                    pe.wait_ge(s["mhl_ready"], n + 1)
                    pe.wait_ge(s["o_free"], n + 1)
                    pe.transpose(O[b][0:2 * H, 256:320].bitcast(BF16), mhl[:, b, :], identb[:]).then_inc(s["mt_ready"], 1)

                def scoresT(n, u, j, b):
                    for c in range(4):
                        pe.wait_ge(s["st_free"], 4 * n + c + 1)
                        pe.matmul(T[c % 2][:], identb[:], maskT[:].rearrange("p a k -> p (a k)"),
                                  start=True, stop=False, skip_group_check=True)
                        for h in range(4 * c, 4 * c + 4):
                            pe.matmul(T[c % 2][:, (h % 4) * P:(h % 4 + 1) * P],
                                      stack_k[u][:, h, j * P:(j + 1) * P],
                                      stack_q[u][:, h, j * P:(j + 1) * P],
                                      start=False, stop=False, skip_group_check=True)
                        if c == 0:
                            pe.wait_ge(s["mts_ready"], n + 1)
                        for h in range(4 * c, 4 * c + 4):
                            mm = pe.matmul(T[c % 2][:, (h % 4) * P:(h % 4 + 1) * P],
                                           shift_rows[:, h, :], mts[:, b, :],
                                           start=False, stop=(h % 4 == 3), skip_group_check=True)
                        mm.then_inc(s["st_ready"], 1)

                def attend(n, u, j, b):
                    for c in range(4):
                        pe.wait_ge(s["st_free"], 4 * n + c + 3)
                        rows = slice(32 * c, 32 * c + 32)
                        for k, lhs in enumerate((lambda h: values[u][:, j, h, :], lambda h: ones_cols[:, h % 4, :])):
                            for h in range(4 * c, 4 * c + 4):
                                mm = pe.matmul(O[b][rows, k * P:(k + 1) * P], lhs(h), probs[b][:, h, :],
                                               start=(h % 4 == 0), stop=(h % 4 == 3), skip_group_check=True)
                    mm.then_inc(s["pv_ready"], 1)

                pe.wait_ge(w_in[l], 16 * (8 + (l == 2) * 2))
                front(0, 0, first=True)
                pe.wait_ge(s["stack_in0"], 16 * 2 * nk)
                scores(0, 0, 0)

                def group(g, u, last):
                    for j in range(G):
                        n, b = g * G + j, j % 2
                        turn_max(n, b)
                        if j == 0:
                            pe.wait_ge(s["v_evac"], g + 1)
                        scoresT(n, u, j, b)
                        if j < G - 1:
                            scores(n + 1, u, j + 1)
                        elif not last:
                            pe.wait_ge(s[f"stack_in{1 - u}"], stack_count(g + 1, 1 - u))
                            scores(n + 1, 1 - u, 0)
                        attend(n, u, j, b)
                        if j == 0 and not last:
                            front(g + 1, 1 - u)
                    pe.wait_ge(s["k_evac"], g + 1 if last else g + 2)
                    pe.wait_ge(s["o_free"], g * G + G + 2)
                    for j in range(G):
                        mm = pe.matmul(M[0][:, j * P:(j + 1) * P], attnT[:, u, j, :], wo[:], start=True, stop=True)
                    mm.then_inc(s["o_ready"], 1)
                loop(pe, group)
                barrier(pe, phase)

            def stack_count(g, u):
                return (g - u) * (16 * nk) + 32 * nk

            def scalar(act):
                def front(g, u):
                    act.wait_ge(s["tr_ready"], g + 1)
                    act.activation(xnT, M[0][:], ACT.Copy).then_inc(s["xnT_ready"], 1)
                    act.wait_ge(s["q_ready"], g + 1)
                    act.wait_ge(s["parts_ready"], g)
                    act.activation(qf, M[1][:], ACT.Identity, bias=acol[l][:, 2:3],
                                   scale=float(DH) ** -0.5).then_inc(s["q_evac"], 1)
                    act.wait_ge(s["k_ready"], g + 1)
                    act.activation(kf, M[0][:], ACT.Identity, bias=acol[l][:, 1:2]).then_inc(s["k_evac"], 1)

                front(0, 0)
                for b in range(2):
                    act.activation(mts[:, b, :], identb[:], ACT.Copy, scale=0.0)
                act.drain()

                def group(g, u, last):
                    for j in range(G):
                        n, b = g * G + j, j % 2
                        act.wait_ge(s["mt_ready"], n + 1)
                        act.activation(mts[0:2 * H, b, :], O[b][0:2 * H, 256:320].bitcast(BF16),
                                       ACT.Copy).then_inc(s["mts_ready"], 1)
                        for c in range(4):
                            act.wait_ge(s["st_ready"], 4 * n + c + 1)
                            act.activation(probs[b][:, 4 * c:4 * c + 4, :].rearrange("p a q -> p (a q)"),
                                           T[c % 2][:], ACT.Exp).then_inc(s["st_free"], 1)
                        if j == 0 and not last:
                            front(g + 1, 1 - u)
                loop(act, group)
                barrier(act, phase)

            def vector(dve):
                def normed(g, u):
                    for j in range(G):
                        mm = dve.tensor_scalar(xn[u][:, j, :], x[:, ds(g * G + j, 1), :], mean[:, ds(g * G + j, 1)],
                                               rstd[:, ds(g * G + j, 1)], ALU.subtract, ALU.mult)
                    mm.then_inc(s["xn_ready"], 1)

                def front(g, u, first=False):
                    dve.wait_ge(s["v_mm"], g + 1)
                    for j in range(G):
                        src = M[1][:, j * P:(j + 1) * P].rearrange("p (c j e) -> p c j e", c=4, j=4)
                        bias = arow[l][:, 0, :].rearrange("p (c j e) -> p c j e", c=4, j=4)
                        mm = dve.tensor_tensor(diagonal(values[u], j), src, bias, ALU.add)
                    mm.then_inc(s["v_evac"], 1)
                    if not first:
                        dve.wait_ge(s["parts_out"], 32 * g)
                    for a, (full, ready) in enumerate(((qf, "q_evac"), (kf, "k_evac"))):
                        dve.wait_ge(s[ready], g + 1)
                        dve.tensor_copy(parts[a][:, 0, :], full)
                        dve.drain()
                        dve.tensor_tensor(rest, full, parts[a][:, 0, :], ALU.subtract)
                        dve.drain()
                        dve.tensor_copy(parts[a][:, 1, :], rest)
                        dve.drain()
                        mm = dve.tensor_tensor(parts[a][:, 2, :], rest, parts[a][:, 1, :], ALU.subtract)
                    mm.then_inc(s["parts_ready"], 1)

                def maxima(n, b):
                    for c in range(4):
                        dve.wait_ge(s["s_ready"], 4 * n + c + 1)
                        dve.tensor_reduce(mx[:, b, 4 * c:4 * c + 4], S[c % 2][:].rearrange("p (a k) -> p a k", a=4),
                                          AX.X, ALU.max).then_inc(s["s_free"], 1)
                    dve.drain()
                    dve.tensor_scalar(mhl[:, b, 0:H], mx[:, b, :], -1.0, None, ALU.mult)
                    dve.drain()
                    dve.scalar_tensor_tensor(out=mhl[:, b, H:2 * H], in0=mx[:, b, :], scalar=-1.0,
                                             in1=mhl[:, b, 0:H], op0=ALU.mult, op1=ALU.subtract
                                             ).then_inc(s["mhl_ready"], 1)

                for u in range(2):
                    dve.memset(values[u].rearrange("p a b c -> p (a b c)"), 0.0)
                    dve.memset(stack_q[u].rearrange("p h t -> p (h t)").bitcast(F32), 0.0)
                    mm = dve.memset(stack_k[u].rearrange("p h t -> p (h t)").bitcast(F32), 0.0)
                mm.then_inc(s["zero_ready"], 1)
                dve.drain().then_inc(s["s_free"], 2)
                normed(0, 0)
                front(0, 0, first=True)
                maxima(0, 0)

                def group(g, u, last):
                    for j in range(G):
                        n, b = g * G + j, j % 2
                        if j == 0 and not last:
                            normed(g + 1, 1 - u)
                        if j < G - 1 or not last:
                            maxima(n + 1, 1 - b)
                        dve.wait_ge(s["pv_ready"], n + 1)
                        dve.reciprocal(inv[:, b, :], O[b][:, P:2 * P])
                        dve.drain()
                        dve.tensor_tensor(attnT[:, u, j, :], O[b][:, 0:P], inv[:, b, :], ALU.mult).then_inc(s["o_free"], 1)
                        if j == 0 and not last:
                            front(g + 1, 1 - u)
                    dve.wait_ge(s["o_ready"], g + 1)
                    dve.wait_ge(s["xb_ready"], g + 1)
                    dve.tensor_tensor(x[:, ds(g * G, G), :], M[0][:].rearrange("p (a b) -> p a b", a=G), xb[u],
                                      ALU.add).then_inc(s["x_done"], 1)
                    dve.drain()
                    stats_of(dve, g * G, bn, agg).then_inc(s["stats_ready"], 1)
                loop(dve, group)
                barrier(dve, phase)

            def gpsimd(pool):
                pool.engine_nop().then_inc(s["st_free"], 2)
                pool.engine_nop().then_inc(s["o_free"], 2)

                def group(g, u, last):
                    bo = arow[l][:, 1, :].unsqueeze(1).broadcast_to([P, G, P])
                    pool.tensor_tensor(xb[u], x[:, ds(g * G, G), :], bo, ALU.add).then_inc(s["xb_ready"], 1)
                    pool.wait_ge(s["stats_ready"], g + 1)
                    rstd_of(pool, g * G)
                pool.wait_ge(w_in[l], 16 * (8 + (l == 2) * 2))
                loop(pool, group)
                barrier(pool, phase)

            return sync, tensor, scalar, vector, gpsimd

        def diagonal(tile, j):
            v = tile[:, j, :, :].rearrange("p h e -> p (h e)")
            a = v.copy()
            step, count = v.ap[0]
            return bass.AP(tensor=v.tensor, offset=v.offset, ap=[[step, count], [P, 4], [40, 4], [1, 8]])

        def rank_below(dve, logits, cmp, cmp2, rank, below):
            mine = logits.unsqueeze(3).broadcast_to([P, G, E, E])
            other = logits.unsqueeze(2).broadcast_to([P, G, E, E])
            early = earlier[:].unsqueeze(1).broadcast_to([P, G, E * E]).rearrange("p g (e f) -> p g e f", e=E)
            dve.tensor_tensor(cmp, other, mine, ALU.is_gt)
            dve.tensor_tensor(cmp2, other, mine, ALU.is_equal)
            dve.drain()
            dve.tensor_tensor(cmp2.rearrange("p g e f -> p g (e f)"), cmp2.rearrange("p g e f -> p g (e f)"),
                              early.rearrange("p g e f -> p g (e f)"), ALU.mult)
            dve.drain()
            dve.tensor_tensor(cmp, cmp, cmp2, ALU.add)
            dve.drain()
            dve.tensor_reduce(rank, cmp, AX.X, ALU.add)
            dve.drain()
            dve.tensor_scalar(rank, rank, float(below), None, ALU.is_lt)
            dve.drain()

        def narrow(l, phase):
            s = twin_sems("narrow", (
                "xn_ready", "tr_ready", "xnT_ready", "logits_ready", "shifted_ready", "exp_ready", "h_ready",
                "h_free", "stats_ready", "fold_ready", "folded"))
            n_exp = 2 if l == 0 else E
            arena.restart()
            xn = [arena.take([G, P]) for _ in range(2)]
            xnT = [arena.take([W]) for _ in range(2)]
            z, ez = arena.take([G, E]), arena.take([G, E])
            logits = arena.take([G, E])
            cmp, cmp2 = arena.take([G, E, E]), arena.take([G, E, E])
            sel, top = arena.take([G, E]), arena.take([G])
            total, count = arena.take([G]), arena.take([G, 2])
            weight = [arena.take([G, E]) for _ in range(2)]
            bn, agg = arena.take([G, 6]), arena.take([G, 2])
            banks = n_exp * P // 512 or 1
            ring = 4 // banks
            gate = gates[l]
            experts = folded if l == 0 else we3

            def sync(sp):
                barrier(sp, phase)

            def tensor(pe):
                def front(g, u):
                    pe.wait_ge(s["xn_ready"], g + 1)
                    for j in range(G):
                        mm = pe.transpose(bank[u][:, j * P:(j + 1) * P], xn[u][:, j, :], ident[:])
                    mm.then_inc(s["tr_ready"], 1)
                    pe.wait_ge(s["xnT_ready"], g + 1)
                    for j in range(G):
                        mm = pe.matmul(bank[2 + u][:, j * E:(j + 1) * E], xnT[u][:, j * P:(j + 1) * P], gate[:],
                                       start=True, stop=True)
                    mm.then_inc(s["logits_ready"], 1)

                pe.wait_ge(fw_in[l], 16 * fw_loads[l])
                if l == 0:
                    for e in range(n_exp):
                        mm = pe.matmul(bank[4][:, e * P:(e + 1) * P], expert0[:, e, :], outw0[:], start=True, stop=True)
                    mm.then_inc(s["fold_ready"], 1)
                    pe.wait_ge(s["folded"], 1)
                front(0, 0)

                def group(g, u, last):
                    if not last:
                        front(g + 1, 1 - u)
                    for j in range(G):
                        n = g * G + j
                        pe.wait_ge(s["h_free"], n + 1)
                        for k in range(banks):
                            width = min(512, n_exp * P)
                            mm = pe.matmul(bank[4 + (j % ring) * banks + k][:, 0:width],
                                           xnT[u][:, j * P:(j + 1) * P],
                                           experts.rearrange("p e m -> p (e m)")[:, 512 * k:512 * k + width],
                                           start=True, stop=True)
                        mm.then_inc(s["h_ready"], 1)
                loop(pe, group)
                barrier(pe, phase)

            def scalar(act):
                def front(g, u):
                    act.wait_ge(s["tr_ready"], g + 1)
                    act.activation(xnT[u], bank[u][:], ACT.Copy).then_inc(s["xnT_ready"], 1)
                    act.wait_ge(s["shifted_ready"], g + 1)
                    act.activation(ez, z, ACT.Exp).then_inc(s["exp_ready"], 1)

                if l == 0:
                    act.wait_ge(s["fold_ready"], 1)
                    act.activation(folded.rearrange("p e m -> p (e m)"), bank[4][:, 0:2 * P], ACT.Copy).then_inc(s["folded"], 1)
                front(0, 0)

                def group(g, u, last):
                    if not last:
                        front(g + 1, 1 - u)
                loop(act, group)
                barrier(act, phase)

            def vector(dve):
                def normed(g, u):
                    for j in range(G):
                        mm = dve.tensor_scalar(xn[u][:, j, :], x[:, ds(g * G + j, 1), :], mean[:, ds(g * G + j, 1)],
                                               rstd[:, ds(g * G + j, 1)], ALU.subtract, ALU.mult)
                    mm.then_inc(s["xn_ready"], 1)

                def weights(g, u):
                    lg = bank[2 + u][:, 0:G * E].rearrange("p (g e) -> p g e", g=G)
                    dve.wait_ge(s["logits_ready"], g + 1)
                    dve.tensor_copy(logits, lg)
                    dve.drain()
                    dve.tensor_reduce(top, logits, AX.X, ALU.max)
                    dve.drain()
                    dve.tensor_tensor(z, logits, top.unsqueeze(2).broadcast_to([P, G, E]),
                                      ALU.subtract).then_inc(s["shifted_ready"], 1)
                    if l == 3:
                        rank_below(dve, logits, cmp, cmp2, sel, 2)
                    dve.wait_ge(s["exp_ready"], g + 1)
                    if l == 3:
                        dve.tensor_tensor(ez, ez, sel, ALU.mult)
                        dve.drain()
                    dve.tensor_reduce(total, ez, AX.X, ALU.add)
                    dve.drain()
                    dve.reciprocal(total, total)
                    dve.drain()
                    dve.tensor_tensor(weight[u], ez, total.unsqueeze(2).broadcast_to([P, G, E]), ALU.mult)
                    dve.drain()
                    if l == 0:
                        dve.tensor_scalar(sel, weight[u], 0.3, None, ALU.is_gt)
                        dve.drain()
                        dve.tensor_reduce(count[:, :, 1:2].rearrange("p g a -> p (g a)"), sel, AX.X, ALU.add)
                        dve.drain()
                        dve.tensor_scalar(count[:, :, 0], count[:, :, 1], -1.0, float(E), ALU.mult, ALU.add)
                        dve.drain()
                        dve.tensor_tensor(weight[u][:, :, 0:2], weight[u][:, :, 0:2], count, ALU.mult)
                        dve.drain()

                dve.drain().then_inc(s["h_free"], ring)
                normed(0, 0)
                weights(0, 0)

                def group(g, u, last):
                    if not last:
                        normed(g + 1, 1 - u)
                    for j in range(G):
                        n = g * G + j
                        dve.wait_ge(s["h_ready"], n + 1)
                        for e in range(n_exp):
                            slot = bank[4 + (j % ring) * banks + e // 4]
                            here = x[:, ds(n, 1), :].rearrange("p a m -> p (a m)")
                            mm = dve.scalar_tensor_tensor(out=here, in0=slot[:, (e % 4) * P:(e % 4 + 1) * P],
                                                          scalar=weight[u][:, j, e:e + 1], in1=here,
                                                          op0=ALU.mult, op1=ALU.add)
                            if e == n_exp - 1:
                                mm.then_inc(s["h_free"], 1)
                            dve.drain()
                    if l == 0:
                        stats_of(dve, g * G, bn, agg).then_inc(s["stats_ready"], 1)
                    if not last:
                        weights(g + 1, 1 - u)
                loop(dve, group)
                barrier(dve, phase)

            def gpsimd(pool):
                if l == 0:
                    def group(g, u, last):
                        pool.wait_ge(s["stats_ready"], g + 1)
                        rstd_of(pool, g * G)
                    loop(pool, group)
                barrier(pool, phase)

            return sync, tensor, scalar, vector, gpsimd

        def linear_attention(phase):
            s = {n: sem(f"{n}_1") for n in (
                "ctx_in0", "ctx_in1", "xn_ready", "tr_ready", "xnT_ready", "proj_ready", "var_ready", "rs_ready",
                "normed_ready", "q_final", "kv_final", "v_scaled", "qT_ready", "qT_evac", "kv_ready", "kv_masked",
                "att_ready", "att_normed", "swap_ready", "swap_a", "swap_v",
                "attT_ready", "attT_evac", "y_ready", "yvar_ready", "yrs_ready",
                "x_done", "stats_ready")}
            KW = P + H
            EPS_K = EPS_1 = 1e-6
            arena.restart()
            ctxT = [arena.take([W]) for _ in range(2)]
            xn = arena.take([G, P])
            xnT = arena.take([W])
            proj = [[arena.take([G, P]) for _ in range(3)] for _ in range(2)]
            v_wide = [arena.take([G, KW]) for _ in range(2)]
            qT = arena.take([W])
            kvx = arena.take([G, KW])
            den = arena.take([G, H])
            att = arena.take([G, P])
            attT = arena.take([W])
            y = arena.take([G, P])
            bn, agg = arena.take([3 * G, 6]), arena.take([3 * G, 2])
            bny, aggy = arena.take([G, 6]), arena.take([G, 2])
            ve, rs, nm = arena.take([3 * G]), arena.take([3 * G]), arena.take([3 * G])
            vey, rsy = arena.take([G]), arena.take([G])
            bnx, aggx = arena.take([G, 6]), arena.take([G, 2])
            gb = arena.take([3, P])
            em = arena.take([B])
            block_mask = arena.take([KW])
            w = arena.take([4, P])
            half = arena.take([3 * G])
            swap = arena.take([2, DH, P])
            T, Q, K, V, KV0, KV1, A0, A1 = bank
            swap_bank = ((A0, A1), (KV0, KV1))

            def swapped(j, half):
                return swap[0:H, j % 2, :, :].rearrange("p k (n e) -> p e (k n)", e=DH)[:, 4 * half:4 * half + 4, :]

            def bc(row):
                return row.unsqueeze(1).broadcast_to([P, G, P])

            def sync(sp):
                for i in range(4):
                    sp.dma_start(w[:, i, :], t["w1"][i]).then_inc(ww_in, 16)
                for i in range(3):
                    row = t["row1"][i].rearrange("(a n) -> a n", a=1)
                    sp.dma_start(gb[:, i, :], row.broadcast_to([P, P])).then_inc(ww_in, 16)
                sp.dma_start(em, t["mask1"]).then_inc(ww_in, 16)
                for g in range(2):
                    sp.dma_start(ctxT[g], t["ctxT"][:, g * W:(g + 1) * W]).then_inc(s[f"ctx_in{g}"], 16)

                def group(g, u, last):
                    if isinstance(g, int) and g + 2 >= NG:
                        return
                    sp.wait_ge(s["proj_ready"], 3 * g + 3)
                    sp.dma_start(ctxT[u], t["ctxT"][:, ds((g + 2) * W, W)]).then_inc(s[f"ctx_in{u}"], 16)
                loop(sp, group)
                barrier(sp, phase)

            def tensor(pe):
                def project(g, u, first=False):
                    pe.wait_ge(s["xn_ready"], g + 1)
                    if not first:
                        pe.wait_ge(s["normed_ready"], 3 * g)
                        pe.wait_ge(s["attT_evac"], g - 1)
                        pe.wait_ge(s["qT_evac"], g - 1)
                    for j in range(G):
                        mm = pe.transpose(T[:, j * P:(j + 1) * P], xn[:, j, :], ident[:])
                    mm.then_inc(s["tr_ready"], 1)
                    pe.wait_ge(s["xnT_ready"], g + 1)
                    pe.wait_ge(s[f"ctx_in{u}"], (g - u) * 8 + 16)
                    for i, (dst, src) in enumerate(((Q, xnT), (K, ctxT[u]), (V, ctxT[u]))):
                        for j in range(G):
                            mm = pe.matmul(dst[:, j * P:(j + 1) * P], src[:, j * P:(j + 1) * P], w[:, i, :],
                                           start=True, stop=True)
                        mm.then_inc(s["proj_ready"], 1)

                def regroup(g, j):
                    pe.wait_ge(s["swap_a"], G * g + j + 1)
                    pe.wait_ge(s["swap_v"], G * g + j + 1)
                    pe.nop(nofuse=True)
                    for k in range(DH):
                        mm = pe.transpose(T[:, j * P + k * H:j * P + (k + 1) * H], swap[0:H, j % 2, k, :],
                                          ident[0:H, 0:H])
                    if j == G - 1:
                        mm.then_inc(s["attT_ready"], 1)

                def attend(g, u, last):
                    pe.wait_ge(s["q_final"], g + 1)
                    if not last:
                        pe.wait_ge(s["xnT_ready"], g + 2)
                    for j in range(G):
                        mm = pe.transpose(T[:, j * P:(j + 1) * P], proj[u][0][:, j, :], ident[:])
                    mm.then_inc(s["qT_ready"], 1)
                    pe.wait_ge(s["kv_final"], g + 1)
                    pe.wait_ge(s["v_scaled"], g + 1)
                    for j in range(G):
                        mm = pe.matmul((KV0, KV1)[j // 2][:, (j % 2) * KW:(j % 2 + 1) * KW], proj[u][1][:, j, :],
                                       v_wide[u][:, j, :], start=True, stop=True)
                    mm.then_inc(s["kv_ready"], 1)
                    pe.wait_ge(s["qT_evac"], g + 1)
                    pe.wait_ge(s["kv_masked"], g + 1)
                    for j in range(G):
                        mm = pe.matmul((A0, A1)[j // 2][:, (j % 2) * KW:(j % 2 + 1) * KW], qT[:, j * P:(j + 1) * P],
                                       kvx[:, j, :], start=True, stop=True)
                    mm.then_inc(s["att_ready"], 1)
                    pe.wait_ge(s["att_normed"], g + 1)
                    for j in range(G):
                        if j >= 2:
                            pe.wait_ge(s["swap_a"], G * g + j - 1)
                            pe.wait_ge(s["swap_v"], G * g + j - 1)
                        for e in range(DH):
                            mm = pe.transpose(swap_bank[j % 2][e // 4][0:H, (e % 4) * P:(e % 4 + 1) * P],
                                              att[:, j, :].rearrange("p (h e) -> p h e", h=H)[:, :, e], ident[:])
                        mm.then_inc(s["swap_ready"], 1)
                        if j >= 1:
                            regroup(g, j - 1)
                    regroup(g, G - 1)
                    pe.wait_ge(s["attT_evac"], g + 1)
                    for j in range(G):
                        mm = pe.matmul(KV1[:, j * P:(j + 1) * P], attT[:, j * P:(j + 1) * P], w[:, 3, :],
                                       start=True, stop=True)
                    mm.then_inc(s["y_ready"], 1)

                pe.wait_ge(ww_in, 16 * 8)
                project(0, 0, first=True)

                def group(g, u, last):
                    if not last:
                        project(g + 1, 1 - u)
                    attend(g, u, last)
                loop(pe, group)
                barrier(pe, phase)

            def scalar(act):
                def project(g, u):
                    act.wait_ge(s["tr_ready"], g + 1)
                    act.activation(xnT, T[:], ACT.Copy).then_inc(s["xnT_ready"], 1)
                    act.wait_ge(s["rs_ready"], g + 1)
                    for i, src in enumerate((Q, K, V)):
                        for j in range(G):
                            c = i * G + j
                            mm = act.activation(proj[u][i][:, j, :], src[:, j * P:(j + 1) * P], ACT.Identity,
                                                bias=nm[:, c:c + 1], scale=rs[:, c:c + 1])
                        mm.then_inc(s["normed_ready"], 1)

                project(0, 0)

                def group(g, u, last):
                    if not last:
                        project(g + 1, 1 - u)
                    act.wait_ge(s["qT_ready"], g + 1)
                    act.activation(qT, T[:], ACT.Copy).then_inc(s["qT_evac"], 1)
                    for j in range(G):
                        act.wait_ge(s["swap_ready"], G * g + j + 1)
                        act.activation(swapped(j, 0), swap_bank[j % 2][0][0:H, :].rearrange("p (e n) -> p e n", e=4),
                                       ACT.Copy).then_inc(s["swap_a"], 1)
                    act.wait_ge(s["attT_ready"], g + 1)
                    act.activation(attT.rearrange("p (j h k) -> p j k h", j=G, h=H),
                                   T[:].rearrange("p (j k h) -> p j k h", j=G, h=H), ACT.Copy
                                   ).then_inc(s["attT_evac"], 1)
                loop(act, group)
                barrier(act, phase)

            def vector(dve):
                def project(g, u):
                    for j in range(G):
                        mm = dve.tensor_scalar(xn[:, j, :], x[:, ds(g * G + j, 1), :], mean[:, ds(g * G + j, 1)],
                                               rstd[:, ds(g * G + j, 1)], ALU.subtract, ALU.mult)
                    mm.then_inc(s["xn_ready"], 1)
                    for i, src in enumerate((Q, K, V)):
                        dve.wait_ge(s["proj_ready"], 3 * g + i + 1)
                        for j in range(G):
                            dve.bn_stats(bn[:, i * G + j, :], src[:, j * P:(j + 1) * P])
                    dve.drain()
                    for c in range(3 * G):
                        dve.bn_aggr(agg[:, c, :], bn[:, c, :])
                    dve.drain()
                    dve.tensor_scalar(ve, agg[:, :, 1], EPS_1, None, ALU.add).then_inc(s["var_ready"], 1)

                def finish(g, u):
                    gamma, beta = bc(gb[:, 0, :]), bc(gb[:, 1, :])
                    for i in range(2):
                        dve.wait_ge(s["normed_ready"], 3 * g + i + 1)
                        dve.tensor_tensor(proj[u][i], proj[u][i], gamma, ALU.mult)
                        dve.drain()
                        dve.tensor_tensor(proj[u][i], proj[u][i], beta, ALU.add)
                        dve.drain()
                        mm = dve.tensor_scalar(proj[u][i], proj[u][i], 0.0, EPS_K, ALU.max, ALU.add)
                        if i == 0:
                            mm.then_inc(s["q_final"], 1)
                    dve.drain()
                    for j in range(G):
                        mm = dve.tensor_scalar(proj[u][1][:, j, :], proj[u][1][:, j, :], em[:, ds(g * G + j, 1)], None, ALU.mult)
                    mm.then_inc(s["kv_final"], 1)

                for u in range(2):
                    dve.memset(v_wide[u], 1.0)
                dve.drain().then_inc(s["x_done"], 1)
                project(0, 0)

                def group(g, u, last):
                    finish(g, u)
                    if not last:
                        project(g + 1, 1 - u)
                    dve.wait_ge(s["kv_ready"], g + 1)
                    for k, src in enumerate((KV0, KV1)):
                        mm = dve.tensor_tensor(kvx[:, 2 * k:2 * k + 2, :],
                                               src[:, 0:2 * KW].rearrange("p (a k) -> p a k", a=2),
                                               block_mask.unsqueeze(1).broadcast_to([P, 2, KW]), ALU.mult)
                    mm.then_inc(s["kv_masked"], 1)
                    dve.wait_ge(s["att_ready"], g + 1)
                    views = [src[:, 0:2 * KW].rearrange("p (a k) -> p a k", a=2) for src in (A0, A1)]
                    for k, v in enumerate(views):
                        dve.tensor_scalar(den[:, 2 * k:2 * k + 2, :], v[:, :, P:KW], EPS_K, None, ALU.add)
                    dve.drain()
                    dve.reciprocal(den, den)
                    dve.drain()
                    for k, v in enumerate(views):
                        for a in range(2):
                            j = 2 * k + a
                            mm = dve.tensor_tensor(att[:, j, :].rearrange("p (h e) -> p h e", h=H),
                                                   v[:, a, 0:P].rearrange("p (h e) -> p h e", h=H),
                                                   den[:, j, :].unsqueeze(2).broadcast_to([P, H, DH]), ALU.mult)
                    mm.then_inc(s["att_normed"], 1)
                    for j in range(G):
                        dve.wait_ge(s["swap_ready"], G * g + j + 1)
                        dve.tensor_copy(swapped(j, 1), swap_bank[j % 2][1][0:H, :].rearrange("p (e n) -> p e n", e=4)
                                        ).then_inc(s["swap_v"], 1)
                    dve.wait_ge(s["y_ready"], g + 1)
                    dve.tensor_tensor(y, KV1[:].rearrange("p (a k) -> p a k", a=G), bc(gb[:, 2, :]), ALU.add)
                    dve.drain()
                    for j in range(G):
                        dve.bn_stats(bny[:, j, :], y[:, j, :])
                    dve.drain()
                    for j in range(G):
                        dve.bn_aggr(aggy[:, j, :], bny[:, j, :])
                    dve.drain()
                    dve.tensor_scalar(vey, aggy[:, :, 1], EPS_1, None, ALU.add).then_inc(s["yvar_ready"], 1)
                    dve.wait_ge(s["yrs_ready"], g + 1)
                    for j in range(G):
                        dve.tensor_scalar(y[:, j, :], y[:, j, :], aggy[:, j, 0:1], rsy[:, j:j + 1],
                                          ALU.subtract, ALU.mult)
                    dve.drain()
                    dve.tensor_tensor(y, y, bc(gb[:, 0, :]), ALU.mult)
                    dve.drain()
                    dve.tensor_tensor(y, y, bc(gb[:, 1, :]), ALU.add)
                    dve.drain()
                    here = x[:, ds(g * G, G), :]
                    dve.tensor_tensor(here, here, y, ALU.add)
                    dve.drain()
                    stats_of(dve, g * G, bnx, aggx).then_inc(s["stats_ready"], 1)
                loop(dve, group)
                barrier(dve, phase)

            def gpsimd(pool):
                pool.memset(half, -0.5)
                for view, n, wide in ((block_mask[:, 0:P], H, DH), (block_mask[:, P:KW], H, 1)):
                    pool.memset(view, 1.0)
                    pool.drain()
                    v3 = view.rearrange("p (h e) -> p h e", e=wide)
                    pool.affine_select(out=v3, in_=v3, compare_op=ALU.is_ge, fill=0.0, base=0,
                                       pattern=[[-DH, n], [0, wide]], channel_multiplier=1)
                    pool.drain()
                    pool.affine_select(out=v3, in_=v3, compare_op=ALU.is_ge, fill=0.0, base=DH - 1,
                                       pattern=[[DH, n], [0, wide]], channel_multiplier=-1)
                pool.wait_ge(s["x_done"], 1)
                pool.wait_ge(ww_in, 16 * 8)

                def scales(g):
                    pool.wait_ge(s["var_ready"], g + 1)
                    pool.tensor_tensor(rs, ve, half, ALU.pow)
                    pool.drain()
                    pool.tensor_tensor(nm, agg[:, :, 0], rs, ALU.mult)
                    pool.drain()
                    pool.tensor_scalar(nm, nm, -1.0, None, ALU.mult).then_inc(s["rs_ready"], 1)

                def group(g, u, last):
                    pool.wait_ge(s["normed_ready"], 3 * g + 3)
                    v = proj[u][2]
                    pool.tensor_tensor(v, v, bc(gb[:, 0, :]), ALU.mult)
                    pool.drain()
                    pool.tensor_tensor(v, v, bc(gb[:, 1, :]), ALU.add)
                    pool.drain()
                    pool.tensor_tensor(v_wide[u][:, :, 0:P], v,
                                       em[:, ds(g * G, G)].unsqueeze(2).broadcast_to([P, G, P]),
                                       ALU.mult).then_inc(s["v_scaled"], 1)
                    if not last:
                        scales(g + 1)
                    pool.wait_ge(s["yvar_ready"], g + 1)
                    pool.tensor_tensor(rsy, vey, neg_half[:], ALU.pow).then_inc(s["yrs_ready"], 1)
                    pool.wait_ge(s["stats_ready"], g + 1)
                    rstd_of(pool, g * G)
                scales(0)
                loop(pool, group)
                clear_twins(pool)
                barrier(pool, phase)

            return sync, tensor, scalar, vector, gpsimd

        def expert_choice(phase):
            s = {n: sem(f"{n}_f1") for n in (
                "xn_ready", "tr_ready", "xnT_ready", "logits_ready", "shifted_ready", "exp_ready", "gates_ready",
                "gT_ready", "sel_ready", "selT_ready", "selT_copied", "pos_ready",
                "xg_ready", "oh_ready", "pg_ready", "ga_ready", "ga_evac", "pt_ready", "pt_evac", "h_ready",
                "h_evac", "w2_ready", "o2_evac", "y_ready", "x_done", "stats_ready")}
            K, F = 64, 512
            FB = F // P
            arena.restart()
            xn = [arena.take([G, P]) for _ in range(2)]
            xnT = [arena.take([W]) for _ in range(2)]
            lg = arena.take([B, E])
            gate_of = arena.take([B, E])
            top, total = arena.take([B]), arena.take([B])
            work = arena.take([2, P])
            best = arena.take([2, E])
            sel, selT = arena.take([2, P]), arena.take([2, P])
            slot = arena.take([B, E])
            iota = arena.take([K])
            upper = arena.take([P])
            onehot = [arena.take([E, K]) for _ in range(2)]
            weighted = [arena.take([E, K]) for _ in range(2)]
            weightedT = [arena.take([G, E // 2, P]) for _ in range(2)]
            exT = [arena.take([E, G * K]) for _ in range(2)]
            h1T = [arena.take([FB, G * K]) for _ in range(2)]
            out2 = arena.take([E // 2, G, P])
            b1c = arena.take([E, FB])
            b2p = arena.take([E // 2, P])
            bn, agg = arena.take([G, 6]), arena.take([G, 2])
            w1 = wide[:, 0:E * F].rearrange("p (e f) -> p e f", e=E)
            w2 = wide[:, E * F:2 * E * F].rearrange("p (e b m) -> p e b m", e=E, b=FB)

            def sync(sp):
                sp.dma_start(b1c, t["b1_1"]).then_inc(fw_in[1], 16)
                for e in range(E):
                    row = t["b2_1"][e].rearrange("(a n) -> a n", a=1)
                    sp.dma_start(b2p[K * (e % 2):K * (e % 2) + K, e // 2, :], row.broadcast_to([K, P])).then_inc(fw_in[1], 16)
                barrier(sp, phase)

            def tensor(pe):
                def turn(g, u):
                    pe.wait_ge(s["xn_ready"], g + 1)
                    for j in range(G):
                        mm = pe.transpose(bank[u][:, j * P:(j + 1) * P], xn[u][:, j, :], ident[:])
                    mm.then_inc(s["tr_ready"], 1)

                def prep(g, u, j, first=False):
                    pe.wait_ge(s["oh_ready"], G * g + j + 1)
                    if j == 0:
                        if not first:
                            pe.wait_ge(s["x_done"], g - 1)
                    if not (first and j == 0):
                        pe.wait_ge(s["ga_evac"], G * g + j)
                    pe.matmul(bank[0][:], xn[u][:, j, :], onehot[j % 2].rearrange("p e k -> p (e k)"),
                              start=True, stop=True).then_inc(s["ga_ready"], 1)
                    pe.wait_ge(s["pg_ready"], G * g + j + 1)
                    if not (first and j == 0):
                        pe.wait_ge(s["pt_evac"], G * g + j)
                    for k in range(E // 2):
                        mm = pe.transpose(bank[1][:, k * P:(k + 1) * P],
                                          weighted[j % 2][:, 2 * k:2 * k + 2, :].rearrange("p e k -> p (e k)"), ident[:])
                    mm.then_inc(s["pt_ready"], 1)

                pe.wait_ge(fw_in[1], 16 * fw_loads[1])
                turn(0, 0)

                def logits(g, u, last):
                    if not last:
                        turn(g + 1, 1 - u)
                    pe.wait_ge(s["xnT_ready"], g + 1)
                    for j in range(G):
                        mm = pe.matmul(bank[2 + u][:, j * E:(j + 1) * E], xnT[u][:, j * P:(j + 1) * P], gates[1][:],
                                       start=True, stop=True)
                    mm.then_inc(s["logits_ready"], 1)
                loop(pe, logits)
                pe.wait_ge(s["gates_ready"], 1)
                for k in range(2):
                    mm = pe.transpose(bank[4][:, k * P:(k + 1) * P],
                                      gate_of[:, 16 * k:16 * k + 16, :].rearrange("p b e -> p (b e)"), ident[:])
                mm.then_inc(s["gT_ready"], 1)
                pe.wait_ge(s["sel_ready"], 1)
                for k in range(2):
                    mm = pe.transpose(bank[5][:, k * P:(k + 1) * P], sel[:, k, :], ident[:])
                mm.then_inc(s["selT_ready"], 1)
                pe.wait_ge(s["selT_copied"], 1)
                pe.matmul(bank[6][:, 0:2 * P], upper, selT.rearrange("p a k -> p (a k)"),
                          start=True, stop=True).then_inc(s["pos_ready"], 1)
                for j in range(G):
                    prep(0, 0, j, first=True)

                def second(g, e):
                    n = (E * g + e) * FB
                    pe.wait_ge(s["h_evac"], n + 2 * FB)
                    pair = (E // 2) * g + e // 2
                    if e % 2 == 0:
                        pe.wait_ge(s["o2_evac"], pair + 1)
                    rows = slice(K * (e % 2), K * (e % 2) + K)
                    for j in range(G):
                        for f in range(FB):
                            mm = pe.matmul(bank[6 + (e // 2) % 2][rows, j * P:(j + 1) * P],
                                           h1T[e % 2][:, f, j * K:(j + 1) * K], w2[:, e, f, :],
                                           start=(f == 0), stop=(f == FB - 1), skip_group_check=True)
                    if e % 2:
                        mm.then_inc(s["w2_ready"], 1)

                def group(g, u, last):
                    pe.wait_ge(s["ga_evac"], G * g + G)
                    for e in range(E):
                        for f in range(FB):
                            pe.wait_ge(s["h_evac"], (E * g + e) * FB + f + 1)
                            pe.matmul(bank[2 + f][:, 0:G * K], w1[:, e, f * P:(f + 1) * P], exT[u][:, e, :],
                                      start=True, stop=True).then_inc(s["h_ready"], 1)
                        if e:
                            second(g, e - 1)
                        if e in (2, 4, 5, 6) and not last:
                            prep(g + 1, 1 - u, (2, 4, 5, 6).index(e))
                    second(g, E - 1)
                    pe.wait_ge(s["o2_evac"], (E // 2) * g + E // 2 + 2)
                    pe.wait_ge(s["ga_evac"], G * g + (G if last else 2 * G))
                    pe.wait_ge(s["pt_evac"], G * g + G)
                    for j in range(G):
                        for k in range(E // 2):
                            mm = pe.matmul(bank[0][:, j * P:(j + 1) * P], weightedT[u][:, j, k, :], out2[:, k, j, :],
                                           start=(k == 0), stop=(k == E // 2 - 1), skip_group_check=True)
                    mm.then_inc(s["y_ready"], 1)
                loop(pe, group)
                barrier(pe, phase)

            def scalar(act):
                def turned(g, u, last):
                    act.wait_ge(s["tr_ready"], g + 1)
                    act.activation(xnT[u], bank[u][:], ACT.Copy).then_inc(s["xnT_ready"], 1)
                loop(act, turned)
                act.wait_ge(s["shifted_ready"], 1)
                act.activation(gate_of.rearrange("p b e -> p (b e)"), lg.rearrange("p b e -> p (b e)"),
                               ACT.Exp).then_inc(s["exp_ready"], 1)

                def prep(g, u, j):
                    act.wait_ge(s["ga_ready"], G * g + j + 1)
                    act.activation(exT[u][:, :, j * K:(j + 1) * K], bank[0][:].rearrange("p (e k) -> p e k", e=E),
                                   ACT.Copy).then_inc(s["ga_evac"], 1)
                    act.wait_ge(s["pt_ready"], G * g + j + 1)
                    act.activation(weightedT[u][:, j, :, :].rearrange("p e k -> p (e k)"), bank[1][:],
                                   ACT.Copy).then_inc(s["pt_evac"], 1)
                for j in range(G):
                    prep(0, 0, j)
                act.drain().then_inc(s["h_evac"], FB)

                def group(g, u, last):
                    for e in range(E):
                        for f in range(FB):
                            n = (E * g + e) * FB + f
                            act.wait_ge(s["h_ready"], n + 1)
                            act.activation(h1T[e % 2][:, f, :], bank[2 + f][:, 0:G * K], ACT.Gelu_apprx_tanh,
                                           bias=b1c[:, e, f:f + 1]).then_inc(s["h_evac"], 1)
                        if e in (2, 4, 5, 6) and not last:
                            prep(g + 1, 1 - u, (2, 4, 5, 6).index(e))
                loop(act, group)
                barrier(act, phase)

            def vector(dve):
                def normed(g, u, done):
                    for j in range(G):
                        mm = dve.tensor_scalar(xn[u][:, j, :], x[:, ds(g * G + j, 1), :], mean[:, ds(g * G + j, 1)],
                                               rstd[:, ds(g * G + j, 1)], ALU.subtract, ALU.mult)
                    mm.then_inc(done, 1)

                normed(0, 0, s["xn_ready"])

                def logits(g, u, last):
                    if not last:
                        normed(g + 1, 1 - u, s["xn_ready"])
                    dve.wait_ge(s["logits_ready"], g + 1)
                    dve.tensor_copy(lg[:, ds(g * G, G), :], bank[2 + u][:, 0:G * E].rearrange("p (b e) -> p b e", b=G))
                    dve.drain()
                loop(dve, logits)

                def bc(col):
                    return col.unsqueeze(2).broadcast_to([P, B, E])
                dve.tensor_reduce(top, lg, AX.X, ALU.max)
                dve.drain()
                dve.tensor_tensor(lg, lg, bc(top), ALU.subtract).then_inc(s["shifted_ready"], 1)
                dve.wait_ge(s["exp_ready"], 1)
                dve.tensor_reduce(total, gate_of, AX.X, ALU.add)
                dve.drain()
                dve.reciprocal(total, total)
                dve.drain()
                dve.tensor_tensor(gate_of, gate_of, bc(total), ALU.mult).then_inc(s["gates_ready"], 1)
                dve.wait_ge(s["gT_ready"], 1)
                dve.tensor_copy(work.rearrange("p a k -> p (a k)"), bank[4][:, 0:2 * P])
                dve.drain()
                for _ in range(K // 8):
                    for k in range(2):
                        dve.max(best[:, k, :], work[:, k, :])
                    dve.drain()
                    for k in range(2):
                        dve.match_replace(work[:, k, :], best[:, k, :], work[:, k, :], -1.0)
                    dve.drain()
                dve.tensor_scalar(sel, work, 0.0, None, ALU.is_lt).then_inc(s["sel_ready"], 1)
                dve.wait_ge(s["selT_ready"], 1)
                dve.tensor_copy(selT.rearrange("p a k -> p (a k)"), bank[5][:, 0:2 * P]).then_inc(s["selT_copied"], 1)
                dve.wait_ge(s["pos_ready"], 1)
                flat = slot.rearrange("p b e -> p (b e)")
                dve.tensor_tensor(flat, bank[6][:, 0:2 * P], selT.rearrange("p a k -> p (a k)"), ALU.mult)
                dve.drain()
                dve.tensor_scalar(flat, flat, -1.0, None, ALU.add)
                dve.drain()
                dve.drain().then_inc(s["o2_evac"], 2)

                def one_hot(g, u, j, first=False):
                    if not (first and j < 2):
                        dve.wait_ge(s["ga_ready"], G * g + j - 1)
                        dve.wait_ge(s["pg_ready"], G * g + j - 1)
                    dve.tensor_tensor(onehot[j % 2], iota.unsqueeze(1).broadcast_to([P, E, K]),
                                      slot[:, ds(g * G + j, 1), :].rearrange("p a e -> p (a e)").unsqueeze(2)
                                      .broadcast_to([P, E, K]), ALU.is_equal).then_inc(s["oh_ready"], 1)

                normed(0, 0, s["xg_ready"])
                dve.drain()
                for j in range(G):
                    one_hot(0, 0, j, first=True)

                def group(g, u, last):
                    if not last:
                        normed(g + 1, 1 - u, s["xg_ready"])
                        dve.drain()
                        one_hot(g + 1, 1 - u, 0)
                        one_hot(g + 1, 1 - u, 1)
                    for k in range(E // 2):
                        dve.wait_ge(s["w2_ready"], (E // 2) * g + k + 1)
                        if k == 0 and not (isinstance(g, int) and g == 0):
                            dve.wait_ge(s["y_ready"], g)
                        dve.tensor_tensor(out2[:, k, :, :], bank[6 + k % 2][:].rearrange("p (a m) -> p a m", a=G),
                                          b2p[:, k, :].unsqueeze(1).broadcast_to([P, G, P]),
                                          ALU.add).then_inc(s["o2_evac"], 1)
                        if k == 1 and not last:
                            one_hot(g + 1, 1 - u, 2)
                        if k == 2 and not last:
                            one_hot(g + 1, 1 - u, 3)
                    dve.wait_ge(s["y_ready"], g + 1)
                    here = x[:, ds(g * G, G), :]
                    dve.tensor_tensor(here, here, bank[0][:].rearrange("p (a m) -> p a m", a=G), ALU.add
                                      ).then_inc(s["x_done"], 1)
                    dve.drain()
                    stats_of(dve, g * G, bn, agg).then_inc(s["stats_ready"], 1)
                loop(dve, group)
                barrier(dve, phase)

            def gpsimd(pool):
                pool.iota(iota_i, pattern=[[1, K]], base=0, channel_multiplier=0)
                pool.memset(upper, 1.0)
                pool.drain()
                pool.tensor_copy(iota, iota_i)
                pool.affine_select(out=upper, in_=upper, compare_op=ALU.is_ge, fill=0.0, base=0,
                                   pattern=[[1, P]], channel_multiplier=-1)
                pool.drain().then_inc(fw_in[1], 16)

                def weigh(g, j, first=False):
                    pool.wait_ge(s["oh_ready"], G * g + j + 1)
                    if not (first and j < 2):
                        pool.wait_ge(s["pt_ready"], G * g + j - 1)
                    pool.tensor_tensor(weighted[j % 2], onehot[j % 2],
                                       gate_of[:, ds(g * G + j, 1), :].rearrange("p a e -> p (a e)").unsqueeze(2)
                                       .broadcast_to([P, E, K]), ALU.mult).then_inc(s["pg_ready"], 1)
                for j in range(G):
                    weigh(0, j, first=True)

                def group(g, u, last):
                    if not last:
                        for j in range(G):
                            weigh(g + 1, j)
                    pool.wait_ge(s["stats_ready"], g + 1)
                    rstd_of(pool, g * G)
                loop(pool, group)
                barrier(pool, phase)

            return sync, tensor, scalar, vector, gpsimd

        def gated_experts(phase):
            s = {n: sem(f"{n}_f2") for n in (
                "xn_ready", "tr_ready", "xnT_ready", "sq_ready", "c_squared", "c2_ready", "c2_copied",
                "logits_ready", "d2_ready", "dist_ready", "shifted_ready", "exp_ready", "weights_ready",
                "wT_ready", "wT_copied", "b2_ready", "acc_ready", "gu_ready", "sg_ready",
                "hid_free", "y_ready", "y_free", "stats_ready")}
            F = 342
            FB, FR = 3, F // 3
            arena.restart()
            xn = [arena.take([G, P]) for _ in range(2)]
            xnT = [arena.take([W]) for _ in range(2)]
            sq, sq_sum = arena.take([P]), arena.take([2, G])
            cT2, c2 = arena.take([E]), arena.take([E])
            ones = arena.take([P])
            dist = arena.take([G, E])
            z, ez = arena.take([G, E]), arena.take([G, E])
            cmp, cmp2 = arena.take([G, E, E]), arena.take([G, E, E])
            sel, top, total = arena.take([G, E]), arena.take([G]), arena.take([G])
            half = arena.take([G, E])
            weight = [arena.take([G, E]) for _ in range(2)]
            wT = arena.take([W])
            b2 = arena.take([P])
            bgc, b1c = arena.take([E, FB]), arena.take([E, FB])
            sg = arena.take([2, W])
            hid = [arena.take([FB, W]) for _ in range(2)]
            acc = [arena.take([G, P]) for _ in range(2)]
            bn, agg = arena.take([G, 6]), arena.take([G, 2])
            wg = wide[:, 0:E * F].rearrange("p (e f) -> p e f", e=E)
            w1 = wide[:, E * F:2 * E * F].rearrange("p (e f) -> p e f", e=E)
            w2 = wide[:, 2 * E * F:2 * E * F + E * FB * P].rearrange("p (e b m) -> p e b m", e=E, b=FB)
            KB = E * FB

            def sync(sp):
                sp.dma_start(bgc[0:FR], t["bg_2"]).then_inc(fw_in[2], 16)
                sp.dma_start(b1c[0:FR], t["b1_2"]).then_inc(fw_in[2], 16)
                sp.dma_start(b2[0:E], t["b2_2"]).then_inc(fw_in[2], 16)
                barrier(sp, phase)

            def tensor(pe):
                def front_a(g, u, first=False):
                    pe.wait_ge(s["xn_ready"], g + 1)
                    if not first:
                        pe.wait_ge(s["wT_copied"], g)
                        pe.wait_ge(s["acc_ready"], g)
                    for j in range(G):
                        mm = pe.transpose(bank[0][:, j * P:(j + 1) * P], xn[u][:, j, :], ident[:])
                    mm.then_inc(s["tr_ready"], 1)
                    pe.wait_ge(s["xnT_ready"], g + 1)
                    for j in range(G):
                        mm = pe.matmul(bank[1][:, j * E:(j + 1) * E], xnT[u][:, j * P:(j + 1) * P], gates[2][:],
                                       start=True, stop=True)
                    mm.then_inc(s["logits_ready"], 1)

                def front_b(g, u):
                    pe.wait_ge(s["weights_ready"], g + 1)
                    for j in range(G):
                        mm = pe.transpose(bank[0][0:E, j * P:(j + 1) * P], weight[u][:, j, :], ident[:])
                    mm.then_inc(s["wT_ready"], 1)
                    pe.wait_ge(s["wT_copied"], g + 1)
                    for j in range(G):
                        mm = pe.matmul(bank[1][:, j * P:(j + 1) * P], wT[0:E, j * P:(j + 1) * P], b2[0:E, :],
                                       start=True, stop=True)
                    mm.then_inc(s["b2_ready"], 1)

                pe.wait_ge(fw_in[2], 16 * fw_loads[2])
                pe.wait_ge(s["c_squared"], 1)
                pe.matmul(bank[1][:, 0:E], ones, cT2, start=True, stop=True).then_inc(s["c2_ready"], 1)
                pe.wait_ge(s["c2_copied"], 1)
                front_a(0, 0, first=True)
                front_b(0, 0)

                def second(g, e):
                    pe.wait_ge(s["hid_free"], KB * g + FB * e + FB + 2)
                    pe.wait_ge(s["y_free"], E * g + e + 1)
                    for j in range(G):
                        for f in range(FB):
                            mm = pe.matmul(bank[6 + e % 2][:, j * P:(j + 1) * P],
                                           hid[e % 2][0:FR, f, j * P:(j + 1) * P], w2[0:FR, e, f, :],
                                           start=(f == 0), stop=(f == FB - 1), skip_group_check=True)
                    mm.then_inc(s["y_ready"], 1)

                def group(g, u, last):
                    for e in range(E):
                        for f in range(FB):
                            k = FB * e + f
                            pe.wait_ge(s["hid_free"], KB * g + k + 1)
                            cols = slice(f * FR, (f + 1) * FR)
                            pe.matmul(bank[2 + k % 2][0:FR, :], wg[:, e, cols], xnT[u], start=True, stop=True)
                            pe.matmul(bank[4 + k % 2][0:FR, :], w1[:, e, cols], xnT[u], start=True, stop=True
                                      ).then_inc(s["gu_ready"], 1)
                        if e:
                            second(g, e - 1)
                        if e == 2 and not last:
                            front_a(g + 1, 1 - u)
                        if e == 6 and not last:
                            front_b(g + 1, 1 - u)
                    second(g, E - 1)
                loop(pe, group)
                barrier(pe, phase)

            def scalar(act):
                def front_a(g, u):
                    for j in range(G):
                        if j == 0:
                            act.wait_ge(s["xn_ready"], g + 1)
                        act.activation(sq, xn[u][:, j, :], ACT.Square, accum_out=sq_sum[:, u, j:j + 1])
                        act.drain()
                    act.drain().then_inc(s["sq_ready"], 1)
                    act.wait_ge(s["tr_ready"], g + 1)
                    act.activation(xnT[u], bank[0][:], ACT.Copy).then_inc(s["xnT_ready"], 1)

                def front_e(g, u):
                    act.wait_ge(s["shifted_ready"], g + 1)
                    act.activation(ez, z, ACT.Exp).then_inc(s["exp_ready"], 1)

                def front_b(g, u):
                    act.wait_ge(s["wT_ready"], g + 1)
                    act.activation(wT[0:E, :], bank[0][0:E, :], ACT.Copy).then_inc(s["wT_copied"], 1)

                act.wait_ge(fw_in[2], 16 * fw_loads[2])
                act.activation(cT2, gates[2][:], ACT.Square).then_inc(s["c_squared"], 1)
                act.wait_ge(s["c2_ready"], 1)
                act.activation(c2, bank[1][:, 0:E], ACT.Copy).then_inc(s["c2_copied"], 1)
                front_a(0, 0)
                front_e(0, 0)
                front_b(0, 0)

                def group(g, u, last):
                    for e in range(E):
                        for f in range(FB):
                            k = FB * e + f
                            act.wait_ge(s["gu_ready"], KB * g + k + 1)
                            act.activation(sg[0:FR, k % 2, :], bank[2 + k % 2][0:FR, :], ACT.Silu,
                                           bias=bgc[0:FR, e, f:f + 1]).then_inc(s["sg_ready"], 1)
                        if not last:
                            if e == 2:
                                front_a(g + 1, 1 - u)
                            if e == 4:
                                front_e(g + 1, 1 - u)
                            if e == 6:
                                front_b(g + 1, 1 - u)
                loop(act, group)
                barrier(act, phase)

            def vector(dve):
                def normed(g, u):
                    for j in range(G):
                        mm = dve.tensor_scalar(xn[u][:, j, :], x[:, ds(g * G + j, 1), :], mean[:, ds(g * G + j, 1)],
                                               rstd[:, ds(g * G + j, 1)], ALU.subtract, ALU.mult)
                    mm.then_inc(s["xn_ready"], 1)

                def wide_bc(col):
                    return col.unsqueeze(2).broadcast_to([P, G, E])

                def distances(g, u):
                    dve.wait_ge(s["logits_ready"], g + 1)
                    dve.wait_ge(s["sq_ready"], g + 1)
                    dve.scalar_tensor_tensor(out=dist, in0=bank[1][:, 0:G * E].rearrange("p (g e) -> p g e", g=G),
                                             scalar=-2.0, in1=c2.unsqueeze(1).broadcast_to([P, G, E]),
                                             op0=ALU.mult, op1=ALU.add)
                    dve.drain()
                    dve.tensor_tensor(dist, dist, wide_bc(sq_sum[:, u, :]), ALU.add)
                    dve.drain()
                    dve.tensor_scalar(dist, dist, 1e-12, None, ALU.max).then_inc(s["d2_ready"], 1)

                def weights_a(g):
                    dve.wait_ge(s["dist_ready"], g + 1)
                    dve.tensor_reduce(top, dist, AX.X, ALU.max)
                    dve.drain()
                    dve.tensor_tensor(z, dist, wide_bc(top), ALU.subtract).then_inc(s["shifted_ready"], 1)
                    rank_below(dve, dist, cmp, cmp2, sel, 2)

                def weights_b(g, u):
                    dve.wait_ge(s["exp_ready"], g + 1)
                    dve.tensor_tensor(ez, ez, sel, ALU.mult)
                    dve.drain()
                    dve.tensor_reduce(total, ez, AX.X, ALU.add)
                    dve.drain()
                    dve.reciprocal(total, total)
                    dve.drain()
                    dve.tensor_tensor(weight[u], ez, wide_bc(total), ALU.mult).then_inc(s["weights_ready"], 1)

                def start_acc(g, u):
                    dve.wait_ge(s["b2_ready"], g + 1)
                    dve.tensor_tensor(acc[u], bank[1][:].rearrange("p (a m) -> p a m", a=G), x[:, ds(g * G, G), :],
                                      ALU.add).then_inc(s["acc_ready"], 1)

                dve.drain().then_inc(s["hid_free"], 2)
                dve.drain().then_inc(s["y_free"], 2)
                normed(0, 0)
                distances(0, 0)
                weights_a(0)
                weights_b(0, 0)
                start_acc(0, 0)

                def add_expert(g, u, e):
                    dve.drain()
                    dve.wait_ge(s["y_ready"], E * g + e + 1)
                    for j in range(G):
                        here = acc[u][:, j, :]
                        if e == E - 1:
                            dst = x[:, ds(g * G + j, 1), :].rearrange("p a m -> p (a m)")
                        else:
                            dst = here
                        mm = dve.scalar_tensor_tensor(out=dst, in0=bank[6 + e % 2][:, j * P:(j + 1) * P],
                                                      scalar=weight[u][:, j, e:e + 1], in1=here,
                                                      op0=ALU.mult, op1=ALU.add)
                    mm.then_inc(s["y_free"], 1)

                def group(g, u, last):
                    if not last:
                        normed(g + 1, 1 - u)
                    for e in range(E):
                        for f in range(FB):
                            k = FB * e + f
                            dve.wait_ge(s["sg_ready"], KB * g + k + 1)
                            dve.scalar_tensor_tensor(out=hid[e % 2][0:FR, f, :], in0=bank[4 + k % 2][0:FR, :],
                                                     scalar=b1c[0:FR, e, f:f + 1], in1=sg[0:FR, k % 2, :],
                                                     op0=ALU.add, op1=ALU.mult).then_inc(s["hid_free"], 1)
                        if e:
                            add_expert(g, u, e - 1)
                        if not last:
                            if e == 3:
                                distances(g + 1, 1 - u)
                            if e == 4:
                                weights_a(g + 1)
                            if e == 5:
                                weights_b(g + 1, 1 - u)
                            if e == 7:
                                start_acc(g + 1, 1 - u)
                    add_expert(g, u, E - 1)
                    dve.drain()
                    stats_of(dve, g * G, bn, agg).then_inc(s["stats_ready"], 1)
                loop(dve, group)
                barrier(dve, phase)

            def gpsimd(pool):
                pool.memset(ones, 1.0)
                pool.memset(half, 0.5)
                pool.drain().then_inc(fw_in[2], 16)

                def root(g):
                    pool.wait_ge(s["d2_ready"], g + 1)
                    pool.tensor_tensor(dist, dist, half, ALU.pow).then_inc(s["dist_ready"], 1)

                root(0)

                def group(g, u, last):
                    if not last:
                        root(g + 1)
                    pool.wait_ge(s["stats_ready"], g + 1)
                    rstd_of(pool, g * G)
                loop(pool, group)
                barrier(pool, phase)

            return sync, tensor, scalar, vector, gpsimd

        def load_wide2(sp):
            F, FR = 342, 114
            sp.dma_start(wide[:, 0:2 * E * F], t["wgu_2"]).then_inc(fw_in[2], 16)
            sp.dma_start(wide[0:FR, 2 * E * F:2 * E * F + 3 * E * P], t["w2_2"]).then_inc(fw_in[2], 16)

        def wide_heads(phase):
            s = {n: sem(f"{n}_3") for n in (
                "ctx_in0", "ctx_in1", "xn_ready", "m_ready0", "m_ready1", "m_free0", "m_free1",
                "s_ready", "s_free", "mhl_ready", "mts_ready", "st_ready", "st_free", "pv_ready",
                "o_copied", "inv_ready", "attn_ready", "xb_ready", "stats_ready", "xnT_ready",
                "front_a", "front_v")}
            G3 = 2
            NG3, W3 = B // G3, G3 * P
            HB = H // 2
            SCALE = 0.125
            arena.restart()
            q_pad = [arena.take([HB, 2, W3]) for _ in range(2)]
            kT = [arena.take([HB, W3]) for _ in range(2)]
            values = [arena.take([G3, H * 64]) for _ in range(2)]
            probs = [arena.take([H, P]) for _ in range(2)]
            ctxT = [arena.take([W3]) for _ in range(2)]
            xn = [arena.take([G3, P]) for _ in range(2)]
            xb = [arena.take([G3, P]) for _ in range(2)]
            xnT = arena.take([W3])
            o_raw = arena.take([HB, P])
            attnT = arena.take([2, HB, P])
            mx, mhl = arena.take([2, H]), arena.take([2, 2 * H], BF16)
            mts = arena.take([2, P], BF16)
            inv = arena.take([2, P])
            bn, agg = arena.take([G3, 6]), arena.take([G3, 2])
            bcol = arena.take([3, HB])
            spread = arena.take([HB, P])
            bv = arena.take([H * 64])
            bo = arena.take([P])
            wq, wk, wv, wo = (wide[:, i * 1024:(i + 1) * 1024] for i in range(4))
            S, T, O, M = bank[0:2], bank[2:4], bank[4:6], bank[6:8]
            maskS, maskT = mask_bias[3]
            FRONT, USES = 14, 24
            LOADS = 4 + 2 + 2

            def count(g, k):
                return k % 2, g * (USES // 2) + (FRONT + k) // 2 + 1

            def front_count(g, k):
                if isinstance(g, int) and g == 0:
                    return k % 2, k // 2 + 1
                return count(g - 1, 4 + k)

            def own_count(g, k, last):
                return count(g, k + (FRONT if k >= 4 and not last else 0))

            def m_take(pe, where):
                b, n = where
                pe.wait_ge(s[f"m_free{b}"], n)
                return M[b]

            def m_done(mm, where):
                mm.then_inc(s[f"m_ready{where[0]}"], 1)

            def m_read(eng, where):
                b, n = where
                eng.wait_ge(s[f"m_ready{b}"], n)
                return M[b]

            def m_release(mm, where):
                mm.then_inc(s[f"m_free{where[0]}"], 1)

            def sync(sp):
                for i, name in enumerate("qkvo"):
                    sp.dma_start(wide[:, i * 1024:(i + 1) * 1024], t[f"w{name}3"]).then_inc(w_in[3], 16)
                sp.dma_start(bcol[:, 0:2, :], t["bqk3"]).then_inc(w_in[3], 16)
                sp.dma_start(bv, t["bv3"].rearrange("(a n) -> a n", a=1).broadcast_to([P, H * 64])).then_inc(w_in[3], 16)
                sp.dma_start(bo, t["bo3"].rearrange("(a n) -> a n", a=1).broadcast_to([P, P])).then_inc(w_in[3], 16)
                for g in range(2):
                    sp.dma_start(ctxT[g], t["ctxT"][:, g * W3:(g + 1) * W3]).then_inc(s[f"ctx_in{g}"], 16)

                def group(g, u, last):
                    if isinstance(g, int) and g + 2 >= NG3:
                        return
                    sp.wait_ge(s["front_v"], g + 1)
                    sp.dma_start(ctxT[u], t["ctxT"][:, ds((g + 2) * W3, W3)]).then_inc(s[f"ctx_in{u}"], 16)
                loop(sp, group, NG3)
                barrier(sp, phase)

            def tensor(pe):
                def front(g, u):
                    pe.wait_ge(s["xn_ready"], g + 1)
                    for j in range(G3):
                        c = front_count(g, j)
                        dst = m_take(pe, c)
                        m_done(pe.transpose(dst[:, 0:P], xn[u][:, j, :], ident[:]), c)
                    pe.wait_ge(s["xnT_ready"], G3 * g + G3)
                    for k in range(4):
                        c = front_count(g, 2 + k)
                        dst = m_take(pe, c)
                        for a in range(2):
                            mm = pe.matmul(dst[:, a * W3:(a + 1) * W3], wq[:, (2 * k + a) * P:(2 * k + a + 1) * P],
                                           xnT, start=True, stop=True)
                        m_done(mm, c)
                    pe.wait_ge(s[f"ctx_in{u}"], (g - u) * 8 + 16)
                    for k in range(4):
                        c = front_count(g, 6 + k)
                        dst = m_take(pe, c)
                        for a in range(2):
                            mm = pe.matmul(dst[:, a * W3:(a + 1) * W3], wk[:, (2 * k + a) * P:(2 * k + a + 1) * P],
                                           ctxT[u], start=True, stop=True)
                        m_done(mm, c)
                    for j in range(G3):
                        for a in range(2):
                            c = front_count(g, 10 + 2 * j + a)
                            dst = m_take(pe, c)
                            mm = pe.matmul(dst[:], ctxT[u][:, j * P:(j + 1) * P], wv[:, a * 512:(a + 1) * 512],
                                           start=True, stop=True)
                            m_done(mm, c)

                def scores(n, u, j):
                    for c in range(4):
                        pe.wait_ge(s["s_free"], 4 * n + c + 1)
                        pe.matmul(S[c % 2][:], identb[:], maskS[:].rearrange("p a k -> p (a k)"),
                                  start=True, stop=False, skip_group_check=True)
                        for h in range(4 * c, 4 * c + 4):
                            mm = pe.matmul(S[c % 2][:, (h % 4) * P:(h % 4 + 1) * P],
                                           q_pad[u][:, h // 2, h % 2, j * P:(j + 1) * P],
                                           kT[u][:, h // 2, j * P:(j + 1) * P],
                                           start=False, stop=(h % 4 == 3), skip_group_check=True)
                        mm.then_inc(s["s_ready"], 1)

                def scoresT(n, u, j, b):
                    for c in range(4):
                        pe.wait_ge(s["st_free"], 4 * n + c + 1)
                        pe.matmul(T[c % 2][:], identb[:], maskT[:].rearrange("p a k -> p (a k)"),
                                  start=True, stop=False, skip_group_check=True)
                        for k in range(2 * c, 2 * c + 2):
                            pe.matmul(T[c % 2][:, (k % 2) * 2 * P:(k % 2 + 1) * 2 * P],
                                      kT[u][:, k, j * P:(j + 1) * P], q_pad[u][:, k, :, j * P:(j + 1) * P],
                                      start=False, stop=False, skip_group_check=True)
                        if c == 0:
                            pe.wait_ge(s["mts_ready"], n + 1)
                        for h in range(4 * c, 4 * c + 4):
                            mm = pe.matmul(T[c % 2][:, (h % 4) * P:(h % 4 + 1) * P],
                                           shift_rows[:, h, :], mts[:, b, :],
                                           start=False, stop=(h % 4 == 3), skip_group_check=True)
                        mm.then_inc(s["st_ready"], 1)

                def attend(n, g, u, j, b, last):
                    first = 4 if j else 0
                    for c in range(4):
                        pe.wait_ge(s["st_free"], 4 * n + c + 3)
                        if c % 2 == 0:
                            pe.wait_ge(s["o_copied"], 2 * n + c // 2 + 1)
                        for h in range(4 * c, 4 * c + 4):
                            mm = pe.matmul(O[c // 2][64 * (h % 2):64 * (h % 2) + 64, ((h // 2) % 4) * P:((h // 2) % 4 + 1) * P],
                                           values[u][:, j, h * 64:(h + 1) * 64], probs[b][:, h, :],
                                           start=True, stop=True, skip_group_check=True)
                        if c % 2:
                            mm.then_inc(s["pv_ready"], 1)
                    w = own_count(g, first + 1, last)
                    dst = m_take(pe, w)
                    for c in range(4):
                        for h in range(4 * c, 4 * c + 4):
                            mm = pe.matmul(dst[32 * c:32 * c + 32, 0:P], ones_cols[:, h % 4, :], probs[b][:, h, :],
                                           start=(h % 4 == 0), stop=(h % 4 == 3), skip_group_check=True)
                    m_done(mm, w)

                def spread_inv(n, g, j, b, last):
                    first = 4 if j else 0
                    pe.wait_ge(s["inv_ready"], n + 1)
                    for k in range(2):
                        w = own_count(g, first + 2 + k, last)
                        dst = m_take(pe, w)
                        for a in range(4):
                            mm = pe.matmul(dst[:, a * P:(a + 1) * P], spread[:, 4 * k + a, :], inv[:, b, :],
                                           start=True, stop=True)
                        m_done(mm, w)

                pe.wait_ge(w_in[3], 16 * LOADS)
                front(0, 0)
                pe.wait_ge(s["front_v"], 1)
                pe.wait_ge(s["front_a"], 1)
                scores(0, 0, 0)

                def group(g, u, last):
                    for j in range(G3):
                        n, b = g * G3 + j, j % 2
                        first = 4 if j else 0
                        pe.wait_ge(s["mhl_ready"], n + 1)
                        w = own_count(g, first, last)
                        dst = m_take(pe, w)
                        m_done(pe.transpose(dst[0:2 * H, 0:64].bitcast(BF16), mhl[:, b, :], identb[:]), w)
                        scoresT(n, u, j, b)
                        if j < G3 - 1:
                            scores(n + 1, u, j + 1)
                        elif not last:
                            pe.wait_ge(s["front_a"], g + 2)
                            pe.wait_ge(s["front_v"], g + 2)
                            scores(n + 1, 1 - u, 0)
                        attend(n, g, u, j, b, last)
                        spread_inv(n, g, j, b, last)
                        if j == 0 and not last:
                            front(g + 1, 1 - u)
                    for j in range(G3):
                        w = own_count(g, 8 + j, last)
                        pe.wait_ge(s["attn_ready"], 2 * (g * G3 + j) + 2)
                        dst = m_take(pe, w)
                        for k in range(HB):
                            mm = pe.matmul(dst[:, 0:P], attnT[:, j, k, :], wo[:, k * P:(k + 1) * P],
                                           start=(k == 0), stop=(k == HB - 1))
                        m_done(mm, w)
                loop(pe, group, NG3)
                barrier(pe, phase)

            def scalar(act):
                def front(g, u):
                    for j in range(G3):
                        w = front_count(g, j)
                        src = m_read(act, w)
                        mm = act.activation(xnT[:, j * P:(j + 1) * P], src[:, 0:P], ACT.Copy)
                        mm.then_inc(s[f"m_free{w[0]}"], 1)
                        act.drain().then_inc(s["xnT_ready"], 1)
                    for k in range(4):
                        w = front_count(g, 2 + k)
                        src = m_read(act, w)
                        for a in range(2):
                            for r in range(2):
                                rows = slice(64 * r, 64 * r + 64)
                                mm = act.activation(q_pad[u][rows, 2 * k + a, r, :], src[rows, a * W3:(a + 1) * W3],
                                                    ACT.Identity, bias=bcol[rows, 2, 2 * k + a:2 * k + a + 1], scale=SCALE)
                        m_release(mm, w)
                    act.drain().then_inc(s["front_a"], 1)

                act.wait_ge(s["stats_ready"], 1)
                for b in range(2):
                    act.activation(mts[:, b, :], identb[:], ACT.Copy, scale=0.0)
                act.drain()
                front(0, 0)

                def group(g, u, last):
                    for j in range(G3):
                        n, b = g * G3 + j, j % 2
                        first = 4 if j else 0
                        w = own_count(g, first, last)
                        src = m_read(act, w)
                        mm = act.activation(mts[0:2 * H, b, :], src[0:2 * H, 0:64].bitcast(BF16), ACT.Copy)
                        m_release(mm, w)
                        act.drain().then_inc(s["mts_ready"], 1)
                        for c in range(4):
                            act.wait_ge(s["st_ready"], 4 * n + c + 1)
                            act.activation(probs[b][:, 4 * c:4 * c + 4, :].rearrange("p a q -> p (a q)"),
                                           T[c % 2][:], ACT.Exp).then_inc(s["st_free"], 1)
                        for k in range(2):
                            act.wait_ge(s["pv_ready"], 2 * n + k + 1)
                            if not (isinstance(g, int) and g == 0 and j == 0):
                                act.wait_ge(s["attn_ready"], 2 * n)
                            act.activation(o_raw[:, 4 * k:4 * k + 4, :].rearrange("p a q -> p (a q)"), O[k][:],
                                           ACT.Copy).then_inc(s["o_copied"], 1)
                        if j == 0 and not last:
                            front(g + 1, 1 - u)
                loop(act, group, NG3)
                barrier(act, phase)

            def vector(dve):
                def normed(g, u):
                    for j in range(G3):
                        mm = dve.tensor_scalar(xn[u][:, j, :], x[:, ds(g * G3 + j, 1), :], mean[:, ds(g * G3 + j, 1)],
                                               rstd[:, ds(g * G3 + j, 1)], ALU.subtract, ALU.mult)
                    mm.then_inc(s["xn_ready"], 1)

                def front(g, u):
                    for k in range(4):
                        w = front_count(g, 6 + k)
                        src = m_read(dve, w)
                        for a in range(2):
                            mm = dve.tensor_scalar(kT[u][:, 2 * k + a, :], src[:, a * W3:(a + 1) * W3],
                                                   bcol[:, 1, 2 * k + a:2 * k + a + 1], None, ALU.add)
                        m_release(mm, w)
                    for j in range(G3):
                        for a in range(2):
                            w = front_count(g, 10 + 2 * j + a)
                            src = m_read(dve, w)
                            mm = dve.tensor_tensor(values[u][:, j, a * 512:(a + 1) * 512], src[:],
                                                   bv[:, a * 512:(a + 1) * 512], ALU.add)
                            m_release(mm, w)
                    dve.drain().then_inc(s["front_v"], 1)

                def maxima(n, b):
                    for c in range(4):
                        dve.wait_ge(s["s_ready"], 4 * n + c + 1)
                        dve.tensor_reduce(mx[:, b, 4 * c:4 * c + 4], S[c % 2][:].rearrange("p (a k) -> p a k", a=4),
                                          AX.X, ALU.max).then_inc(s["s_free"], 1)
                    dve.drain()
                    dve.tensor_scalar(mhl[:, b, 0:H], mx[:, b, :], -1.0, None, ALU.mult)
                    dve.drain()
                    dve.scalar_tensor_tensor(out=mhl[:, b, H:2 * H], in0=mx[:, b, :], scalar=-1.0,
                                             in1=mhl[:, b, 0:H], op0=ALU.mult, op1=ALU.subtract
                                             ).then_inc(s["mhl_ready"], 1)

                for u in range(2):
                    dve.memset(q_pad[u].rearrange("p a r t -> p (a r t)"), 0.0)
                dve.wait_ge(w_in[3], 16 * LOADS)
                dve.tensor_scalar(bcol[:, 2, :], bcol[:, 0, :], SCALE, None, ALU.mult)
                dve.drain().then_inc(s["stats_ready"], 1)
                for n in ("m_free0", "m_free1"):
                    dve.drain().then_inc(s[n], 1)
                for n in ("s_free", "st_free", "o_copied"):
                    dve.drain().then_inc(s[n], 2)
                normed(0, 0)
                front(0, 0)
                maxima(0, 0)

                def group(g, u, last):
                    for j in range(G3):
                        n, b = g * G3 + j, j % 2
                        first = 4 if j else 0
                        if j == 0 and not last:
                            normed(g + 1, 1 - u)
                        if j < G3 - 1 or not last:
                            maxima(n + 1, 1 - b)
                        w = own_count(g, first + 1, last)
                        src = m_read(dve, w)
                        mm = dve.reciprocal(inv[:, b, :], src[:, 0:P])
                        m_release(mm, w)
                        dve.drain().then_inc(s["inv_ready"], 1)
                        for k in range(2):
                            w = own_count(g, first + 2 + k, last)
                            src = m_read(dve, w)
                            dve.wait_ge(s["o_copied"], 2 * n + k + 3)
                            mm = dve.tensor_tensor(attnT[:, j, 4 * k:4 * k + 4, :].rearrange("p a q -> p (a q)"),
                                                   o_raw[:, 4 * k:4 * k + 4, :].rearrange("p a q -> p (a q)"),
                                                   src[:], ALU.mult)
                            m_release(mm, w)
                            dve.drain().then_inc(s["attn_ready"], 1)
                        if j == 0 and not last:
                            front(g + 1, 1 - u)
                    for j in range(G3):
                        w = own_count(g, 8 + j, last)
                        src = m_read(dve, w)
                        if j == 0:
                            dve.wait_ge(s["xb_ready"], g + 1)
                        mm = dve.tensor_tensor(x[:, ds(g * G3 + j, 1), :].rearrange("p a m -> p (a m)"), src[:, 0:P],
                                               xb[u][:, j, :], ALU.add)
                        m_release(mm, w)
                    dve.drain()
                    for j in range(G3):
                        dve.bn_stats(bn[:, j, :], x[:, ds(g * G3 + j, 1), :])
                    dve.drain()
                    for j in range(G3):
                        dve.bn_aggr(agg[:, j, :], bn[:, j, :])
                    dve.drain()
                    dve.tensor_copy(mean[:, ds(g * G3, G3)], agg[:, :, 0])
                    dve.tensor_scalar(var_eps[:, ds(g * G3, G3)], agg[:, :, 1], LN_EPS, None,
                                      ALU.add).then_inc(s["stats_ready"], 1)
                loop(dve, group, NG3)
                barrier(dve, phase)

            def gpsimd(pool):
                pool.memset(spread, 0.0)
                pool.drain()
                v = spread.rearrange("p k (r d) -> p k r d", r=2)
                pool.affine_select(out=v, in_=v, compare_op=ALU.not_equal, fill=1.0, base=0,
                                   pattern=[[-16, HB], [-8, 2], [0, 64]], channel_multiplier=1)
                pool.drain().then_inc(w_in[3], 16)

                def group(g, u, last):
                    pool.tensor_tensor(xb[u], x[:, ds(g * G3, G3), :], bo.unsqueeze(1).broadcast_to([P, G3, P]),
                                       ALU.add).then_inc(s["xb_ready"], 1)
                    pool.wait_ge(s["stats_ready"], g + 2)
                    pool.tensor_tensor(rstd[:, ds(g * G3, G3)], var_eps[:, ds(g * G3, G3)], neg_half[:, 0:G3], ALU.pow)
                pool.wait_ge(w_in[3], 16 * LOADS)
                loop(pool, group, NG3)
                barrier(pool, phase)

            return sync, tensor, scalar, vector, gpsimd

        phases = []

        def load_other(eng):
            barrier(eng, 0)
        phases.append((load_sync, load_other, load_other, load_dve, load_pool))
        makers = [lambda n: small_heads(0, n), lambda n: narrow(0, n), linear_attention, expert_choice, lambda n: small_heads(2, n),
                  gated_experts, wide_heads, lambda n: narrow(3, n)]
        for n, make in enumerate(makers):
            phases.append(make(n + 1))

        block = ctx.enter_context(nc.Block())

        @block.sync
        def _(sp):
            for phase in phases:
                phase[0](sp)
            for g in range(NG):
                sp.dma_start(out[g * G:(g + 1) * G].rearrange("b s d -> s b d"),
                             x[:, g * G:(g + 1) * G, :]).then_inc(x_out, 16)
            sp.wait_ge(x_out, 16 * NG)

        @block.tensor
        def _(pe):
            for phase in phases:
                phase[1](pe)

        @block.scalar
        def _(act):
            for phase in phases:
                phase[2](act)

        @block.vector
        def _(dve):
            for phase in phases:
                phase[3](dve)

        @block.gpsimd
        def _(pool):
            for phase in phases:
                phase[4](pool)


def kernel(**inputs):
    import numpy as np
    import concourse.bacc as bacc
    from concourse.bass_utils import run_bass_kernel_spmd

    def a(name):
        return np.asarray(inputs[name])

    def by_feature(w):
        return np.ascontiguousarray(w.reshape(H, DH, -1).swapaxes(0, 1).reshape(w.shape))

    lay = {"x": a("x"), "ctxT": np.ascontiguousarray(a("ctx_1024").reshape(B * P, P).T)}
    for l, names in ((0, "L0_xattn_{}{}"), (2, "L2_xattn_{}_{}")):
        for n in "qkvo":
            w, b = a(names.format("W", n)), a(names.format("b", n))
            if n in "qk":
                w, b = by_feature(w), by_feature(b)
            lay[f"w{n}{l}"], lay[f"b{n}{l}"] = np.ascontiguousarray(w.T), b
    lay["gate0"] = np.ascontiguousarray(a("L0_ffn_gate_W").T)
    lay["expert0"] = np.ascontiguousarray(a("L0_ffn_expert_W")[:2].swapaxes(0, 1))
    lay["outw0"] = np.ascontiguousarray(a("L0_ffn_out_W").T)
    lay["gate2"] = np.ascontiguousarray(a("L2_ffn_centroid").T)
    lay["wgu_2"] = np.stack([a("L2_ffn_Wg"), a("L2_ffn_W1")]).transpose(2, 0, 1, 3).reshape(P, -1)
    lay["w2_2"] = a("L2_ffn_W2").reshape(E, 3, 114, P).transpose(2, 0, 1, 3).reshape(114, -1)
    lay["bg_2"] = a("L2_ffn_bg").reshape(E, 3, 114).transpose(2, 0, 1)
    lay["b1_2"] = a("L2_ffn_b1").reshape(E, 3, 114).transpose(2, 0, 1)
    lay["b2_2"] = a("L2_ffn_b2")
    for n in "qkv":
        lay[f"w{n}3"] = a(f"L3_xattn_W{n}").T
    lay["wo3"] = a("L3_xattn_Wo").T.reshape(8, P, P).swapaxes(0, 1).reshape(P, -1)
    lay["bqk3"] = np.stack([a("L3_xattn_bq"), a("L3_xattn_bk")]).reshape(2, 8, P).transpose(2, 0, 1)
    lay["bv3"], lay["bo3"] = a("L3_xattn_bv"), a("L3_xattn_bo")
    lay["gate1"] = np.ascontiguousarray(a("L1_ffn_Wg").T)
    lay["w1_1"] = np.ascontiguousarray(a("L1_ffn_W1").swapaxes(0, 1).reshape(P, -1))
    lay["w2_1"] = np.ascontiguousarray(a("L1_ffn_W2").reshape(E, 4, P, P).transpose(2, 0, 1, 3).reshape(P, -1))
    lay["b1_1"] = np.ascontiguousarray(a("L1_ffn_b1").reshape(E, 4, P).transpose(2, 0, 1))
    lay["b2_1"] = a("L1_ffn_b2")
    lay["w1"] = np.stack([a("L1_xattn_wq"), a("L1_xattn_wk"), a("L1_xattn_wv"), a("L1_xattn_dense_w")])
    lay["row1"] = np.stack([a("L1_xattn_ln_gamma"), a("L1_xattn_ln_beta"), a("L1_xattn_dense_b")])
    lay["mask1"] = np.ascontiguousarray(a("mask_BxS2_ff1").T)
    lay["gate3"] = np.ascontiguousarray(a("L3_ffn_gate_w").T)
    lay["we3"] = np.ascontiguousarray(a("L3_ffn_We").swapaxes(0, 1))
    m = a("mask_1x1xSxS2_bk0")[0, 0].view(np.uint8)
    lay["mask2"] = np.ascontiguousarray(np.stack([m, m.T])).view(np.int32)

    nc = bacc.Bacc("TRN2", target_bir_lowering=False, num_devices=1)
    arrays, handles = {}, {}
    for name, v in lay.items():
        v = np.ascontiguousarray(v)
        arrays[f"in_{name}"] = v
        handles[name] = nc.dram_tensor(f"in_{name}", v.shape, mybir.dt.from_np(v.dtype), kind="ExternalInput").ap()
    out = nc.dram_tensor("out_x", (B, P, P), F32, kind="ExternalOutput").ap()
    program(nc, handles, out)
    r = run_bass_kernel_spmd(nc, [arrays], core_ids=[0])
    return r.results[0]["out_x"]
```

```python
from contextlib import ExitStack

import concourse.bass as bass
from concourse import mybir

F32 = mybir.dt.float32
BF16 = mybir.dt.bfloat16
U8 = mybir.dt.uint8
I32 = mybir.dt.int32
ALU = mybir.AluOpType
ACT = mybir.ActivationFunctionType
AX = mybir.AxisListType

P = 128
B = 32
G = 4
NG = B // G
W = G * P
H = 16
DH = P // H
E = 8
LN_EPS = 1e-5
NEG = -3.38e38
PARTS = 3
TERMS = ((0, 0), (1, 0), (2, 0), (0, 1), (1, 1), (0, 2))


def ds(start, n):
    return bass.ds(start, n)


class Arena:

    def __init__(self, tensor, words):
        self.tensor, self.words, self.at = tensor, words, 0

    def restart(self):
        self.at = 0

    def take(self, shape, dtype=F32):
        n = 1
        for s in shape:
            n *= s
        words = n if dtype == F32 else (n + 1) // 2
        words = (words + 15) // 16 * 16
        piece = self.tensor[:, self.at:self.at + words]
        self.at += words
        assert self.at <= self.words, self.at
        if dtype != F32:
            piece = piece.bitcast(dtype)
        piece = piece[:, 0:n]
        names = " ".join(f"a{i}" for i in range(len(shape)))
        sizes = {f"a{i}": s for i, s in enumerate(shape)}
        return piece if len(shape) == 1 else piece.rearrange(f"p ({names}) -> p {names}", **sizes)


def program(nc, t, out):
    ctx = ExitStack()
    with ctx:
        def sb(name, shape, dtype=F32):
            return ctx.enter_context(nc.sbuf_tensor(name, shape, dtype))

        def sem(name):
            return ctx.enter_context(nc.semaphore(name))

        x = sb("x", [P, B, P])
        mean = sb("mean", [P, B])
        var_eps = sb("var_eps", [P, B])
        rstd = sb("rstd", [P, B])
        ident = sb("ident", [P, P])
        identb = sb("identb", [P, P], BF16)
        shift_rows = sb("shift_rows", [P, H, P], BF16)
        ones_cols = sb("ones_cols", [P, 4, 32])
        neg_half = sb("neg_half", [P, G])
        mask_bias = {l: [sb(f"mask{n}{l}", [P, 4, P], BF16) for n in names]
                     for l, names in ((0, "ST"), (2, "ST"), (3, "S"))}
        mask_words = sb("mask_words", [P, 2, P // 4], I32)
        aw = {l: {n: sb(f"w{n}{l}", [P, P]) for n in "qkvo"} for l in (0, 2)}
        acol = {l: sb(f"acol{l}", [P, 4]) for l in (0, 2)}
        arow = {l: sb(f"arow{l}", [P, 2, P]) for l in (0, 2)}
        gates = {l: sb(f"gate{l}", [P, E]) for l in range(4)}
        expert0 = sb("expert0", [P, 2, P])
        outw0 = sb("outw0", [P, P])
        folded = sb("folded", [P, 2, P])[:]
        we3 = sb("we3", [P, E, P])[:]
        iota_i = sb("iota_i", [P, 64], mybir.dt.int32)[:]
        wide = sb("wide", [P, 8704])[:]
        earlier = sb("earlier", [P, E * E])
        ARENA = 33 * 1024
        arena = Arena(sb("arena", [P, ARENA]), ARENA)
        bank = [ctx.enter_context(nc.psum_tensor(f"bank{i}", [P, 512], F32)) for i in range(8)]

        phase_done = sem("phase_done")
        XL = NG // 4
        x_in = [sem(f"x_in{i}") for i in range(4)]
        ww_in = sem("ww_in")
        x_out = sem("x_out")
        fw_in = {l: sem(f"fw_in{l}") for l in range(4)}
        fw_loads = {0: 3, 1: 3 + 1 + E + 1, 2: 1 + 3 + 2 + 1, 3: 2}
        w_in = {l: sem(f"w_in{l}") for l in range(4)}
        setup_v = sem("setup_v")

        def barrier(eng, phase):
            eng.drain().then_inc(phase_done, 1)
            eng.wait_ge(phase_done, 5 * (phase + 1))

        twins = {}

        def twin_sems(maker, names):
            if maker not in twins:
                twins[maker] = {n: sem(f"{n}_{maker}") for n in names}
            return twins[maker]

        def clear_twins(pool):
            for maker in twins.values():
                for signal in maker.values():
                    pool.sem_clear(signal)

        def loop(eng, group, groups=NG):
            with eng.Fori(0, groups // 2 - 1) as i:
                for u in range(2):
                    group(2 * i + u, u, False)
            for u in range(2):
                group(groups - 2 + u, u, u == 1)

        def load_sync(sp):
            for i in range(4):
                part = slice(i * XL * G, (i + 1) * XL * G)
                sp.dma_start(x[:, part, :], t["x"][part].rearrange("b s d -> s b d")).then_inc(x_in[i], 16)
            for l in (0, 2):
                for n in "qkvo":
                    sp.dma_start(aw[l][n][:], t[f"w{n}{l}"]).then_inc(w_in[l], 16)
                for i, n in enumerate("qk"):
                    sp.dma_start(acol[l][:, i:i + 1], t[f"b{n}{l}"].rearrange("(p a) -> p a", a=1)).then_inc(w_in[l], 16)
                for i, n in enumerate("vo"):
                    row = t[f"b{n}{l}"].rearrange("(a n) -> a n", a=1)
                    sp.dma_start(arow[l][:, i, :], row.broadcast_to([P, P])).then_inc(w_in[l], 16)
            for i in range(2):
                sp.dma_start(mask_words[:, i, :], t["mask2"][i]).then_inc(w_in[2], 16)
            sp.dma_start(gates[0][:], t["gate0"]).then_inc(fw_in[0], 16)
            sp.dma_start(expert0[:], t["expert0"]).then_inc(fw_in[0], 16)
            sp.dma_start(outw0[:], t["outw0"]).then_inc(fw_in[0], 16)
            sp.dma_start(gates[1][:], t["gate1"]).then_inc(fw_in[1], 16)
            sp.dma_start(wide[:, 0:4096], t["w1_1"]).then_inc(fw_in[1], 16)
            sp.dma_start(wide[:, 4096:8192], t["w2_1"]).then_inc(fw_in[1], 16)
            sp.dma_start(gates[2][:], t["gate2"]).then_inc(fw_in[2], 16)
            sp.dma_start(gates[3][:], t["gate3"]).then_inc(fw_in[3], 16)
            sp.dma_start(we3, t["we3"]).then_inc(fw_in[3], 16)
            barrier(sp, 0)

        def load_pool(pool):
            pool.memset(ident[:], 0.0)
            pool.memset(identb[:], 0.0)
            pool.memset(shift_rows[:], 0.0)
            pool.memset(ones_cols[:], 0.0)
            pool.memset(neg_half[:], -0.5)
            pool.memset(earlier[:], 1.0)
            for l in (0, 3):
                for m in mask_bias[l]:
                    pool.memset(m[:], 0.0)
            pool.drain()
            for m in (ident, identb):
                pool.affine_select(out=m[:], in_=m[:], compare_op=ALU.not_equal, fill=1.0, base=0,
                                   pattern=[[-1, P]], channel_multiplier=1)
            pool.affine_select(out=shift_rows[:], in_=shift_rows[:], compare_op=ALU.not_equal, fill=1.0,
                               base=0, pattern=[[-1, H], [0, P]], channel_multiplier=1)
            for j in range(4):
                pool.memset(ones_cols[:, j, 8 * j:8 * j + 8], 1.0)
            for m in mask_bias[0]:
                pool.affine_select(out=m[:], in_=m[:], compare_op=ALU.is_ge, fill=NEG, base=64,
                                   pattern=[[0, 4], [-1, P]], channel_multiplier=1)
            pool.affine_select(out=mask_bias[3][0][:], in_=mask_bias[3][0][:], compare_op=ALU.is_ge, fill=NEG,
                               base=0, pattern=[[0, 4], [-1, P]], channel_multiplier=1)
            pool.drain()
            pool.affine_select(out=shift_rows[:], in_=shift_rows[:], compare_op=ALU.not_equal, fill=1.0,
                               base=-H, pattern=[[-1, H], [0, P]], channel_multiplier=1)
            for m in mask_bias[0]:
                pool.affine_select(out=m[:], in_=m[:], compare_op=ALU.is_ge, fill=NEG, base=64,
                                   pattern=[[0, 4], [1, P]], channel_multiplier=-1)
            pool.affine_select(out=earlier[:].rearrange("p (e f) -> p e f", e=E),
                               in_=earlier[:].rearrange("p (e f) -> p e f", e=E), compare_op=ALU.is_gt, fill=0.0,
                               base=0, pattern=[[1, E], [-1, E]], channel_multiplier=0)
            for g in range(NG):
                pool.wait_ge(setup_v, g + 1)
                rstd_of(pool, g * G)
            barrier(pool, 0)

        def stats_of(dve, first, bn, agg):
            for j in range(G):
                dve.bn_stats(bn[:, j, :], x[:, ds(first + j, 1), :])
            dve.drain()
            for j in range(G):
                dve.bn_aggr(agg[:, j, :], bn[:, j, :])
            dve.drain()
            dve.tensor_copy(mean[:, ds(first, G)], agg[:, :, 0])
            return dve.tensor_scalar(var_eps[:, ds(first, G)], agg[:, :, 1], LN_EPS, None, ALU.add)

        def rstd_of(pool, first):
            pool.tensor_tensor(rstd[:, ds(first, G)], var_eps[:, ds(first, G)], neg_half[:], ALU.pow)

        bn0 = sb("bn0", [P, G, 6])
        agg0 = sb("agg0", [P, G, 2])

        def load_dve(dve):
            for g in range(NG):
                if g % XL == 0:
                    dve.wait_ge(x_in[g // XL], 16)
                stats_of(dve, g * G, bn0, agg0).then_inc(setup_v, 1)
                dve.drain()
            dve.wait_ge(w_in[2], 16 * 10)
            for i, m in enumerate(mask_bias[2]):
                for j in range(4):
                    dve.tensor_scalar(m[:, j, :], mask_words[:, i, :].bitcast(U8), -1.0, -NEG, ALU.add, ALU.mult)
            for l in (0, 2):
                dve.wait_ge(w_in[l], 16 * (8 + (l == 2) * 2))
                dve.tensor_scalar(acol[l][:, 2:3], acol[l][:, 0:1], float(DH) ** -0.5, None, ALU.mult)
            barrier(dve, 0)

        def small_heads(l, phase):
            s = twin_sems("heads8", (
                "ctx_in0", "ctx_in1", "xn_ready", "tr_ready", "xnT_ready", "q_ready", "q_evac", "k_ready",
                "k_evac", "v_mm", "v_evac", "parts_ready", "parts_out", "stack_in0", "stack_in1", "s_ready",
                "s_free", "mhl_ready", "mt_ready", "mts_ready", "st_ready", "st_free", "pv_ready", "o_free",
                "o_ready", "x_done", "xb_ready", "zero_ready", "stats_ready"))
            arena.restart()
            stack_q = [arena.take([H, W], BF16) for _ in range(2)]
            stack_k = [arena.take([H, W], BF16) for _ in range(2)]
            probs = [arena.take([H, P]) for _ in range(2)]
            values = [arena.take([G, H, 32]) for _ in range(2)]
            ctxT = [arena.take([W]) for _ in range(2)]
            xn = [arena.take([G, P]) for _ in range(2)]
            xb = [arena.take([G, P]) for _ in range(2)]
            xnT = arena.take([W])
            qf, kf, rest = arena.take([W]), arena.take([W]), arena.take([W])
            parts = [arena.take([PARTS, W], BF16) for _ in range(2)]
            attnT = arena.take([2, G, P])
            mx, mhl = arena.take([2, H]), arena.take([2, 2 * H], BF16)
            mts = arena.take([2, P], BF16)
            inv = arena.take([2, P])
            bn, agg = arena.take([G, 6]), arena.take([G, 2])
            qd = [[nc.dram_tensor(f"parts{n}{l}{u}", [PARTS, P, W], BF16).ap() for u in range(2)] for n in "qk"]
            S, T, O, M = bank[0:2], bank[2:4], bank[4:6], bank[6:8]
            wq, wk, wv, wo = (aw[l][n] for n in "qkvo")
            maskS, maskT = mask_bias[l]
            nk = len(TERMS)

            def sync(sp):
                def load_ctx(g, u):
                    sp.dma_start(ctxT[u], t["ctxT"][:, ds(g * W, W)]).then_inc(s[f"ctx_in{u}"], 16)

                def exchange(g, u):
                    sp.wait_ge(s["parts_ready"], g + 1)
                    for a in range(2):
                        sp.dma_start(qd[a][u].rearrange("a p t -> p a t"), parts[a]).then_inc(s["parts_out"], 16)
                    sp.wait_ge(s["parts_out"], 32 * g + 32)
                    rows = [qd[a][u].rearrange("a (d h) t -> a d (h t)", h=H) for a in range(2)]
                    for a, stack in ((0, stack_q[u]), (1, stack_k[u])):
                        flat = stack.rearrange("p h t -> p (h t)")
                        for n, term in enumerate(TERMS):
                            sp.dma_start(flat[DH * n:DH * n + DH, :], rows[a][term[a]]).then_inc(s[f"stack_in{u}"], 16)

                load_ctx(0, 0)
                load_ctx(1, 1)
                if l == 2:
                    load_wide2(sp)
                sp.wait_ge(s["zero_ready"], 1)
                exchange(0, 0)
                sp.wait_ge(s["zero_ready"], 2)

                def group(g, u, last):
                    if last:
                        return
                    sp.wait_ge(s["v_mm"], g + 1)
                    if not isinstance(g, int) or g + 2 < NG:
                        load_ctx(g + 2, u)
                    exchange(g + 1, 1 - u)
                loop(sp, group)
                barrier(sp, phase)

            def tensor(pe):
                def front(g, u, first=False):
                    pe.wait_ge(s["xn_ready"], g + 1)
                    if not first:
                        pe.wait_ge(s["k_evac"], g)
                        pe.wait_ge(s["x_done"], g)
                    for j in range(G):
                        mm = pe.transpose(M[0][:, j * P:(j + 1) * P], xn[u][:, j, :], ident[:])
                    mm.then_inc(s["tr_ready"], 1)
                    pe.wait_ge(s["xnT_ready"], g + 1)
                    if not first:
                        pe.wait_ge(s["v_evac"], g)
                    pe.matmul(M[1][:], wq[:], xnT, start=True, stop=True).then_inc(s["q_ready"], 1)
                    pe.wait_ge(s[f"ctx_in{u}"], (g - u) * 8 + 16)
                    pe.matmul(M[0][:], wk[:], ctxT[u], start=True, stop=True).then_inc(s["k_ready"], 1)
                    pe.wait_ge(s["q_evac"], g + 1)
                    for j in range(G):
                        mm = pe.matmul(M[1][:, j * P:(j + 1) * P], ctxT[u][:, j * P:(j + 1) * P], wv[:],
                                       start=True, stop=True)
                    mm.then_inc(s["v_mm"], 1)

                def scores(n, u, j):
                    for c in range(4):
                        pe.wait_ge(s["s_free"], 4 * n + c + 1)
                        pe.matmul(S[c % 2][:], identb[:], maskS[:].rearrange("p a k -> p (a k)"),
                                  start=True, stop=False, skip_group_check=True)
                        for h in range(4 * c, 4 * c + 4):
                            mm = pe.matmul(S[c % 2][:, (h % 4) * P:(h % 4 + 1) * P],
                                           stack_q[u][:, h, j * P:(j + 1) * P],
                                           stack_k[u][:, h, j * P:(j + 1) * P],
                                           start=False, stop=(h % 4 == 3), skip_group_check=True)
                        mm.then_inc(s["s_ready"], 1)

                def turn_max(n, b):
                    pe.wait_ge(s["mhl_ready"], n + 1)
                    pe.wait_ge(s["o_free"], n + 1)
                    pe.transpose(O[b][0:2 * H, 256:320].bitcast(BF16), mhl[:, b, :], identb[:]).then_inc(s["mt_ready"], 1)

                def scoresT(n, u, j, b):
                    for c in range(4):
                        pe.wait_ge(s["st_free"], 4 * n + c + 1)
                        pe.matmul(T[c % 2][:], identb[:], maskT[:].rearrange("p a k -> p (a k)"),
                                  start=True, stop=False, skip_group_check=True)
                        for h in range(4 * c, 4 * c + 4):
                            pe.matmul(T[c % 2][:, (h % 4) * P:(h % 4 + 1) * P],
                                      stack_k[u][:, h, j * P:(j + 1) * P],
                                      stack_q[u][:, h, j * P:(j + 1) * P],
                                      start=False, stop=False, skip_group_check=True)
                        if c == 0:
                            pe.wait_ge(s["mts_ready"], n + 1)
                        for h in range(4 * c, 4 * c + 4):
                            mm = pe.matmul(T[c % 2][:, (h % 4) * P:(h % 4 + 1) * P],
                                           shift_rows[:, h, :], mts[:, b, :],
                                           start=False, stop=(h % 4 == 3), skip_group_check=True)
                        mm.then_inc(s["st_ready"], 1)

                def attend(n, u, j, b):
                    for c in range(4):
                        pe.wait_ge(s["st_free"], 4 * n + c + 3)
                        rows = slice(32 * c, 32 * c + 32)
                        for k, lhs in enumerate((lambda h: values[u][:, j, h, :], lambda h: ones_cols[:, h % 4, :])):
                            for h in range(4 * c, 4 * c + 4):
                                mm = pe.matmul(O[b][rows, k * P:(k + 1) * P], lhs(h), probs[b][:, h, :],
                                               start=(h % 4 == 0), stop=(h % 4 == 3), skip_group_check=True)
                    mm.then_inc(s["pv_ready"], 1)

                pe.wait_ge(w_in[l], 16 * (8 + (l == 2) * 2))
                front(0, 0, first=True)
                pe.wait_ge(s["stack_in0"], 16 * 2 * nk)
                scores(0, 0, 0)

                def group(g, u, last):
                    for j in range(G):
                        n, b = g * G + j, j % 2
                        turn_max(n, b)
                        if j == 0:
                            pe.wait_ge(s["v_evac"], g + 1)
                        scoresT(n, u, j, b)
                        if j < G - 1:
                            scores(n + 1, u, j + 1)
                        elif not last:
                            pe.wait_ge(s[f"stack_in{1 - u}"], stack_count(g + 1, 1 - u))
                            scores(n + 1, 1 - u, 0)
                        attend(n, u, j, b)
                        if j == 0 and not last:
                            front(g + 1, 1 - u)
                    pe.wait_ge(s["k_evac"], g + 1 if last else g + 2)
                    pe.wait_ge(s["o_free"], g * G + G + 2)
                    for j in range(G):
                        mm = pe.matmul(M[0][:, j * P:(j + 1) * P], attnT[:, u, j, :], wo[:], start=True, stop=True)
                    mm.then_inc(s["o_ready"], 1)
                loop(pe, group)
                barrier(pe, phase)

            def stack_count(g, u):
                return (g - u) * (16 * nk) + 32 * nk

            def scalar(act):
                def front(g, u):
                    act.wait_ge(s["tr_ready"], g + 1)
                    act.activation(xnT, M[0][:], ACT.Copy).then_inc(s["xnT_ready"], 1)
                    act.wait_ge(s["q_ready"], g + 1)
                    act.wait_ge(s["parts_ready"], g)
                    act.activation(qf, M[1][:], ACT.Identity, bias=acol[l][:, 2:3],
                                   scale=float(DH) ** -0.5).then_inc(s["q_evac"], 1)
                    act.wait_ge(s["k_ready"], g + 1)
                    act.activation(kf, M[0][:], ACT.Identity, bias=acol[l][:, 1:2]).then_inc(s["k_evac"], 1)

                front(0, 0)
                for b in range(2):
                    act.activation(mts[:, b, :], identb[:], ACT.Copy, scale=0.0)
                act.drain()

                def group(g, u, last):
                    for j in range(G):
                        n, b = g * G + j, j % 2
                        act.wait_ge(s["mt_ready"], n + 1)
                        act.activation(mts[0:2 * H, b, :], O[b][0:2 * H, 256:320].bitcast(BF16),
                                       ACT.Copy).then_inc(s["mts_ready"], 1)
                        for c in range(4):
                            act.wait_ge(s["st_ready"], 4 * n + c + 1)
                            act.activation(probs[b][:, 4 * c:4 * c + 4, :].rearrange("p a q -> p (a q)"),
                                           T[c % 2][:], ACT.Exp).then_inc(s["st_free"], 1)
                        if j == 0 and not last:
                            front(g + 1, 1 - u)
                loop(act, group)
                barrier(act, phase)

            def vector(dve):
                def normed(g, u):
                    for j in range(G):
                        mm = dve.tensor_scalar(xn[u][:, j, :], x[:, ds(g * G + j, 1), :], mean[:, ds(g * G + j, 1)],
                                               rstd[:, ds(g * G + j, 1)], ALU.subtract, ALU.mult)
                    mm.then_inc(s["xn_ready"], 1)

                def front(g, u, first=False):
                    dve.wait_ge(s["v_mm"], g + 1)
                    for j in range(G):
                        src = M[1][:, j * P:(j + 1) * P].rearrange("p (c j e) -> p c j e", c=4, j=4)
                        bias = arow[l][:, 0, :].rearrange("p (c j e) -> p c j e", c=4, j=4)
                        mm = dve.tensor_tensor(diagonal(values[u], j), src, bias, ALU.add)
                    mm.then_inc(s["v_evac"], 1)
                    if not first:
                        dve.wait_ge(s["parts_out"], 32 * g)
                    for a, (full, ready) in enumerate(((qf, "q_evac"), (kf, "k_evac"))):
                        dve.wait_ge(s[ready], g + 1)
                        dve.tensor_copy(parts[a][:, 0, :], full)
                        dve.drain()
                        dve.tensor_tensor(rest, full, parts[a][:, 0, :], ALU.subtract)
                        dve.drain()
                        dve.tensor_copy(parts[a][:, 1, :], rest)
                        dve.drain()
                        mm = dve.tensor_tensor(parts[a][:, 2, :], rest, parts[a][:, 1, :], ALU.subtract)
                    mm.then_inc(s["parts_ready"], 1)

                def maxima(n, b):
                    for c in range(4):
                        dve.wait_ge(s["s_ready"], 4 * n + c + 1)
                        dve.tensor_reduce(mx[:, b, 4 * c:4 * c + 4], S[c % 2][:].rearrange("p (a k) -> p a k", a=4),
                                          AX.X, ALU.max).then_inc(s["s_free"], 1)
                    dve.drain()
                    dve.tensor_scalar(mhl[:, b, 0:H], mx[:, b, :], -1.0, None, ALU.mult)
                    dve.drain()
                    dve.scalar_tensor_tensor(out=mhl[:, b, H:2 * H], in0=mx[:, b, :], scalar=-1.0,
                                             in1=mhl[:, b, 0:H], op0=ALU.mult, op1=ALU.subtract
                                             ).then_inc(s["mhl_ready"], 1)

                for u in range(2):
                    dve.memset(values[u].rearrange("p a b c -> p (a b c)"), 0.0)
                dve.drain().then_inc(s["s_free"], 2)
                dve.drain().then_inc(s["x_done"], 1)
                normed(0, 0)
                front(0, 0, first=True)
                maxima(0, 0)

                def group(g, u, last):
                    for j in range(G):
                        n, b = g * G + j, j % 2
                        if j == 0 and not last:
                            normed(g + 1, 1 - u)
                        if j < G - 1 or not last:
                            maxima(n + 1, 1 - b)
                        dve.wait_ge(s["pv_ready"], n + 1)
                        dve.reciprocal(inv[:, b, :], O[b][:, P:2 * P])
                        dve.drain()
                        dve.tensor_tensor(attnT[:, u, j, :], O[b][:, 0:P], inv[:, b, :], ALU.mult).then_inc(s["o_free"], 1)
                        if j == 0 and not last:
                            front(g + 1, 1 - u)
                    dve.wait_ge(s["o_ready"], g + 1)
                    dve.wait_ge(s["xb_ready"], g + 1)
                    dve.tensor_tensor(x[:, ds(g * G, G), :], M[0][:].rearrange("p (a b) -> p a b", a=G), xb[u],
                                      ALU.add).then_inc(s["x_done"], 1)
                    dve.drain()
                    stats_of(dve, g * G, bn, agg).then_inc(s["stats_ready"], 1)
                loop(dve, group)
                barrier(dve, phase)

            def gpsimd(pool):
                pool.engine_nop().then_inc(s["st_free"], 2)
                pool.engine_nop().then_inc(s["o_free"], 2)
                for u in range(2):
                    pool.memset(stack_q[u].rearrange("p h t -> p (h t)").bitcast(F32), 0.0)
                    pool.memset(stack_k[u].rearrange("p h t -> p (h t)").bitcast(F32), 0.0
                                ).then_inc(s["zero_ready"], 1)

                def group(g, u, last):
                    bo = arow[l][:, 1, :].unsqueeze(1).broadcast_to([P, G, P])
                    pool.tensor_tensor(xb[u], x[:, ds(g * G, G), :], bo, ALU.add).then_inc(s["xb_ready"], 1)
                    pool.wait_ge(s["stats_ready"], g + 1)
                    rstd_of(pool, g * G)
                pool.wait_ge(w_in[l], 16 * (8 + (l == 2) * 2))
                loop(pool, group)
                barrier(pool, phase)

            return sync, tensor, scalar, vector, gpsimd

        def diagonal(tile, j):
            v = tile[:, j, :, :].rearrange("p h e -> p (h e)")
            a = v.copy()
            step, count = v.ap[0]
            return bass.AP(tensor=v.tensor, offset=v.offset, ap=[[step, count], [P, 4], [40, 4], [1, 8]])

        def rank_below(dve, logits, cmp, cmp2, rank, below, n=G):
            mine = logits.unsqueeze(3).broadcast_to([P, n, E, E])
            other = logits.unsqueeze(2).broadcast_to([P, n, E, E])
            early = earlier[:].unsqueeze(1).broadcast_to([P, n, E * E]).rearrange("p g (e f) -> p g e f", e=E)
            dve.tensor_tensor(cmp, other, mine, ALU.is_gt)
            dve.tensor_tensor(cmp2, other, mine, ALU.is_equal)
            dve.drain()
            dve.tensor_tensor(cmp2.rearrange("p g e f -> p g (e f)"), cmp2.rearrange("p g e f -> p g (e f)"),
                              early.rearrange("p g e f -> p g (e f)"), ALU.mult)
            dve.drain()
            dve.tensor_tensor(cmp, cmp, cmp2, ALU.add)
            dve.drain()
            dve.tensor_reduce(rank, cmp, AX.X, ALU.add)
            dve.drain()
            dve.tensor_scalar(rank, rank, float(below), None, ALU.is_lt)
            dve.drain()

        def narrow(l, phase):
            s = twin_sems("narrow", (
                "xn_ready", "tr_ready", "xnT_ready", "logits_ready", "shifted_ready", "exp_ready", "h_ready",
                "h_free", "stats_ready", "fold_ready", "folded"))
            n_exp = 2 if l == 0 else E
            arena.restart()
            xn = [arena.take([G, P]) for _ in range(2)]
            xnT = [arena.take([W]) for _ in range(2)]
            logits, z, ez, sel = (arena.take([B, E]) for _ in range(4))
            cmp, cmp2 = arena.take([B, E, E]), arena.take([B, E, E])
            top, total, count = arena.take([B]), arena.take([B]), arena.take([B, 2])
            weight_flat = arena.take([B * E])
            weight = weight_flat.rearrange("p (b e) -> p b e", b=B)
            bn, agg = arena.take([G, 6]), arena.take([G, 2])
            gate = gates[l]
            experts = (folded if l == 0 else we3).rearrange("p e m -> p (e m)")
            BLOCK = min(512, n_exp * P)
            blocks = n_exp * P // BLOCK

            def slot(j, k):
                return bank[4 + j] if l == 0 else bank[4 + 2 * k + j % 2]

            def sync(sp):
                barrier(sp, phase)

            def tensor(pe):
                def turn(g, u):
                    pe.wait_ge(s["xn_ready"], g + 1)
                    for j in range(G):
                        mm = pe.transpose(bank[u][:, j * P:(j + 1) * P], xn[u][:, j, :], ident[:])
                    mm.then_inc(s["tr_ready"], 1)

                pe.wait_ge(fw_in[l], 16 * fw_loads[l])
                if l == 0:
                    for e in range(n_exp):
                        mm = pe.matmul(bank[4][:, e * P:(e + 1) * P], expert0[:, e, :], outw0[:], start=True, stop=True)
                    mm.then_inc(s["fold_ready"], 1)
                turn(0, 0)

                def gate_group(g, u, last):
                    if not last:
                        turn(g + 1, 1 - u)
                    pe.wait_ge(s["xnT_ready"], g + 1)
                    for j in range(G):
                        mm = pe.matmul(bank[2 + u][:, j * E:(j + 1) * E], xnT[u][:, j * P:(j + 1) * P], gate[:],
                                       start=True, stop=True)
                    mm.then_inc(s["logits_ready"], 1)
                loop(pe, gate_group)
                if l == 0:
                    pe.wait_ge(s["folded"], 1)
                turn(NG, 0)

                def group(g, u, last):
                    pe.wait_ge(s["xnT_ready"], NG + g + 1)
                    for pair in range(2):
                        if pair == 1 and not last:
                            turn(NG + g + 1, 1 - u)
                        for k in range(blocks):
                            pe.wait_ge(s["h_free"], 2 * blocks * g + blocks * pair + k + 1)
                            for j in (2 * pair, 2 * pair + 1):
                                mm = pe.matmul(slot(j, k)[:, 0:BLOCK], xnT[u][:, j * P:(j + 1) * P],
                                               experts[:, BLOCK * k:BLOCK * (k + 1)], start=True, stop=True)
                            mm.then_inc(s["h_ready"], 1)
                loop(pe, group)
                barrier(pe, phase)

            def scalar(act):
                if l == 0:
                    act.wait_ge(s["fold_ready"], 1)
                    act.activation(folded.rearrange("p e m -> p (e m)"), bank[4][:, 0:2 * P], ACT.Copy).then_inc(s["folded"], 1)

                def gate_group(g, u, last):
                    act.wait_ge(s["tr_ready"], g + 1)
                    act.activation(xnT[u], bank[u][:], ACT.Copy).then_inc(s["xnT_ready"], 1)
                loop(act, gate_group)
                act.wait_ge(s["shifted_ready"], 1)
                act.activation(ez, z, ACT.Exp).then_inc(s["exp_ready"], 1)

                def group(g, u, last):
                    act.wait_ge(s["tr_ready"], NG + g + 1)
                    act.activation(xnT[u], bank[u][:], ACT.Copy).then_inc(s["xnT_ready"], 1)
                loop(act, group)
                barrier(act, phase)

            def vector(dve):
                def normed(g, u):
                    for j in range(G):
                        mm = dve.tensor_scalar(xn[u][:, j, :], x[:, ds(g * G + j, 1), :], mean[:, ds(g * G + j, 1)],
                                               rstd[:, ds(g * G + j, 1)], ALU.subtract, ALU.mult)
                    mm.then_inc(s["xn_ready"], 1)

                normed(0, 0)
                normed(1, 1)

                def gate_group(g, u, last):
                    dve.wait_ge(s["logits_ready"], g + 1)
                    dve.tensor_scalar(logits[:, ds(g * G, G), :],
                                      bank[2 + u][:, 0:G * E].rearrange("p (g e) -> p g e", g=G), 1.0, None, ALU.mult)
                    if not (isinstance(g, int) and g + 2 >= NG):
                        normed(g + 2, u)
                loop(dve, gate_group)
                dve.drain().then_inc(s["h_free"], 2)

                dve.tensor_reduce(top, logits, AX.X, ALU.max)
                dve.drain()
                dve.tensor_tensor(z, logits, top.unsqueeze(2).broadcast_to([P, B, E]),
                                  ALU.subtract).then_inc(s["shifted_ready"], 1)
                if l == 3:
                    rank_below(dve, logits, cmp, cmp2, sel, 2, B)
                dve.wait_ge(s["exp_ready"], 1)
                if l == 3:
                    dve.tensor_tensor(ez, ez, sel, ALU.mult)
                    dve.drain()
                dve.tensor_reduce(total, ez, AX.X, ALU.add)
                dve.drain()
                dve.reciprocal(total, total)
                dve.drain()
                dve.tensor_tensor(weight, ez, total.unsqueeze(2).broadcast_to([P, B, E]), ALU.mult)
                dve.drain()
                if l == 0:
                    dve.tensor_scalar(sel, weight, 0.3, None, ALU.is_gt)
                    dve.drain()
                    dve.tensor_reduce(count[:, :, 1:2].rearrange("p g a -> p (g a)"), sel, AX.X, ALU.add)
                    dve.drain()
                    dve.tensor_scalar(count[:, :, 0], count[:, :, 1], -1.0, float(E), ALU.mult, ALU.add)
                    dve.drain()
                    dve.tensor_tensor(weight[:, :, 0:2], weight[:, :, 0:2], count, ALU.mult)
                    dve.drain()

                normed(0, 0)

                def group(g, u, last):
                    if not last:
                        normed(g + 1, 1 - u)
                    for pair in range(2):
                        for k in range(blocks):
                            dve.wait_ge(s["h_ready"], 2 * blocks * g + blocks * pair + k + 1)
                            for i in range(BLOCK // P):
                                for j in (2 * pair, 2 * pair + 1):
                                    n, e = g * G + j, k * (BLOCK // P) + i
                                    here = x[:, ds(n, 1), :].rearrange("p a m -> p (a m)")
                                    mm = dve.scalar_tensor_tensor(out=here, in0=slot(j, k)[:, i * P:(i + 1) * P],
                                                                  scalar=weight_flat[:, ds(n * E + e, 1)], in1=here,
                                                                  op0=ALU.mult, op1=ALU.add)
                                if i == BLOCK // P - 1:
                                    mm.then_inc(s["h_free"], 1)
                                dve.drain()
                    if l == 0:
                        stats_of(dve, g * G, bn, agg).then_inc(s["stats_ready"], 1)
                loop(dve, group)
                barrier(dve, phase)

            def gpsimd(pool):
                if l == 0:
                    def group(g, u, last):
                        pool.wait_ge(s["stats_ready"], g + 1)
                        rstd_of(pool, g * G)
                    loop(pool, group)
                barrier(pool, phase)

            return sync, tensor, scalar, vector, gpsimd

        def linear_attention(phase):
            s = {n: sem(f"{n}_1") for n in (
                "ctx_in0", "ctx_in1", "xn_ready", "tr_ready", "xnT_ready", "proj_ready", "var_ready", "rs_ready",
                "normed_ready", "q_final", "kv_final", "v_scaled", "qT_ready", "qT_evac", "kv_ready", "kv_masked",
                "att_ready", "att_normed", "swap_ready", "swap_a", "swap_v",
                "attT_ready", "attT_evac", "y_ready", "yvar_ready", "yrs_ready",
                "x_done", "stats_ready")}
            KW = P + H
            EPS_K = EPS_1 = 1e-6
            arena.restart()
            ctxT = [arena.take([W]) for _ in range(2)]
            xn = arena.take([G, P])
            xnT = arena.take([W])
            proj = [[arena.take([G, P]) for _ in range(3)] for _ in range(2)]
            v_wide = [arena.take([G, KW]) for _ in range(2)]
            qT = arena.take([W])
            kvx = arena.take([G, KW])
            den = arena.take([G, H])
            att = arena.take([G, P])
            attT = arena.take([W])
            y = arena.take([G, P])
            bn, agg = arena.take([3 * G, 6]), arena.take([3 * G, 2])
            bny, aggy = arena.take([G, 6]), arena.take([G, 2])
            ve, rs, nm = arena.take([3 * G]), arena.take([3 * G]), arena.take([3 * G])
            vey, rsy = arena.take([G]), arena.take([G])
            bnx, aggx = arena.take([G, 6]), arena.take([G, 2])
            gb = arena.take([3, P])
            em = arena.take([B])
            block_mask = arena.take([KW])
            w = arena.take([4, P])
            half = arena.take([3 * G])
            swap = arena.take([2, DH, P])
            T, Q, K, V, KV0, KV1, A0, A1 = bank
            swap_bank = ((A0, A1), (KV0, KV1))

            def swapped(j, half):
                return swap[0:H, j % 2, :, :].rearrange("p k (n e) -> p e (k n)", e=DH)[:, 4 * half:4 * half + 4, :]

            def bc(row):
                return row.unsqueeze(1).broadcast_to([P, G, P])

            def sync(sp):
                for i in range(4):
                    sp.dma_start(w[:, i, :], t["w1"][i]).then_inc(ww_in, 16)
                for i in range(3):
                    row = t["row1"][i].rearrange("(a n) -> a n", a=1)
                    sp.dma_start(gb[:, i, :], row.broadcast_to([P, P])).then_inc(ww_in, 16)
                sp.dma_start(em, t["mask1"]).then_inc(ww_in, 16)
                for g in range(2):
                    sp.dma_start(ctxT[g], t["ctxT"][:, g * W:(g + 1) * W]).then_inc(s[f"ctx_in{g}"], 16)

                def group(g, u, last):
                    if isinstance(g, int) and g + 2 >= NG:
                        return
                    sp.wait_ge(s["proj_ready"], 3 * g + 3)
                    sp.dma_start(ctxT[u], t["ctxT"][:, ds((g + 2) * W, W)]).then_inc(s[f"ctx_in{u}"], 16)
                loop(sp, group)
                barrier(sp, phase)

            def tensor(pe):
                def turn(g, first=False):
                    pe.wait_ge(s["xn_ready"], g + 1)
                    if not first:
                        pe.wait_ge(s["normed_ready"], 3 * g)
                        pe.wait_ge(s["attT_evac"], g)
                        pe.wait_ge(s["qT_evac"], g)
                    for j in range(G):
                        mm = pe.transpose(T[:, j * P:(j + 1) * P], xn[:, j, :], ident[:])
                    mm.then_inc(s["tr_ready"], 1)
                    pe.wait_ge(s["xnT_ready"], g + 1)

                def project(g, u, i):
                    if i == 1:
                        pe.wait_ge(s[f"ctx_in{u}"], (g - u) * 8 + 16)
                    dst, src = ((Q, xnT), (K, ctxT[u]), (V, ctxT[u]))[i]
                    for j in range(G):
                        mm = pe.matmul(dst[:, j * P:(j + 1) * P], src[:, j * P:(j + 1) * P], w[:, i, :],
                                       start=True, stop=True)
                    mm.then_inc(s["proj_ready"], 1)

                def regroup(g, j):
                    pe.wait_ge(s["swap_a"], G * g + j + 1)
                    pe.wait_ge(s["swap_v"], G * g + j + 1)
                    pe.nop(nofuse=True)
                    for k in range(DH):
                        mm = pe.transpose(T[:, j * P + k * H:j * P + (k + 1) * H], swap[0:H, j % 2, k, :],
                                          ident[0:H, 0:H])
                    if j == G - 1:
                        mm.then_inc(s["attT_ready"], 1)

                def attend(g, u, last):
                    pe.wait_ge(s["q_final"], g + 1)
                    for j in range(G):
                        mm = pe.transpose(T[:, j * P:(j + 1) * P], proj[u][0][:, j, :], ident[:])
                    mm.then_inc(s["qT_ready"], 1)
                    pe.wait_ge(s["kv_final"], g + 1)
                    pe.wait_ge(s["v_scaled"], g + 1)
                    for j in range(G):
                        mm = pe.matmul((KV0, KV1)[j // 2][:, (j % 2) * KW:(j % 2 + 1) * KW], proj[u][1][:, j, :],
                                       v_wide[u][:, j, :], start=True, stop=True)
                    mm.then_inc(s["kv_ready"], 1)
                    if not last:
                        project(g + 1, 1 - u, 0)
                        project(g + 1, 1 - u, 1)
                    pe.wait_ge(s["qT_evac"], g + 2)
                    pe.wait_ge(s["kv_masked"], g + 1)
                    for j in range(G):
                        mm = pe.matmul((A0, A1)[j // 2][:, (j % 2) * KW:(j % 2 + 1) * KW], qT[:, j * P:(j + 1) * P],
                                       kvx[:, j, :], start=True, stop=True)
                    mm.then_inc(s["att_ready"], 1)
                    if not last:
                        project(g + 1, 1 - u, 2)
                    pe.wait_ge(s["att_normed"], g + 1)
                    for j in range(G):
                        if j >= 2:
                            pe.wait_ge(s["swap_a"], G * g + j - 1)
                            pe.wait_ge(s["swap_v"], G * g + j - 1)
                        for e in range(DH):
                            mm = pe.transpose(swap_bank[j % 2][e // 4][0:H, (e % 4) * P:(e % 4 + 1) * P],
                                              att[:, j, :].rearrange("p (h e) -> p h e", h=H)[:, :, e], ident[:])
                        mm.then_inc(s["swap_ready"], 1)
                        if j >= 1:
                            regroup(g, j - 1)
                    regroup(g, G - 1)
                    pe.wait_ge(s["attT_evac"], g + 2)
                    for j in range(G):
                        mm = pe.matmul(KV1[:, j * P:(j + 1) * P], attT[:, j * P:(j + 1) * P], w[:, 3, :],
                                       start=True, stop=True)
                    mm.then_inc(s["y_ready"], 1)

                pe.wait_ge(ww_in, 16 * 8)
                turn(0, first=True)
                for i in range(3):
                    project(0, 0, i)

                def group(g, u, last):
                    if not last:
                        turn(g + 1)
                    attend(g, u, last)
                loop(pe, group)
                barrier(pe, phase)

            def scalar(act):
                def copy_xnT(g):
                    act.wait_ge(s["tr_ready"], g + 1)
                    act.activation(xnT, T[:], ACT.Copy).then_inc(s["xnT_ready"], 1)

                def normed(g, u):
                    act.wait_ge(s["rs_ready"], g + 1)
                    for i, src in enumerate((Q, K, V)):
                        for j in range(G):
                            c = i * G + j
                            mm = act.activation(proj[u][i][:, j, :], src[:, j * P:(j + 1) * P], ACT.Identity,
                                                bias=nm[:, c:c + 1], scale=rs[:, c:c + 1])
                        mm.then_inc(s["normed_ready"], 1)

                copy_xnT(0)
                normed(0, 0)

                def group(g, u, last):
                    if not last:
                        copy_xnT(g + 1)
                    act.wait_ge(s["qT_ready"], g + 1)
                    act.activation(qT, T[:], ACT.Copy).then_inc(s["qT_evac"], 1)
                    for j in range(G):
                        act.wait_ge(s["swap_ready"], G * g + j + 1)
                        act.activation(swapped(j, 0), swap_bank[j % 2][0][0:H, :].rearrange("p (e n) -> p e n", e=4),
                                       ACT.Copy).then_inc(s["swap_a"], 1)
                    act.wait_ge(s["attT_ready"], g + 1)
                    act.activation(attT.rearrange("p (j h k) -> p j k h", j=G, h=H),
                                   T[:].rearrange("p (j k h) -> p j k h", j=G, h=H), ACT.Copy
                                   ).then_inc(s["attT_evac"], 1)
                    if not last:
                        normed(g + 1, 1 - u)
                loop(act, group)
                barrier(act, phase)

            def vector(dve):
                def normed(g):
                    for j in range(G):
                        mm = dve.tensor_scalar(xn[:, j, :], x[:, ds(g * G + j, 1), :], mean[:, ds(g * G + j, 1)],
                                               rstd[:, ds(g * G + j, 1)], ALU.subtract, ALU.mult)
                    mm.then_inc(s["xn_ready"], 1)

                def moments(g, i):
                    dve.wait_ge(s["proj_ready"], 3 * g + i + 1)
                    for j in range(G):
                        dve.bn_stats(bn[:, i * G + j, :], (Q, K, V)[i][:, j * P:(j + 1) * P])

                def variances():
                    dve.drain()
                    for c in range(3 * G):
                        dve.bn_aggr(agg[:, c, :], bn[:, c, :])
                    dve.drain()
                    dve.tensor_scalar(ve, agg[:, :, 1], EPS_1, None, ALU.add).then_inc(s["var_ready"], 1)

                def finish(g, u):
                    gamma, beta = bc(gb[:, 0, :]), bc(gb[:, 1, :])
                    for i in range(2):
                        dve.wait_ge(s["normed_ready"], 3 * g + i + 1)
                        dve.tensor_tensor(proj[u][i], proj[u][i], gamma, ALU.mult)
                        dve.drain()
                        dve.tensor_tensor(proj[u][i], proj[u][i], beta, ALU.add)
                        dve.drain()
                        mm = dve.tensor_scalar(proj[u][i], proj[u][i], 0.0, EPS_K, ALU.max, ALU.add)
                        if i == 0:
                            mm.then_inc(s["q_final"], 1)
                    dve.drain()
                    for j in range(G):
                        mm = dve.tensor_scalar(proj[u][1][:, j, :], proj[u][1][:, j, :], em[:, ds(g * G + j, 1)], None, ALU.mult)
                    mm.then_inc(s["kv_final"], 1)

                for u in range(2):
                    dve.memset(v_wide[u], 1.0)
                dve.drain().then_inc(s["x_done"], 1)
                for n in ("attT_evac", "qT_evac"):
                    dve.drain().then_inc(s[n], 1)
                normed(0)
                for i in range(3):
                    moments(0, i)
                variances()

                def group(g, u, last):
                    if not last:
                        normed(g + 1)
                    finish(g, u)
                    dve.wait_ge(s["kv_ready"], g + 1)
                    for k, src in enumerate((KV0, KV1)):
                        mm = dve.tensor_tensor(kvx[:, 2 * k:2 * k + 2, :],
                                               src[:, 0:2 * KW].rearrange("p (a k) -> p a k", a=2),
                                               block_mask.unsqueeze(1).broadcast_to([P, 2, KW]), ALU.mult)
                    mm.then_inc(s["kv_masked"], 1)
                    if not last:
                        moments(g + 1, 0)
                        moments(g + 1, 1)
                    dve.wait_ge(s["att_ready"], g + 1)
                    views = [src[:, 0:2 * KW].rearrange("p (a k) -> p a k", a=2) for src in (A0, A1)]
                    for k, v in enumerate(views):
                        dve.tensor_scalar(den[:, 2 * k:2 * k + 2, :], v[:, :, P:KW], EPS_K, None, ALU.add)
                    dve.drain()
                    dve.reciprocal(den, den)
                    dve.drain()
                    for k, v in enumerate(views):
                        for a in range(2):
                            j = 2 * k + a
                            mm = dve.tensor_tensor(att[:, j, :].rearrange("p (h e) -> p h e", h=H),
                                                   v[:, a, 0:P].rearrange("p (h e) -> p h e", h=H),
                                                   den[:, j, :].unsqueeze(2).broadcast_to([P, H, DH]), ALU.mult)
                    mm.then_inc(s["att_normed"], 1)
                    if not last:
                        moments(g + 1, 2)
                        variances()
                    for j in range(G):
                        dve.wait_ge(s["swap_ready"], G * g + j + 1)
                        dve.tensor_copy(swapped(j, 1), swap_bank[j % 2][1][0:H, :].rearrange("p (e n) -> p e n", e=4)
                                        ).then_inc(s["swap_v"], 1)
                    dve.wait_ge(s["y_ready"], g + 1)
                    dve.tensor_tensor(y, KV1[:].rearrange("p (a k) -> p a k", a=G), bc(gb[:, 2, :]), ALU.add)
                    dve.drain()
                    for j in range(G):
                        dve.bn_stats(bny[:, j, :], y[:, j, :])
                    dve.drain()
                    for j in range(G):
                        dve.bn_aggr(aggy[:, j, :], bny[:, j, :])
                    dve.drain()
                    dve.tensor_scalar(vey, aggy[:, :, 1], EPS_1, None, ALU.add).then_inc(s["yvar_ready"], 1)
                    dve.wait_ge(s["yrs_ready"], g + 1)
                    for j in range(G):
                        dve.tensor_scalar(y[:, j, :], y[:, j, :], aggy[:, j, 0:1], rsy[:, j:j + 1],
                                          ALU.subtract, ALU.mult)
                    dve.drain()
                    dve.tensor_tensor(y, y, bc(gb[:, 0, :]), ALU.mult)
                    dve.drain()
                    dve.tensor_tensor(y, y, bc(gb[:, 1, :]), ALU.add)
                    dve.drain()
                    here = x[:, ds(g * G, G), :]
                    dve.tensor_tensor(here, here, y, ALU.add)
                    dve.drain()
                    stats_of(dve, g * G, bnx, aggx).then_inc(s["stats_ready"], 1)
                loop(dve, group)
                barrier(dve, phase)

            def gpsimd(pool):
                pool.memset(half, -0.5)
                for view, n, wide in ((block_mask[:, 0:P], H, DH), (block_mask[:, P:KW], H, 1)):
                    pool.memset(view, 1.0)
                    pool.drain()
                    v3 = view.rearrange("p (h e) -> p h e", e=wide)
                    pool.affine_select(out=v3, in_=v3, compare_op=ALU.is_ge, fill=0.0, base=0,
                                       pattern=[[-DH, n], [0, wide]], channel_multiplier=1)
                    pool.drain()
                    pool.affine_select(out=v3, in_=v3, compare_op=ALU.is_ge, fill=0.0, base=DH - 1,
                                       pattern=[[DH, n], [0, wide]], channel_multiplier=-1)
                pool.wait_ge(s["x_done"], 1)
                pool.wait_ge(ww_in, 16 * 8)

                def scales(g):
                    pool.wait_ge(s["var_ready"], g + 1)
                    pool.tensor_tensor(rs, ve, half, ALU.pow)
                    pool.drain()
                    pool.tensor_tensor(nm, agg[:, :, 0], rs, ALU.mult)
                    pool.drain()
                    pool.tensor_scalar(nm, nm, -1.0, None, ALU.mult).then_inc(s["rs_ready"], 1)

                def group(g, u, last):
                    pool.wait_ge(s["normed_ready"], 3 * g + 3)
                    v = proj[u][2]
                    pool.tensor_tensor(v, v, bc(gb[:, 0, :]), ALU.mult)
                    pool.drain()
                    pool.tensor_tensor(v, v, bc(gb[:, 1, :]), ALU.add)
                    pool.drain()
                    pool.tensor_tensor(v_wide[u][:, :, 0:P], v,
                                       em[:, ds(g * G, G)].unsqueeze(2).broadcast_to([P, G, P]),
                                       ALU.mult).then_inc(s["v_scaled"], 1)
                    if not last:
                        scales(g + 1)
                    pool.wait_ge(s["yvar_ready"], g + 1)
                    pool.tensor_tensor(rsy, vey, neg_half[:], ALU.pow).then_inc(s["yrs_ready"], 1)
                    pool.wait_ge(s["stats_ready"], g + 1)
                    rstd_of(pool, g * G)
                scales(0)
                loop(pool, group)
                clear_twins(pool)
                barrier(pool, phase)

            return sync, tensor, scalar, vector, gpsimd

        def expert_choice(phase):
            s = {n: sem(f"{n}_f1") for n in (
                "xn_ready", "tr_ready", "xnT_ready", "logits_ready", "shifted_ready", "exp_ready", "gates_ready",
                "gT_ready", "sel_ready", "selT_ready", "selT_copied", "pos_ready",
                "xg_ready", "oh_ready", "pg_ready", "ga_ready", "ga_evac", "pt_ready", "pt_evac", "h_ready",
                "h_evac", "w2_ready", "o2_evac", "y_ready", "x_done", "stats_ready")}
            K, F = 64, 512
            FB = F // P
            arena.restart()
            xn = [arena.take([G, P]) for _ in range(2)]
            xnT = [arena.take([W]) for _ in range(2)]
            lg = arena.take([B, E])
            gate_of = arena.take([B, E])
            top, total = arena.take([B]), arena.take([B])
            work = arena.take([2, P])
            best = arena.take([2, E])
            sel, selT = arena.take([2, P]), arena.take([2, P])
            slot = arena.take([B, E])
            iota = arena.take([K])
            upper = arena.take([P])
            onehot = [arena.take([E, K]) for _ in range(2)]
            weighted = [arena.take([E, K]) for _ in range(2)]
            weightedT = [arena.take([G, E // 2, P]) for _ in range(2)]
            exT = [arena.take([E, G * K]) for _ in range(2)]
            h1T = [arena.take([FB, G * K]) for _ in range(2)]
            out2 = arena.take([E // 2, G, P])
            b1c = arena.take([E, FB])
            b2p = arena.take([E // 2, P])
            bn, agg = arena.take([G, 6]), arena.take([G, 2])
            w1 = wide[:, 0:E * F].rearrange("p (e f) -> p e f", e=E)
            w2 = wide[:, E * F:2 * E * F].rearrange("p (e b m) -> p e b m", e=E, b=FB)

            def sync(sp):
                sp.dma_start(b1c, t["b1_1"]).then_inc(fw_in[1], 16)
                for e in range(E):
                    row = t["b2_1"][e].rearrange("(a n) -> a n", a=1)
                    sp.dma_start(b2p[K * (e % 2):K * (e % 2) + K, e // 2, :], row.broadcast_to([K, P])).then_inc(fw_in[1], 16)
                barrier(sp, phase)

            def tensor(pe):
                def turn(g, u):
                    pe.wait_ge(s["xn_ready"], g + 1)
                    for j in range(G):
                        mm = pe.transpose(bank[u][:, j * P:(j + 1) * P], xn[u][:, j, :], ident[:])
                    mm.then_inc(s["tr_ready"], 1)

                def prep(g, u, j, first=False):
                    pe.wait_ge(s["oh_ready"], G * g + j + 1)
                    if j == 0:
                        if not first:
                            pe.wait_ge(s["x_done"], g)
                    if not (first and j == 0):
                        pe.wait_ge(s["ga_evac"], G * g + j)
                    pe.matmul(bank[0][:], xn[u][:, j, :], onehot[j % 2].rearrange("p e k -> p (e k)"),
                              start=True, stop=True).then_inc(s["ga_ready"], 1)
                    pe.wait_ge(s["pg_ready"], G * g + j + 1)
                    if not (first and j == 0):
                        pe.wait_ge(s["pt_evac"], G * g + j)
                    for k in range(E // 2):
                        mm = pe.transpose(bank[1][:, k * P:(k + 1) * P],
                                          weighted[j % 2][:, 2 * k:2 * k + 2, :].rearrange("p e k -> p (e k)"), ident[:])
                    mm.then_inc(s["pt_ready"], 1)

                pe.wait_ge(fw_in[1], 16 * fw_loads[1])
                turn(0, 0)

                def logits(g, u, last):
                    if not last:
                        turn(g + 1, 1 - u)
                    pe.wait_ge(s["xnT_ready"], g + 1)
                    for j in range(G):
                        mm = pe.matmul(bank[2 + u][:, j * E:(j + 1) * E], xnT[u][:, j * P:(j + 1) * P], gates[1][:],
                                       start=True, stop=True)
                    mm.then_inc(s["logits_ready"], 1)
                loop(pe, logits)
                pe.wait_ge(s["gates_ready"], 1)
                for k in range(2):
                    mm = pe.transpose(bank[4][:, k * P:(k + 1) * P],
                                      gate_of[:, 16 * k:16 * k + 16, :].rearrange("p b e -> p (b e)"), ident[:])
                mm.then_inc(s["gT_ready"], 1)
                pe.wait_ge(s["sel_ready"], 1)
                for k in range(2):
                    mm = pe.transpose(bank[5][:, k * P:(k + 1) * P], sel[:, k, :], ident[:])
                mm.then_inc(s["selT_ready"], 1)
                pe.wait_ge(s["selT_copied"], 1)
                pe.matmul(bank[6][:, 0:2 * P], upper, selT.rearrange("p a k -> p (a k)"),
                          start=True, stop=True).then_inc(s["pos_ready"], 1)
                for j in range(G):
                    prep(0, 0, j, first=True)

                def second(g, e):
                    n = (E * g + e) * FB
                    pe.wait_ge(s["h_evac"], n + 2 * FB)
                    pair = (E // 2) * g + e // 2
                    if e % 2 == 0:
                        pe.wait_ge(s["o2_evac"], pair + 1)
                    rows = slice(K * (e % 2), K * (e % 2) + K)
                    for j in range(G):
                        for f in range(FB):
                            mm = pe.matmul(bank[6 + (e // 2) % 2][rows, j * P:(j + 1) * P],
                                           h1T[e % 2][:, f, j * K:(j + 1) * K], w2[:, e, f, :],
                                           start=(f == 0), stop=(f == FB - 1), skip_group_check=True)
                    if e % 2:
                        mm.then_inc(s["w2_ready"], 1)

                def group(g, u, last):
                    pe.wait_ge(s["ga_evac"], G * g + G)
                    for e in range(E):
                        for f in range(FB):
                            pe.wait_ge(s["h_evac"], (E * g + e) * FB + f + 1)
                            pe.matmul(bank[2 + f][:, 0:G * K], w1[:, e, f * P:(f + 1) * P], exT[u][:, e, :],
                                      start=True, stop=True).then_inc(s["h_ready"], 1)
                        if e:
                            second(g, e - 1)
                        if e in (2, 4, 5, 6) and not last:
                            prep(g + 1, 1 - u, (2, 4, 5, 6).index(e))
                    second(g, E - 1)
                    pe.wait_ge(s["o2_evac"], (E // 2) * g + E // 2 + 2)
                    pe.wait_ge(s["ga_evac"], G * g + (G if last else 2 * G))
                    pe.wait_ge(s["pt_evac"], G * g + G)
                    for j in range(G):
                        for k in range(E // 2):
                            mm = pe.matmul(bank[0][:, j * P:(j + 1) * P], weightedT[u][:, j, k, :], out2[:, k, j, :],
                                           start=(k == 0), stop=(k == E // 2 - 1), skip_group_check=True)
                    mm.then_inc(s["y_ready"], 1)
                loop(pe, group)
                barrier(pe, phase)

            def scalar(act):
                def turned(g, u, last):
                    act.wait_ge(s["tr_ready"], g + 1)
                    act.activation(xnT[u], bank[u][:], ACT.Copy).then_inc(s["xnT_ready"], 1)
                loop(act, turned)
                act.wait_ge(s["shifted_ready"], 1)
                act.activation(gate_of.rearrange("p b e -> p (b e)"), lg.rearrange("p b e -> p (b e)"),
                               ACT.Exp).then_inc(s["exp_ready"], 1)

                def prep(g, u, j):
                    act.wait_ge(s["ga_ready"], G * g + j + 1)
                    act.activation(exT[u][:, :, j * K:(j + 1) * K], bank[0][:].rearrange("p (e k) -> p e k", e=E),
                                   ACT.Copy).then_inc(s["ga_evac"], 1)
                    act.wait_ge(s["pt_ready"], G * g + j + 1)
                    act.activation(weightedT[u][:, j, :, :].rearrange("p e k -> p (e k)"), bank[1][:],
                                   ACT.Copy).then_inc(s["pt_evac"], 1)
                for j in range(G):
                    prep(0, 0, j)
                act.drain().then_inc(s["h_evac"], FB)

                def group(g, u, last):
                    for e in range(E):
                        for f in range(FB):
                            n = (E * g + e) * FB + f
                            act.wait_ge(s["h_ready"], n + 1)
                            act.activation(h1T[e % 2][:, f, :], bank[2 + f][:, 0:G * K], ACT.Gelu_apprx_tanh,
                                           bias=b1c[:, e, f:f + 1]).then_inc(s["h_evac"], 1)
                        if e in (2, 4, 5, 6) and not last:
                            prep(g + 1, 1 - u, (2, 4, 5, 6).index(e))
                loop(act, group)
                barrier(act, phase)

            def vector(dve):
                def normed(g, u, done):
                    for j in range(G):
                        mm = dve.tensor_scalar(xn[u][:, j, :], x[:, ds(g * G + j, 1), :], mean[:, ds(g * G + j, 1)],
                                               rstd[:, ds(g * G + j, 1)], ALU.subtract, ALU.mult)
                    mm.then_inc(done, 1)

                normed(0, 0, s["xn_ready"])

                def logits(g, u, last):
                    if not last:
                        normed(g + 1, 1 - u, s["xn_ready"])
                    dve.wait_ge(s["logits_ready"], g + 1)
                    dve.tensor_copy(lg[:, ds(g * G, G), :], bank[2 + u][:, 0:G * E].rearrange("p (b e) -> p b e", b=G))
                    dve.drain()
                loop(dve, logits)

                def bc(col):
                    return col.unsqueeze(2).broadcast_to([P, B, E])
                dve.tensor_reduce(top, lg, AX.X, ALU.max)
                dve.drain()
                dve.tensor_tensor(lg, lg, bc(top), ALU.subtract).then_inc(s["shifted_ready"], 1)
                dve.wait_ge(s["exp_ready"], 1)
                dve.tensor_reduce(total, gate_of, AX.X, ALU.add)
                dve.drain()
                dve.reciprocal(total, total)
                dve.drain()
                dve.tensor_tensor(gate_of, gate_of, bc(total), ALU.mult).then_inc(s["gates_ready"], 1)
                dve.wait_ge(s["gT_ready"], 1)
                dve.tensor_copy(work.rearrange("p a k -> p (a k)"), bank[4][:, 0:2 * P])
                dve.drain()
                for _ in range(K // 8):
                    for k in range(2):
                        dve.max(best[:, k, :], work[:, k, :])
                    dve.drain()
                    for k in range(2):
                        dve.match_replace(work[:, k, :], best[:, k, :], work[:, k, :], -1.0)
                    dve.drain()
                dve.tensor_scalar(sel, work, 0.0, None, ALU.is_lt).then_inc(s["sel_ready"], 1)
                dve.wait_ge(s["selT_ready"], 1)
                dve.tensor_copy(selT.rearrange("p a k -> p (a k)"), bank[5][:, 0:2 * P]).then_inc(s["selT_copied"], 1)
                dve.wait_ge(s["pos_ready"], 1)
                flat = slot.rearrange("p b e -> p (b e)")
                dve.tensor_tensor(flat, bank[6][:, 0:2 * P], selT.rearrange("p a k -> p (a k)"), ALU.mult)
                dve.drain()
                dve.tensor_scalar(flat, flat, -1.0, None, ALU.add)
                dve.drain()
                dve.drain().then_inc(s["o2_evac"], 2)
                dve.drain().then_inc(s["x_done"], 1)

                def one_hot(g, u, j, first=False):
                    if not (first and j < 2):
                        dve.wait_ge(s["ga_ready"], G * g + j - 1)
                        dve.wait_ge(s["pg_ready"], G * g + j - 1)
                    dve.tensor_tensor(onehot[j % 2], iota.unsqueeze(1).broadcast_to([P, E, K]),
                                      slot[:, ds(g * G + j, 1), :].rearrange("p a e -> p (a e)").unsqueeze(2)
                                      .broadcast_to([P, E, K]), ALU.is_equal).then_inc(s["oh_ready"], 1)

                normed(0, 0, s["xg_ready"])
                dve.drain()
                for j in range(G):
                    one_hot(0, 0, j, first=True)

                def group(g, u, last):
                    if not last:
                        normed(g + 1, 1 - u, s["xg_ready"])
                        dve.drain()
                        one_hot(g + 1, 1 - u, 0)
                        one_hot(g + 1, 1 - u, 1)
                    for k in range(E // 2):
                        dve.wait_ge(s["w2_ready"], (E // 2) * g + k + 1)
                        dve.tensor_tensor(out2[:, k, :, :], bank[6 + k % 2][:].rearrange("p (a m) -> p a m", a=G),
                                          b2p[:, k, :].unsqueeze(1).broadcast_to([P, G, P]),
                                          ALU.add).then_inc(s["o2_evac"], 1)
                        if k == 1 and not last:
                            one_hot(g + 1, 1 - u, 2)
                        if k == 2 and not last:
                            one_hot(g + 1, 1 - u, 3)
                    dve.wait_ge(s["y_ready"], g + 1)
                    here = x[:, ds(g * G, G), :]
                    dve.tensor_tensor(here, here, bank[0][:].rearrange("p (a m) -> p a m", a=G), ALU.add
                                      ).then_inc(s["x_done"], 1)
                    dve.drain()
                    stats_of(dve, g * G, bn, agg).then_inc(s["stats_ready"], 1)
                loop(dve, group)
                barrier(dve, phase)

            def gpsimd(pool):
                pool.iota(iota_i, pattern=[[1, K]], base=0, channel_multiplier=0)
                pool.memset(upper, 1.0)
                pool.drain()
                pool.tensor_copy(iota, iota_i)
                pool.affine_select(out=upper, in_=upper, compare_op=ALU.is_ge, fill=0.0, base=0,
                                   pattern=[[1, P]], channel_multiplier=-1)
                pool.drain().then_inc(fw_in[1], 16)

                def weigh(g, j, first=False):
                    pool.wait_ge(s["oh_ready"], G * g + j + 1)
                    if not (first and j < 2):
                        pool.wait_ge(s["pt_ready"], G * g + j - 1)
                    pool.tensor_tensor(weighted[j % 2], onehot[j % 2],
                                       gate_of[:, ds(g * G + j, 1), :].rearrange("p a e -> p (a e)").unsqueeze(2)
                                       .broadcast_to([P, E, K]), ALU.mult).then_inc(s["pg_ready"], 1)
                for j in range(G):
                    weigh(0, j, first=True)

                def group(g, u, last):
                    if not last:
                        for j in range(G):
                            weigh(g + 1, j)
                    pool.wait_ge(s["stats_ready"], g + 1)
                    rstd_of(pool, g * G)
                loop(pool, group)
                barrier(pool, phase)

            return sync, tensor, scalar, vector, gpsimd

        def gated_experts(phase):
            s = {n: sem(f"{n}_f2") for n in (
                "xn_ready", "tr_ready", "xnT_ready", "sq_ready", "c_squared", "c2_ready", "c2_copied",
                "logits_ready", "d2_ready", "dist_ready", "shifted_ready", "exp_ready", "weights_ready",
                "wT_ready", "wT_copied", "b2_ready", "acc_ready", "gu_ready", "sg_ready",
                "hid_free", "y_ready", "y_free", "stats_ready")}
            F = 342
            FB, FR = 3, F // 3
            arena.restart()
            xn = [arena.take([G, P]) for _ in range(2)]
            xnT = [arena.take([W]) for _ in range(2)]
            sq, sq_sum = arena.take([P]), arena.take([2, G])
            cT2, c2 = arena.take([E]), arena.take([E])
            ones = arena.take([P])
            dist = arena.take([G, E])
            z, ez = arena.take([G, E]), arena.take([G, E])
            cmp, cmp2 = arena.take([G, E, E]), arena.take([G, E, E])
            sel, top, total = arena.take([G, E]), arena.take([G]), arena.take([G])
            half = arena.take([G, E])
            weight = [arena.take([G, E]) for _ in range(2)]
            wT = arena.take([W])
            b2 = arena.take([P])
            bgc, b1c = arena.take([E, FB]), arena.take([E, FB])
            sg = arena.take([2, W])
            hid = [arena.take([FB, W]) for _ in range(2)]
            acc = [arena.take([G, P]) for _ in range(2)]
            bn, agg = arena.take([G, 6]), arena.take([G, 2])
            wg = wide[:, 0:E * F].rearrange("p (e f) -> p e f", e=E)
            w1 = wide[:, E * F:2 * E * F].rearrange("p (e f) -> p e f", e=E)
            w2 = wide[:, 2 * E * F:2 * E * F + E * FB * P].rearrange("p (e b m) -> p e b m", e=E, b=FB)
            KB = E * FB

            def sync(sp):
                sp.dma_start(bgc[0:FR], t["bg_2"]).then_inc(fw_in[2], 16)
                sp.dma_start(b1c[0:FR], t["b1_2"]).then_inc(fw_in[2], 16)
                sp.dma_start(b2[0:E], t["b2_2"]).then_inc(fw_in[2], 16)
                barrier(sp, phase)

            def tensor(pe):
                def front_a(g, u, first=False):
                    pe.wait_ge(s["xn_ready"], g + 1)
                    if not first:
                        pe.wait_ge(s["wT_copied"], g)
                        pe.wait_ge(s["acc_ready"], g)
                    for j in range(G):
                        mm = pe.transpose(bank[0][:, j * P:(j + 1) * P], xn[u][:, j, :], ident[:])
                    mm.then_inc(s["tr_ready"], 1)
                    pe.wait_ge(s["xnT_ready"], g + 1)
                    for j in range(G):
                        mm = pe.matmul(bank[1][:, j * E:(j + 1) * E], xnT[u][:, j * P:(j + 1) * P], gates[2][:],
                                       start=True, stop=True)
                    mm.then_inc(s["logits_ready"], 1)

                def front_b(g, u):
                    pe.wait_ge(s["weights_ready"], g + 1)
                    for j in range(G):
                        mm = pe.transpose(bank[0][0:E, j * P:(j + 1) * P], weight[u][:, j, :], ident[:])
                    mm.then_inc(s["wT_ready"], 1)
                    pe.wait_ge(s["wT_copied"], g + 1)
                    for j in range(G):
                        mm = pe.matmul(bank[1][:, j * P:(j + 1) * P], wT[0:E, j * P:(j + 1) * P], b2[0:E, :],
                                       start=True, stop=True)
                    mm.then_inc(s["b2_ready"], 1)

                pe.wait_ge(fw_in[2], 16 * fw_loads[2])
                pe.wait_ge(s["c_squared"], 1)
                pe.matmul(bank[1][:, 0:E], ones, cT2, start=True, stop=True).then_inc(s["c2_ready"], 1)
                pe.wait_ge(s["c2_copied"], 1)
                front_a(0, 0, first=True)
                front_b(0, 0)

                def second(g, e):
                    pe.wait_ge(s["hid_free"], KB * g + FB * e + FB + 2)
                    pe.wait_ge(s["y_free"], E * g + e + 1)
                    for j in range(G):
                        for f in range(FB):
                            mm = pe.matmul(bank[6 + e % 2][:, j * P:(j + 1) * P],
                                           hid[e % 2][0:FR, f, j * P:(j + 1) * P], w2[0:FR, e, f, :],
                                           start=(f == 0), stop=(f == FB - 1), skip_group_check=True)
                    mm.then_inc(s["y_ready"], 1)

                def group(g, u, last):
                    for e in range(E):
                        for f in range(FB):
                            k = FB * e + f
                            pe.wait_ge(s["hid_free"], KB * g + k + 1)
                            cols = slice(f * FR, (f + 1) * FR)
                            pe.matmul(bank[2 + k % 2][0:FR, :], wg[:, e, cols], xnT[u], start=True, stop=True)
                            pe.matmul(bank[4 + k % 2][0:FR, :], w1[:, e, cols], xnT[u], start=True, stop=True
                                      ).then_inc(s["gu_ready"], 1)
                        if e:
                            second(g, e - 1)
                        if e == 2 and not last:
                            front_a(g + 1, 1 - u)
                        if e == 6 and not last:
                            front_b(g + 1, 1 - u)
                    second(g, E - 1)
                loop(pe, group)
                barrier(pe, phase)

            def scalar(act):
                def front_a(g, u):
                    for j in range(G):
                        if j == 0:
                            act.wait_ge(s["xn_ready"], g + 1)
                        act.activation(sq, xn[u][:, j, :], ACT.Square, accum_out=sq_sum[:, u, j:j + 1])
                        act.drain()
                    act.drain().then_inc(s["sq_ready"], 1)
                    act.wait_ge(s["tr_ready"], g + 1)
                    act.activation(xnT[u], bank[0][:], ACT.Copy).then_inc(s["xnT_ready"], 1)

                def front_e(g, u):
                    act.wait_ge(s["shifted_ready"], g + 1)
                    act.activation(ez, z, ACT.Exp).then_inc(s["exp_ready"], 1)

                def front_b(g, u):
                    act.wait_ge(s["wT_ready"], g + 1)
                    act.activation(wT[0:E, :], bank[0][0:E, :], ACT.Copy).then_inc(s["wT_copied"], 1)

                act.wait_ge(fw_in[2], 16 * fw_loads[2])
                act.activation(cT2, gates[2][:], ACT.Square).then_inc(s["c_squared"], 1)
                act.wait_ge(s["c2_ready"], 1)
                act.activation(c2, bank[1][:, 0:E], ACT.Copy).then_inc(s["c2_copied"], 1)
                front_a(0, 0)
                front_e(0, 0)
                front_b(0, 0)

                def group(g, u, last):
                    for e in range(E):
                        for f in range(FB):
                            k = FB * e + f
                            act.wait_ge(s["gu_ready"], KB * g + k + 1)
                            act.activation(sg[0:FR, k % 2, :], bank[2 + k % 2][0:FR, :], ACT.Silu,
                                           bias=bgc[0:FR, e, f:f + 1]).then_inc(s["sg_ready"], 1)
                        if not last:
                            if e == 2:
                                front_a(g + 1, 1 - u)
                            if e == 4:
                                front_e(g + 1, 1 - u)
                            if e == 6:
                                front_b(g + 1, 1 - u)
                loop(act, group)
                barrier(act, phase)

            def vector(dve):
                def normed(g, u):
                    for j in range(G):
                        mm = dve.tensor_scalar(xn[u][:, j, :], x[:, ds(g * G + j, 1), :], mean[:, ds(g * G + j, 1)],
                                               rstd[:, ds(g * G + j, 1)], ALU.subtract, ALU.mult)
                    mm.then_inc(s["xn_ready"], 1)

                def wide_bc(col):
                    return col.unsqueeze(2).broadcast_to([P, G, E])

                def distances(g, u):
                    dve.wait_ge(s["logits_ready"], g + 1)
                    dve.wait_ge(s["sq_ready"], g + 1)
                    dve.scalar_tensor_tensor(out=dist, in0=bank[1][:, 0:G * E].rearrange("p (g e) -> p g e", g=G),
                                             scalar=-2.0, in1=c2.unsqueeze(1).broadcast_to([P, G, E]),
                                             op0=ALU.mult, op1=ALU.add)
                    dve.drain()
                    dve.tensor_tensor(dist, dist, wide_bc(sq_sum[:, u, :]), ALU.add)
                    dve.drain()
                    dve.tensor_scalar(dist, dist, 1e-12, None, ALU.max).then_inc(s["d2_ready"], 1)

                def weights_a(g):
                    dve.wait_ge(s["dist_ready"], g + 1)
                    dve.tensor_reduce(top, dist, AX.X, ALU.max)
                    dve.drain()
                    dve.tensor_tensor(z, dist, wide_bc(top), ALU.subtract).then_inc(s["shifted_ready"], 1)
                    rank_below(dve, dist, cmp, cmp2, sel, 2)

                def weights_b(g, u):
                    dve.wait_ge(s["exp_ready"], g + 1)
                    dve.tensor_tensor(ez, ez, sel, ALU.mult)
                    dve.drain()
                    dve.tensor_reduce(total, ez, AX.X, ALU.add)
                    dve.drain()
                    dve.reciprocal(total, total)
                    dve.drain()
                    dve.tensor_tensor(weight[u], ez, wide_bc(total), ALU.mult).then_inc(s["weights_ready"], 1)

                def start_acc(g, u):
                    dve.wait_ge(s["b2_ready"], g + 1)
                    dve.tensor_tensor(acc[u], bank[1][:].rearrange("p (a m) -> p a m", a=G), x[:, ds(g * G, G), :],
                                      ALU.add).then_inc(s["acc_ready"], 1)

                dve.drain().then_inc(s["hid_free"], 2)
                dve.drain().then_inc(s["y_free"], 2)
                normed(0, 0)
                distances(0, 0)
                weights_a(0)
                weights_b(0, 0)
                start_acc(0, 0)

                def add_expert(g, u, e):
                    dve.drain()
                    dve.wait_ge(s["y_ready"], E * g + e + 1)
                    for j in range(G):
                        here = acc[u][:, j, :]
                        if e == E - 1:
                            dst = x[:, ds(g * G + j, 1), :].rearrange("p a m -> p (a m)")
                        else:
                            dst = here
                        mm = dve.scalar_tensor_tensor(out=dst, in0=bank[6 + e % 2][:, j * P:(j + 1) * P],
                                                      scalar=weight[u][:, j, e:e + 1], in1=here,
                                                      op0=ALU.mult, op1=ALU.add)
                    mm.then_inc(s["y_free"], 1)

                def group(g, u, last):
                    if not last:
                        normed(g + 1, 1 - u)
                    for e in range(E):
                        for f in range(FB):
                            k = FB * e + f
                            dve.wait_ge(s["sg_ready"], KB * g + k + 1)
                            dve.scalar_tensor_tensor(out=hid[e % 2][0:FR, f, :], in0=bank[4 + k % 2][0:FR, :],
                                                     scalar=b1c[0:FR, e, f:f + 1], in1=sg[0:FR, k % 2, :],
                                                     op0=ALU.add, op1=ALU.mult).then_inc(s["hid_free"], 1)
                        if e:
                            add_expert(g, u, e - 1)
                        if not last:
                            if e == 3:
                                distances(g + 1, 1 - u)
                            if e == 4:
                                weights_a(g + 1)
                            if e == 5:
                                weights_b(g + 1, 1 - u)
                            if e == 7:
                                start_acc(g + 1, 1 - u)
                    add_expert(g, u, E - 1)
                    dve.drain()
                    stats_of(dve, g * G, bn, agg).then_inc(s["stats_ready"], 1)
                loop(dve, group)
                barrier(dve, phase)

            def gpsimd(pool):
                pool.memset(ones, 1.0)
                pool.memset(half, 0.5)
                pool.drain().then_inc(fw_in[2], 16)

                def root(g):
                    pool.wait_ge(s["d2_ready"], g + 1)
                    pool.tensor_tensor(dist, dist, half, ALU.pow).then_inc(s["dist_ready"], 1)

                root(0)

                def group(g, u, last):
                    if not last:
                        root(g + 1)
                    pool.wait_ge(s["stats_ready"], g + 1)
                    rstd_of(pool, g * G)
                loop(pool, group)
                barrier(pool, phase)

            return sync, tensor, scalar, vector, gpsimd

        def load_wide2(sp):
            F, FR = 342, 114
            sp.dma_start(wide[:, 0:2 * E * F], t["wgu_2"]).then_inc(fw_in[2], 16)
            sp.dma_start(wide[0:FR, 2 * E * F:2 * E * F + 3 * E * P], t["w2_2"]).then_inc(fw_in[2], 16)

        def wide_heads(phase):
            s = {n: sem(f"{n}_3") for n in (
                "ctx_in0", "ctx_in1", "xn_ready", "m_ready0", "m_ready1", "m_free0", "m_free1",
                "s_ready", "max_ready", "exp_done", "norm_ready", "pt_ready", "pt_copied", "pv_ready",
                "o_copied", "xb_ready", "stats_ready", "xnT_ready", "front_a", "front_k", "front_v")}
            G3 = 2
            NG3, W3 = B // G3, G3 * P
            HB = H // 2
            SCALE = 0.125
            arena.restart()
            q_pad = [arena.take([HB, 2, W3]) for _ in range(2)]
            kT = [arena.take([HB, W3]) for _ in range(2)]
            values = [arena.take([G3, H * 64]) for _ in range(2)]
            probs = [arena.take([H, P]) for _ in range(2)]
            probsT = arena.take([H, P])
            ctxT = [arena.take([W3]) for _ in range(2)]
            xn = [arena.take([G3, P]) for _ in range(2)]
            xb = [arena.take([G3, P]) for _ in range(2)]
            xnT = arena.take([W3])
            attnT = arena.take([2, HB, P])
            minus_max, total, inv = arena.take([H]), arena.take([H]), arena.take([H])
            bn, agg = arena.take([G3, 6]), arena.take([G3, 2])
            bcol = arena.take([3, HB])
            bv = arena.take([H * 64])
            bo = arena.take([P])
            wq, wk, wv, wo = (wide[:, i * 1024:(i + 1) * 1024] for i in range(4))
            S, T, O, M = bank[0:2], bank[2:4], bank[4:6], bank[6:8]
            maskS = mask_bias[3][0]
            FRONT, USES = 14, 16
            LOADS = 4 + 2 + 1

            def count(g, k):
                return k % 2, g * (USES // 2) + (FRONT + k) // 2 + 1

            def front_count(g, k):
                if isinstance(g, int) and g == 0:
                    return k % 2, k // 2 + 1
                return count(g - 1, k if k < 10 else k + 1)

            def y_count(g, j, last):
                return count(g, j if last else (10, 15)[j])

            def m_take(pe, where):
                b, n = where
                pe.wait_ge(s[f"m_free{b}"], n)
                return M[b]

            def m_done(mm, where):
                mm.then_inc(s[f"m_ready{where[0]}"], 1)

            def m_read(eng, where):
                b, n = where
                eng.wait_ge(s[f"m_ready{b}"], n)
                return M[b]

            def m_release(mm, where):
                mm.then_inc(s[f"m_free{where[0]}"], 1)

            def sync(sp):
                for i, name in enumerate("qkvo"):
                    sp.dma_start(wide[:, i * 1024:(i + 1) * 1024], t[f"w{name}3"]).then_inc(w_in[3], 16)
                sp.dma_start(bcol[:, 0:2, :], t["bqk3"]).then_inc(w_in[3], 16)
                sp.dma_start(bv, t["bv3"].rearrange("(a n) -> a n", a=1).broadcast_to([P, H * 64])).then_inc(w_in[3], 16)
                sp.dma_start(bo, t["bo3"].rearrange("(a n) -> a n", a=1).broadcast_to([P, P])).then_inc(w_in[3], 16)
                for g in range(2):
                    sp.dma_start(ctxT[g], t["ctxT"][:, g * W3:(g + 1) * W3]).then_inc(s[f"ctx_in{g}"], 16)

                def group(g, u, last):
                    if isinstance(g, int) and g + 2 >= NG3:
                        return
                    sp.wait_ge(s["front_v"], g + 1)
                    sp.dma_start(ctxT[u], t["ctxT"][:, ds((g + 2) * W3, W3)]).then_inc(s[f"ctx_in{u}"], 16)
                loop(sp, group, NG3)
                barrier(sp, phase)

            def tensor(pe):
                def front_q(g, u):
                    pe.wait_ge(s["xn_ready"], g + 1)
                    for j in range(G3):
                        c = front_count(g, j)
                        dst = m_take(pe, c)
                        m_done(pe.transpose(dst[:, 0:P], xn[u][:, j, :], ident[:]), c)
                    pe.wait_ge(s["xnT_ready"], G3 * g + G3)
                    for k in range(4):
                        c = front_count(g, 2 + k)
                        dst = m_take(pe, c)
                        for a in range(2):
                            mm = pe.matmul(dst[:, a * W3:(a + 1) * W3], wq[:, (2 * k + a) * P:(2 * k + a + 1) * P],
                                           xnT, start=True, stop=True)
                        m_done(mm, c)

                def front_k(g, u):
                    pe.wait_ge(s[f"ctx_in{u}"], (g - u) * 8 + 16)
                    for k in range(4):
                        c = front_count(g, 6 + k)
                        dst = m_take(pe, c)
                        for a in range(2):
                            mm = pe.matmul(dst[:, a * W3:(a + 1) * W3], wk[:, (2 * k + a) * P:(2 * k + a + 1) * P],
                                           ctxT[u], start=True, stop=True)
                        m_done(mm, c)

                def front_v(g, u):
                    for j in range(G3):
                        for a in range(2):
                            c = front_count(g, 10 + 2 * j + a)
                            dst = m_take(pe, c)
                            mm = pe.matmul(dst[:], ctxT[u][:, j * P:(j + 1) * P], wv[:, a * 512:(a + 1) * 512],
                                           start=True, stop=True)
                            m_done(mm, c)

                def scores(n, u, j, c):
                    pe.wait_ge(s["exp_done"], 4 * n + c + 1)
                    pe.matmul(S[c % 2][:], identb[:], maskS[:].rearrange("p a k -> p (a k)"),
                              start=True, stop=False, skip_group_check=True)
                    for h in range(4 * c, 4 * c + 4):
                        mm = pe.matmul(S[c % 2][:, (h % 4) * P:(h % 4 + 1) * P],
                                       q_pad[u][:, h // 2, h % 2, j * P:(j + 1) * P],
                                       kT[u][:, h // 2, j * P:(j + 1) * P],
                                       start=False, stop=(h % 4 == 3), skip_group_check=True)
                    mm.then_inc(s["s_ready"], 1)

                def turn(n, b, c):
                    pe.wait_ge(s["norm_ready"], 4 * n + c + 1)
                    pe.wait_ge(s["pt_copied"], 4 * n + c + 1)
                    for h in range(4 * c, 4 * c + 4):
                        mm = pe.transpose(T[c % 2][:, (h % 4) * P:(h % 4 + 1) * P], probs[b][:, h, :], ident[:])
                    mm.then_inc(s["pt_ready"], 1)

                def attend(n, u, j, c):
                    pe.wait_ge(s["pt_copied"], 4 * n + c + 3)
                    if c % 2 == 0:
                        pe.wait_ge(s["o_copied"], 2 * n + c // 2 + 1)
                    for h in range(4 * c, 4 * c + 4):
                        mm = pe.matmul(O[c // 2][64 * (h % 2):64 * (h % 2) + 64, ((h // 2) % 4) * P:((h // 2) % 4 + 1) * P],
                                       values[u][:, j, h * 64:(h + 1) * 64], probsT[:, h, :],
                                       start=True, stop=True, skip_group_check=True)
                    if c % 2:
                        mm.then_inc(s["pv_ready"], 1)

                pe.wait_ge(w_in[3], 16 * LOADS)
                front_q(0, 0)
                front_k(0, 0)
                front_v(0, 0)
                pe.wait_ge(s["front_a"], 1)
                pe.wait_ge(s["front_k"], 1)
                for c in range(4):
                    scores(0, 0, 0, c)

                def group(g, u, last):
                    pe.wait_ge(s["front_v"], g + 1)
                    for j in range(G3):
                        n, b = g * G3 + j, j % 2
                        ahead = j == 0 or not last
                        nu, nj = (u, 1) if j == 0 else (1 - u, 0)
                        if j == 1 and not last:
                            pe.wait_ge(s["front_a"], g + 2)
                            pe.wait_ge(s["front_k"], g + 2)
                        if ahead:
                            scores(n + 1, nu, nj, 0)
                        turn(n, b, 0)
                        if ahead:
                            scores(n + 1, nu, nj, 1)
                        turn(n, b, 1)
                        attend(n, u, j, 0)
                        if j == 0 and not last:
                            front_q(g + 1, 1 - u)
                        if ahead:
                            scores(n + 1, nu, nj, 2)
                        turn(n, b, 2)
                        attend(n, u, j, 1)
                        if ahead:
                            scores(n + 1, nu, nj, 3)
                        turn(n, b, 3)
                        attend(n, u, j, 2)
                        attend(n, u, j, 3)
                        if not last:
                            (front_k, front_v)[j](g + 1, 1 - u)
                        w = y_count(g, j, last)
                        pe.wait_ge(s["o_copied"], 2 * n + 4)
                        dst = m_take(pe, w)
                        for k in range(HB):
                            mm = pe.matmul(dst[:, 0:P], attnT[:, j, k, :], wo[:, k * P:(k + 1) * P],
                                           start=(k == 0), stop=(k == HB - 1))
                        m_done(mm, w)
                loop(pe, group, NG3)
                barrier(pe, phase)

            def scalar(act):
                def front(g, u):
                    for j in range(G3):
                        w = front_count(g, j)
                        src = m_read(act, w)
                        mm = act.activation(xnT[:, j * P:(j + 1) * P], src[:, 0:P], ACT.Copy)
                        mm.then_inc(s[f"m_free{w[0]}"], 1)
                        act.drain().then_inc(s["xnT_ready"], 1)
                    for k in range(4):
                        w = front_count(g, 2 + k)
                        src = m_read(act, w)
                        for a in range(2):
                            for r in range(2):
                                rows = slice(64 * r, 64 * r + 64)
                                mm = act.activation(q_pad[u][rows, 2 * k + a, r, :], src[rows, a * W3:(a + 1) * W3],
                                                    ACT.Identity, bias=bcol[rows, 2, 2 * k + a:2 * k + a + 1], scale=SCALE)
                        m_release(mm, w)
                    act.drain().then_inc(s["front_a"], 1)

                def exps(n, b, c):
                    act.wait_ge(s["max_ready"], 4 * n + c + 1)
                    for h in range(4 * c, 4 * c + 4):
                        mm = act.activation(probs[b][:, h, :], S[c % 2][:, (h % 4) * P:(h % 4 + 1) * P], ACT.Exp,
                                            bias=minus_max[:, h:h + 1], accum_out=total[:, h:h + 1])
                    mm.then_inc(s["exp_done"], 1)

                def copy_o(n, j, k):
                    act.wait_ge(s["pv_ready"], 2 * n + k + 1)
                    act.activation(attnT[:, j, 4 * k:4 * k + 4, :].rearrange("p a q -> p (a q)"), O[k][:],
                                   ACT.Copy).then_inc(s["o_copied"], 1)

                act.wait_ge(s["stats_ready"], 1)
                front(0, 0)
                for c in range(4):
                    exps(0, 0, c)

                def group(g, u, last):
                    for j in range(G3):
                        n, nb = g * G3 + j, 1 - j % 2
                        ahead = j == 0 or not last
                        if ahead:
                            exps(n + 1, nb, 0)
                            exps(n + 1, nb, 1)
                        if j == 0 and not last:
                            front(g + 1, 1 - u)
                        if ahead:
                            exps(n + 1, nb, 2)
                        copy_o(n, j, 0)
                        if ahead:
                            exps(n + 1, nb, 3)
                        copy_o(n, j, 1)
                loop(act, group, NG3)
                barrier(act, phase)

            def vector(dve):
                def normed(g, u):
                    for j in range(G3):
                        mm = dve.tensor_scalar(xn[u][:, j, :], x[:, ds(g * G3 + j, 1), :], mean[:, ds(g * G3 + j, 1)],
                                               rstd[:, ds(g * G3 + j, 1)], ALU.subtract, ALU.mult)
                    mm.then_inc(s["xn_ready"], 1)

                def front_k(g, u):
                    for k in range(4):
                        w = front_count(g, 6 + k)
                        src = m_read(dve, w)
                        for a in range(2):
                            mm = dve.tensor_scalar(kT[u][:, 2 * k + a, :], src[:, a * W3:(a + 1) * W3],
                                                   bcol[:, 1, 2 * k + a:2 * k + a + 1], None, ALU.add)
                        m_release(mm, w)
                    dve.drain().then_inc(s["front_k"], 1)

                def front_v(g, u):
                    for j in range(G3):
                        for a in range(2):
                            w = front_count(g, 10 + 2 * j + a)
                            src = m_read(dve, w)
                            mm = dve.tensor_tensor(values[u][:, j, a * 512:(a + 1) * 512], src[:],
                                                   bv[:, a * 512:(a + 1) * 512], ALU.add)
                            m_release(mm, w)
                    dve.drain().then_inc(s["front_v"], 1)

                def maximum(n, c):
                    dve.wait_ge(s["s_ready"], 4 * n + c + 1)
                    dve.tensor_reduce(minus_max[:, 4 * c:4 * c + 4], S[c % 2][:].rearrange("p (a k) -> p a k", a=4),
                                      AX.X, ALU.max, negate=True).then_inc(s["max_ready"], 1)

                def normalise(n, b, c):
                    dve.wait_ge(s["exp_done"], 4 * n + c + 3)
                    heads = slice(4 * c, 4 * c + 4)
                    dve.reciprocal(inv[:, heads], total[:, heads])
                    dve.drain()
                    dve.tensor_tensor(probs[b][:, heads, :], probs[b][:, heads, :],
                                      inv[:, heads].unsqueeze(2).broadcast_to([P, 4, P]), ALU.mult
                                      ).then_inc(s["norm_ready"], 1)

                def copy_pt(n, c):
                    dve.wait_ge(s["pt_ready"], 4 * n + c + 1)
                    dve.tensor_copy(probsT[:, 4 * c:4 * c + 4, :].rearrange("p a q -> p (a q)"), T[c % 2][:]
                                    ).then_inc(s["pt_copied"], 1)

                for u in range(2):
                    dve.memset(q_pad[u].rearrange("p a r t -> p (a r t)"), 0.0)
                dve.wait_ge(w_in[3], 16 * LOADS)
                dve.tensor_scalar(bcol[:, 2, :], bcol[:, 0, :], SCALE, None, ALU.mult)
                dve.drain().then_inc(s["stats_ready"], 1)
                for n in ("m_free0", "m_free1"):
                    dve.drain().then_inc(s[n], 1)
                for n in ("exp_done", "pt_copied", "o_copied"):
                    dve.drain().then_inc(s[n], 2)
                normed(0, 0)
                front_k(0, 0)
                front_v(0, 0)
                maximum(0, 0)
                maximum(0, 1)
                normalise(0, 0, 0)
                maximum(0, 2)
                normalise(0, 0, 1)
                maximum(0, 3)
                normalise(0, 0, 2)
                normalise(0, 0, 3)

                def group(g, u, last):
                    for j in range(G3):
                        n, nb = g * G3 + j, 1 - j % 2
                        ahead = j == 0 or not last
                        if j == 0 and not last:
                            normed(g + 1, 1 - u)
                        if ahead:
                            maximum(n + 1, 0)
                        copy_pt(n, 0)
                        if ahead:
                            maximum(n + 1, 1)
                        copy_pt(n, 1)
                        if ahead:
                            normalise(n + 1, nb, 0)
                            maximum(n + 1, 2)
                        copy_pt(n, 2)
                        if ahead:
                            normalise(n + 1, nb, 1)
                            maximum(n + 1, 3)
                        copy_pt(n, 3)
                        if ahead:
                            normalise(n + 1, nb, 2)
                        if not last:
                            (front_k, front_v)[j](g + 1, 1 - u)
                        if ahead:
                            normalise(n + 1, nb, 3)
                        w = y_count(g, j, last)
                        src = m_read(dve, w)
                        if j == 0:
                            dve.wait_ge(s["xb_ready"], g + 1)
                        mm = dve.tensor_tensor(x[:, ds(n, 1), :].rearrange("p a m -> p (a m)"), src[:, 0:P],
                                               xb[u][:, j, :], ALU.add)
                        m_release(mm, w)
                    dve.drain()
                    for j in range(G3):
                        dve.bn_stats(bn[:, j, :], x[:, ds(g * G3 + j, 1), :])
                    dve.drain()
                    for j in range(G3):
                        dve.bn_aggr(agg[:, j, :], bn[:, j, :])
                    dve.drain()
                    dve.tensor_copy(mean[:, ds(g * G3, G3)], agg[:, :, 0])
                    dve.tensor_scalar(var_eps[:, ds(g * G3, G3)], agg[:, :, 1], LN_EPS, None,
                                      ALU.add).then_inc(s["stats_ready"], 1)
                loop(dve, group, NG3)
                barrier(dve, phase)

            def gpsimd(pool):
                def group(g, u, last):
                    pool.tensor_tensor(xb[u], x[:, ds(g * G3, G3), :], bo.unsqueeze(1).broadcast_to([P, G3, P]),
                                       ALU.add).then_inc(s["xb_ready"], 1)
                    pool.wait_ge(s["stats_ready"], g + 2)
                    pool.tensor_tensor(rstd[:, ds(g * G3, G3)], var_eps[:, ds(g * G3, G3)], neg_half[:, 0:G3], ALU.pow)
                pool.wait_ge(w_in[3], 16 * LOADS)
                loop(pool, group, NG3)
                barrier(pool, phase)

            return sync, tensor, scalar, vector, gpsimd

        phases = []

        def load_other(eng):
            barrier(eng, 0)
        phases.append((load_sync, load_other, load_other, load_dve, load_pool))
        makers = [lambda n: small_heads(0, n), lambda n: narrow(0, n), linear_attention, expert_choice, lambda n: small_heads(2, n),
                  gated_experts, wide_heads, lambda n: narrow(3, n)]
        for n, make in enumerate(makers):
            phases.append(make(n + 1))

        block = ctx.enter_context(nc.Block())

        @block.sync
        def _(sp):
            for phase in phases:
                phase[0](sp)
            for g in range(NG):
                sp.dma_start(out[g * G:(g + 1) * G].rearrange("b s d -> s b d"),
                             x[:, g * G:(g + 1) * G, :]).then_inc(x_out, 16)
            sp.wait_ge(x_out, 16 * NG)

        @block.tensor
        def _(pe):
            for phase in phases:
                phase[1](pe)

        @block.scalar
        def _(act):
            for phase in phases:
                phase[2](act)

        @block.vector
        def _(dve):
            for phase in phases:
                phase[3](dve)

        @block.gpsimd
        def _(pool):
            for phase in phases:
                phase[4](pool)


def kernel(**inputs):
    import numpy as np
    import concourse.bacc as bacc
    from concourse.bass_utils import run_bass_kernel_spmd

    def a(name):
        return np.asarray(inputs[name])

    def by_feature(w):
        return np.ascontiguousarray(w.reshape(H, DH, -1).swapaxes(0, 1).reshape(w.shape))

    lay = {"x": a("x"), "ctxT": np.ascontiguousarray(a("ctx_1024").reshape(B * P, P).T)}
    for l, names in ((0, "L0_xattn_{}{}"), (2, "L2_xattn_{}_{}")):
        for n in "qkvo":
            w, b = a(names.format("W", n)), a(names.format("b", n))
            if n in "qk":
                w, b = by_feature(w), by_feature(b)
            lay[f"w{n}{l}"], lay[f"b{n}{l}"] = np.ascontiguousarray(w.T), b
    lay["gate0"] = np.ascontiguousarray(a("L0_ffn_gate_W").T)
    lay["expert0"] = np.ascontiguousarray(a("L0_ffn_expert_W")[:2].swapaxes(0, 1))
    lay["outw0"] = np.ascontiguousarray(a("L0_ffn_out_W").T)
    lay["gate2"] = np.ascontiguousarray(a("L2_ffn_centroid").T)
    lay["wgu_2"] = np.stack([a("L2_ffn_Wg"), a("L2_ffn_W1")]).transpose(2, 0, 1, 3).reshape(P, -1)
    lay["w2_2"] = a("L2_ffn_W2").reshape(E, 3, 114, P).transpose(2, 0, 1, 3).reshape(114, -1)
    lay["bg_2"] = a("L2_ffn_bg").reshape(E, 3, 114).transpose(2, 0, 1)
    lay["b1_2"] = a("L2_ffn_b1").reshape(E, 3, 114).transpose(2, 0, 1)
    lay["b2_2"] = a("L2_ffn_b2")
    for n in "qkv":
        lay[f"w{n}3"] = a(f"L3_xattn_W{n}").T
    lay["wo3"] = a("L3_xattn_Wo").T.reshape(8, P, P).swapaxes(0, 1).reshape(P, -1)
    lay["bqk3"] = np.stack([a("L3_xattn_bq"), a("L3_xattn_bk")]).reshape(2, 8, P).transpose(2, 0, 1)
    lay["bv3"], lay["bo3"] = a("L3_xattn_bv"), a("L3_xattn_bo")
    lay["gate1"] = np.ascontiguousarray(a("L1_ffn_Wg").T)
    lay["w1_1"] = np.ascontiguousarray(a("L1_ffn_W1").swapaxes(0, 1).reshape(P, -1))
    lay["w2_1"] = np.ascontiguousarray(a("L1_ffn_W2").reshape(E, 4, P, P).transpose(2, 0, 1, 3).reshape(P, -1))
    lay["b1_1"] = np.ascontiguousarray(a("L1_ffn_b1").reshape(E, 4, P).transpose(2, 0, 1))
    lay["b2_1"] = a("L1_ffn_b2")
    lay["w1"] = np.stack([a("L1_xattn_wq"), a("L1_xattn_wk"), a("L1_xattn_wv"), a("L1_xattn_dense_w")])
    lay["row1"] = np.stack([a("L1_xattn_ln_gamma"), a("L1_xattn_ln_beta"), a("L1_xattn_dense_b")])
    lay["mask1"] = np.ascontiguousarray(a("mask_BxS2_ff1").T)
    lay["gate3"] = np.ascontiguousarray(a("L3_ffn_gate_w").T)
    lay["we3"] = np.ascontiguousarray(a("L3_ffn_We").swapaxes(0, 1))
    m = a("mask_1x1xSxS2_bk0")[0, 0].view(np.uint8)
    lay["mask2"] = np.ascontiguousarray(np.stack([m, m.T])).view(np.int32)

    nc = bacc.Bacc("TRN2", target_bir_lowering=False, num_devices=1)
    arrays, handles = {}, {}
    for name, v in lay.items():
        v = np.ascontiguousarray(v)
        arrays[f"in_{name}"] = v
        handles[name] = nc.dram_tensor(f"in_{name}", v.shape, mybir.dt.from_np(v.dtype), kind="ExternalInput").ap()
    out = nc.dram_tensor("out_x", (B, P, P), F32, kind="ExternalOutput").ap()
    program(nc, handles, out)
    r = run_bass_kernel_spmd(nc, [arrays], core_ids=[0])
    return r.results[0]["out_x"]
```
